# Optimizing a Trainium2 kernel written in Bass

```python
import numpy as np
import jax
import jax.numpy as jnp

def _softmax(x, axis=-1):
    return jax.nn.softmax(x, axis=axis)

def _gelu(x):
    return jax.nn.gelu(x, approximate=True)

def _silu(x):
    return jax.nn.silu(x)

def _sigmoid(x):
    return jax.nn.sigmoid(x)

def _layernorm(x, axis=-1, eps=1e-05):
    m = jnp.mean(x, axis=axis, keepdims=True)
    v = jnp.var(x, axis=axis, keepdims=True)
    return (x - m) / jnp.sqrt(v + eps)

def _scatter_add(tgt, idx, src, axis=0):
    return tgt.at[idx].add(src)

def _segment_sum(src, seg, n):
    return jax.ops.segment_sum(src, seg, n)
kernel_name = 'mk_vit_tower_cls_d1_tok_img768_r4_08d37b'

def setup_inputs(seed: int=0):
    np.random.seed(seed)
    _w = jnp.asarray

    def _rec_inputs():
        import jax
        import jax.numpy as jnp
        _rk = jax.random.key(seed)
        x = -0.00016672 + 0.999947 * jax.random.normal(jax.random.fold_in(_rk, 1), (16, 3, 96, 96), jnp.float32)
        cls_tok = 0.02 * jax.random.normal(jax.random.fold_in(_rk, 5), (1, 1, 192), jnp.float32)
        return (x, cls_tok)
    x, cls_tok = _rec_inputs()

    def _L0_tok_setup():
        import jax, jax.numpy as jnp
        import numpy as np
        P = 16
        EMBED = 192
        EPS = 1e-05

        def _patchify(x):
            N, C, H, W = x.shape
            x = x.reshape(N, C, H // P, P, W // P, P)
            x = x.transpose(0, 2, 4, 1, 3, 5)
            return x.reshape(N, H // P * (W // P), C * P * P)
        key = jax.random.key(seed)
        k1, k2, k3 = jax.random.split(key, 3)
        in_dim = P * P * 3
        x = jax.random.normal(k1, (64, 3, 96, 96), dtype=jnp.float32)
        bound = 1.0 / np.sqrt(in_dim)
        W = jax.random.uniform(k2, (EMBED, in_dim), dtype=jnp.float32, minval=-bound, maxval=bound)
        b = jax.random.uniform(k3, (EMBED,), dtype=jnp.float32, minval=-bound, maxval=bound)
        ln_w = jnp.ones((EMBED,), dtype=jnp.float32)
        ln_b = jnp.zeros((EMBED,), dtype=jnp.float32)
        return {'x': x, 'W': W, 'b': b, 'ln_w': ln_w, 'ln_b': ln_b}
    _L0_tok_all = _L0_tok_setup()
    _L0_tok_in = {k: v for k, v in _L0_tok_all.items() if k in ('W', 'b', 'ln_w', 'ln_b')}
    del _L0_tok_all

    def _L0_attn_setup():
        import jax, jax.numpy as jnp
        import numpy as np
        B, L, D = (2, 1024, 192)
        BN = 96
        DI = 192
        NS = 16
        DC = 4
        R = 24

        def _ln(x, g, b):
            m = x.mean(-1, keepdims=True)
            v = ((x - m) ** 2).mean(-1, keepdims=True)
            return (x - m) / jnp.sqrt(v + 1e-05) * g + b

        def _mamba(x, in_W, conv_w, conv_b, xproj_W, dt_W, dt_b, A_log, Dp, out_W):
            Bb, Ll, _ = x.shape
            xz = x @ in_W
            xs, z = jnp.split(xz, 2, axis=-1)
            xc = jnp.transpose(xs, (0, 2, 1))
            xc = jax.lax.conv_general_dilated(xc, conv_w[:, None, :], (1,), [(DC - 1, 0)], dimension_numbers=('NCH', 'OIH', 'NCH'), feature_group_count=DI)
            xc = jax.nn.silu(xc + conv_b[None, :, None])
            u = jnp.transpose(xc, (0, 2, 1))
            x_dbl = u @ xproj_W
            dt, Bm, Cm = jnp.split(x_dbl, [R, R + NS], axis=-1)
            dt = jax.nn.softplus(dt @ dt_W + dt_b)
            A = -jnp.exp(A_log)

            def step(h, inp):
                dt_t, B_t, C_t, u_t = inp
                dA = jnp.exp(dt_t[:, :, None] * A)
                h = dA * h + (dt_t * u_t)[:, :, None] * B_t[:, None, :]
                y = (h * C_t[:, None, :]).sum(-1)
                return (h, y)
            tm = lambda a: jnp.transpose(a, (1, 0, 2))
            h0 = jnp.zeros((Bb, DI, NS), x.dtype)
            _, ys = jax.lax.scan(step, h0, (tm(dt), tm(Bm), tm(Cm), tm(u)))
            y = jnp.transpose(ys, (1, 0, 2)) + u * Dp
            y = y * jax.nn.silu(z)
            return y @ out_W
        key = jax.random.key(seed)
        ks = jax.random.split(key, 32)
        n = lambda i, shape, s=0.02: jax.random.normal(ks[i], shape, jnp.float32) * s
        inp = {'x': jax.random.normal(ks[0], (B, L, D), jnp.float32), 'down_W': n(1, (D, BN)), 'down_b': jnp.zeros((BN,), jnp.float32), 'up_W': n(2, (BN, D)), 'up_b': jnp.zeros((D,), jnp.float32)}
        A_log = jnp.log(jnp.tile(jnp.arange(1, NS + 1, dtype=jnp.float32), (DI, 1)))
        for pi, p in enumerate(['f', 'b']):
            o = 3 + pi * 10
            inp[p + '_in_W'] = n(o, (BN, 2 * DI))
            inp[p + '_conv_w'] = n(o + 1, (DI, DC), 0.1)
            inp[p + '_conv_b'] = jnp.zeros((DI,), jnp.float32)
            inp[p + '_xproj_W'] = n(o + 2, (DI, R + 2 * NS))
            inp[p + '_dt_W'] = n(o + 3, (R, DI), 0.1)
            inp[p + '_dt_b'] = n(o + 4, (DI,), 0.5)
            inp[p + '_A_log'] = A_log
            inp[p + '_D'] = jnp.ones((DI,), jnp.float32)
            inp[p + '_out_W'] = n(o + 5, (DI, BN))
            inp[p + '_ln_g'] = jnp.ones((BN,), jnp.float32)
            inp[p + '_ln_b'] = jnp.zeros((BN,), jnp.float32)
        return inp
    _L0_attn_all = _L0_attn_setup()
    _L0_attn_in = {k: v for k, v in _L0_attn_all.items() if k in ('down_W', 'down_b', 'up_W', 'up_b', 'f_in_W', 'f_conv_w', 'f_conv_b', 'f_xproj_W', 'f_dt_W', 'f_dt_b', 'f_A_log', 'f_D', 'f_out_W', 'f_ln_g', 'f_ln_b', 'b_in_W', 'b_conv_w', 'b_conv_b', 'b_xproj_W', 'b_dt_W', 'b_dt_b', 'b_A_log', 'b_D', 'b_out_W', 'b_ln_g', 'b_ln_b')}
    del _L0_attn_all

    def _L0_ffn_setup():
        import jax, jax.numpy as jnp
        import numpy as np
        E = 8
        TOP_K = 2
        CAP_RATIO = 1.2
        key = jax.random.key(seed)
        k1, k2, k3, k4 = jax.random.split(key, 4)
        B, L, D, H = (2, 512, 192, 512)
        x = jax.random.normal(k1, (B, L, D), dtype=jnp.float32)
        Wg = jax.random.normal(k2, (D, E), dtype=jnp.float32) * 0.02
        W1 = jax.random.normal(k3, (E, D, 2 * H), dtype=jnp.float32) * 0.02
        W2 = jax.random.normal(k4, (E, H, D), dtype=jnp.float32) * 0.02
        return {'x': x, 'Wg': Wg, 'W1': W1, 'W2': W2}
    _L0_ffn_all = _L0_ffn_setup()
    _L0_ffn_in = {k: v for k, v in _L0_ffn_all.items() if k in ('Wg', 'W1', 'W2')}
    del _L0_ffn_all
    return {'x': x, 'cls_tok': cls_tok, 'L0_tok_W': _L0_tok_in['W'], 'L0_tok_b': _L0_tok_in['b'], 'L0_tok_ln_w': _L0_tok_in['ln_w'], 'L0_tok_ln_b': _L0_tok_in['ln_b'], 'L0_attn_down_W': _L0_attn_in['down_W'], 'L0_attn_down_b': _L0_attn_in['down_b'], 'L0_attn_up_W': _L0_attn_in['up_W'], 'L0_attn_up_b': _L0_attn_in['up_b'], 'L0_attn_f_in_W': _L0_attn_in['f_in_W'], 'L0_attn_f_conv_w': _L0_attn_in['f_conv_w'], 'L0_attn_f_conv_b': _L0_attn_in['f_conv_b'], 'L0_attn_f_xproj_W': _L0_attn_in['f_xproj_W'], 'L0_attn_f_dt_W': _L0_attn_in['f_dt_W'], 'L0_attn_f_dt_b': _L0_attn_in['f_dt_b'], 'L0_attn_f_A_log': _L0_attn_in['f_A_log'], 'L0_attn_f_D': _L0_attn_in['f_D'], 'L0_attn_f_out_W': _L0_attn_in['f_out_W'], 'L0_attn_f_ln_g': _L0_attn_in['f_ln_g'], 'L0_attn_f_ln_b': _L0_attn_in['f_ln_b'], 'L0_attn_b_in_W': _L0_attn_in['b_in_W'], 'L0_attn_b_conv_w': _L0_attn_in['b_conv_w'], 'L0_attn_b_conv_b': _L0_attn_in['b_conv_b'], 'L0_attn_b_xproj_W': _L0_attn_in['b_xproj_W'], 'L0_attn_b_dt_W': _L0_attn_in['b_dt_W'], 'L0_attn_b_dt_b': _L0_attn_in['b_dt_b'], 'L0_attn_b_A_log': _L0_attn_in['b_A_log'], 'L0_attn_b_D': _L0_attn_in['b_D'], 'L0_attn_b_out_W': _L0_attn_in['b_out_W'], 'L0_attn_b_ln_g': _L0_attn_in['b_ln_g'], 'L0_attn_b_ln_b': _L0_attn_in['b_ln_b'], 'L0_ffn_Wg': _L0_ffn_in['Wg'], 'L0_ffn_W1': _L0_ffn_in['W1'], 'L0_ffn_W2': _L0_ffn_in['W2']}

def reference(x, cls_tok, L0_tok_W, L0_tok_b, L0_tok_ln_w, L0_tok_ln_b, L0_attn_down_W, L0_attn_down_b, L0_attn_up_W, L0_attn_up_b, L0_attn_f_in_W, L0_attn_f_conv_w, L0_attn_f_conv_b, L0_attn_f_xproj_W, L0_attn_f_dt_W, L0_attn_f_dt_b, L0_attn_f_A_log, L0_attn_f_D, L0_attn_f_out_W, L0_attn_f_ln_g, L0_attn_f_ln_b, L0_attn_b_in_W, L0_attn_b_conv_w, L0_attn_b_conv_b, L0_attn_b_xproj_W, L0_attn_b_dt_W, L0_attn_b_dt_b, L0_attn_b_A_log, L0_attn_b_D, L0_attn_b_out_W, L0_attn_b_ln_g, L0_attn_b_ln_b, L0_ffn_Wg, L0_ffn_W1, L0_ffn_W2):
    import jax
    import jax.numpy as jnp

    def _L0_tok_ref(x, W, b, ln_w, ln_b):
        import jax, jax.numpy as jnp
        import numpy as np
        P = 16
        EMBED = 192
        EPS = 1e-05

        def _patchify(x):
            N, C, H, W = x.shape
            x = x.reshape(N, C, H // P, P, W // P, P)
            x = x.transpose(0, 2, 4, 1, 3, 5)
            return x.reshape(N, H // P * (W // P), C * P * P)
        patches = _patchify(x)
        y = jnp.einsum('nsi,oi->nso', patches, W) + b
        mu = jnp.mean(y, axis=-1, keepdims=True)
        var = jnp.mean(jnp.square(y - mu), axis=-1, keepdims=True)
        return (y - mu) / jnp.sqrt(var + EPS) * ln_w + ln_b

    def _L0_attn_ref(x, down_W, down_b, up_W, up_b, f_in_W, f_conv_w, f_conv_b, f_xproj_W, f_dt_W, f_dt_b, f_A_log, f_D, f_out_W, f_ln_g, f_ln_b, b_in_W, b_conv_w, b_conv_b, b_xproj_W, b_dt_W, b_dt_b, b_A_log, b_D, b_out_W, b_ln_g, b_ln_b):
        import jax, jax.numpy as jnp
        import numpy as np
        B, L, D = (2, 1024, 192)
        BN = 96
        DI = 192
        NS = 16
        DC = 4
        R = 24

        def _ln(x, g, b):
            m = x.mean(-1, keepdims=True)
            v = ((x - m) ** 2).mean(-1, keepdims=True)
            return (x - m) / jnp.sqrt(v + 1e-05) * g + b

        def _mamba(x, in_W, conv_w, conv_b, xproj_W, dt_W, dt_b, A_log, Dp, out_W):
            Bb, Ll, _ = x.shape
            xz = x @ in_W
            xs, z = jnp.split(xz, 2, axis=-1)
            xc = jnp.transpose(xs, (0, 2, 1))
            xc = jax.lax.conv_general_dilated(xc, conv_w[:, None, :], (1,), [(DC - 1, 0)], dimension_numbers=('NCH', 'OIH', 'NCH'), feature_group_count=DI)
            xc = jax.nn.silu(xc + conv_b[None, :, None])
            u = jnp.transpose(xc, (0, 2, 1))
            x_dbl = u @ xproj_W
            dt, Bm, Cm = jnp.split(x_dbl, [R, R + NS], axis=-1)
            dt = jax.nn.softplus(dt @ dt_W + dt_b)
            A = -jnp.exp(A_log)

            def step(h, inp):
                dt_t, B_t, C_t, u_t = inp
                dA = jnp.exp(dt_t[:, :, None] * A)
                h = dA * h + (dt_t * u_t)[:, :, None] * B_t[:, None, :]
                y = (h * C_t[:, None, :]).sum(-1)
                return (h, y)
            tm = lambda a: jnp.transpose(a, (1, 0, 2))
            h0 = jnp.zeros((Bb, DI, NS), x.dtype)
            _, ys = jax.lax.scan(step, h0, (tm(dt), tm(Bm), tm(Cm), tm(u)))
            y = jnp.transpose(ys, (1, 0, 2)) + u * Dp
            y = y * jax.nn.silu(z)
            return y @ out_W
        h = x @ down_W + down_b
        fwd = _ln(_mamba(h, f_in_W, f_conv_w, f_conv_b, f_xproj_W, f_dt_W, f_dt_b, f_A_log, f_D, f_out_W), f_ln_g, f_ln_b)
        bwd = _ln(_mamba(h[:, ::-1], b_in_W, b_conv_w, b_conv_b, b_xproj_W, b_dt_W, b_dt_b, b_A_log, b_D, b_out_W), b_ln_g, b_ln_b)
        y = fwd + bwd[:, ::-1]
        return y @ up_W + up_b

    def _L0_ffn_ref(x, Wg, W1, W2):
        import jax, jax.numpy as jnp
        import numpy as np
        E = 8
        TOP_K = 2
        CAP_RATIO = 1.2
        B, L, D = x.shape
        H = W2.shape[1]
        xf = x.reshape(-1, D)
        N = xf.shape[0]
        capacity = int(CAP_RATIO * N / E)
        logits = xf @ Wg
        scores, idx = jax.lax.top_k(logits, TOP_K)
        weights = jax.nn.softmax(scores, axis=-1)
        xpad = jnp.concatenate([xf, jnp.zeros((1, D), xf.dtype)], axis=0)
        wpad_zero = jnp.zeros((1,), weights.dtype)
        out = jnp.zeros((N, D), x.dtype)
        for k in range(TOP_K):
            ik = idx[:, k]
            onehot = ik[:, None] == jnp.arange(E)[None, :]
            pos = jnp.cumsum(onehot, axis=0) - 1
            posk = jnp.take_along_axis(pos, ik[:, None], axis=1)[:, 0]
            keep = posk < capacity
            buf = jnp.full((E, capacity), N, dtype=jnp.int32)
            buf = buf.at[ik, posk].set(jnp.arange(N, dtype=jnp.int32), mode='drop')
            xg = xpad[buf]
            h = jnp.einsum('ecd,edh->ech', xg, W1)
            act = h[..., :H] * jax.nn.silu(h[..., H:])
            ye = jnp.einsum('ech,ehd->ecd', act, W2)
            wk = jnp.where(keep, weights[:, k], 0.0)
            w_buf = jnp.concatenate([wk, wpad_zero])[buf]
            out = out.at[buf.reshape(-1)].add((w_buf[..., None] * ye).reshape(E * capacity, D), mode='drop')
        return out.reshape(B, L, D)
    h = _L0_tok_ref(x, L0_tok_W, L0_tok_b, L0_tok_ln_w, L0_tok_ln_b)
    h = jnp.concatenate([jnp.broadcast_to(cls_tok, (h.shape[0], 1, h.shape[2])), h], axis=1)
    h = h + _L0_attn_ref(_layernorm(h, axis=-1), L0_attn_down_W, L0_attn_down_b, L0_attn_up_W, L0_attn_up_b, L0_attn_f_in_W, L0_attn_f_conv_w, L0_attn_f_conv_b, L0_attn_f_xproj_W, L0_attn_f_dt_W, L0_attn_f_dt_b, L0_attn_f_A_log, L0_attn_f_D, L0_attn_f_out_W, L0_attn_f_ln_g, L0_attn_f_ln_b, L0_attn_b_in_W, L0_attn_b_conv_w, L0_attn_b_conv_b, L0_attn_b_xproj_W, L0_attn_b_dt_W, L0_attn_b_dt_b, L0_attn_b_A_log, L0_attn_b_D, L0_attn_b_out_W, L0_attn_b_ln_g, L0_attn_b_ln_b)
    h = h + _L0_ffn_ref(_layernorm(h, axis=-1), L0_ffn_Wg, L0_ffn_W1, L0_ffn_W2)
    return h

_drawn_inputs = setup_inputs


def setup_inputs(seed=0):
    import zlib

    import numpy as np

    out = dict(_drawn_inputs(seed))
    spreads = {'L0_tok_ln_w': (1.0, 0.2),
     'L0_tok_ln_b': (0.0, 0.1),
     'L0_attn_down_b': (0.0, 0.651),
     'L0_attn_up_b': (0.0, 0.1),
     'L0_attn_f_conv_b': (0.0, 0.323),
     'L0_attn_f_D': (1.0, 0.6),
     'L0_attn_f_ln_g': (1.0, 0.6),
     'L0_attn_f_ln_b': (0.0, 0.409),
     'L0_attn_b_conv_b': (0.0, 0.3),
     'L0_attn_b_D': (1.0, 0.6),
     'L0_attn_b_ln_g': (1.0, 0.6),
     'L0_attn_b_ln_b': (0.0, 0.343)}
    factors = {'cls_tok': 8.0,
     'L0_attn_f_conv_w': 8.0,
     'L0_attn_f_xproj_W': 8.0,
     'L0_attn_f_dt_W': 8.0,
     'L0_attn_f_dt_b': 8.0,
     'L0_attn_f_A_log': 8.0,
     'L0_attn_b_conv_w': 8.0,
     'L0_attn_b_xproj_W': 8.0,
     'L0_attn_b_dt_W': 8.0,
     'L0_attn_b_dt_b': 8.0,
     'L0_attn_b_A_log': 8.0,
     'L0_ffn_Wg': 5.487,
     'L0_ffn_W1': 4.785,
     'L0_ffn_W2': 4.776}
    for name, (base, spread) in spreads.items():
        noise = np.random.default_rng([zlib.crc32(name.encode()), seed]).standard_normal(out[name].shape)
        drawn = base * np.exp(spread * noise) if base else spread * noise
        out[name] = jnp.asarray(drawn.astype(out[name].dtype))
    for name, factor in factors.items():
        out[name] = (out[name] * factor).astype(out[name].dtype)
    return out
```

```python
from contextlib import ExitStack

import numpy as np

import concourse.bass as bass
from concourse import mybir

ALU = mybir.AluOpType
ACT = mybir.ActivationFunctionType
AX = mybir.AxisListType
F32 = mybir.dt.float32
BF16 = mybir.dt.bfloat16
F16 = mybir.dt.float16
U32 = mybir.dt.uint32

P = 128
IMAGES, PATCH, SIDE = 16, 16, 6
SEQ = SIDE * SIDE + 1
N = IMAGES * SEQ
HALF = N // 2
TILES = -(-N // P)
NP_ = TILES * P
D = 192
DK = D // 2
PIX = 3 * PATCH * PATCH
PK = PIX // P
BN = 96
DI = 192
CH = 2 * DI
CC = CH // P
NS, TAPS, R = 16, 4, 24
E, TOP, H = 8, 2, 512
CAP = int(1.2 * N / E)
HC = H // P
KSLOTS = E * CAP
SLOTS = TOP * KSLOTS
EPS = 1e-5
SPLIT = 1024.0
QUADS = NS // 4
SEL = CC * NS
DROP = 4096.0

C_W, C_B, C_DTB, C_D, C_A = 0, TAPS, TAPS + 1, TAPS + 2, TAPS + 3
CPAR = C_A + NS
R_TB, R_LW, R_UB, R_G = 0, D, 2 * D, 3 * D
RPAR = R_G + 2 * BN
W_DOWN, W_XS, W_Z, W_UP, W_G = 0, 2 * BN, 2 * BN + CH, 2 * BN + 2 * CH, 2 * BN + 2 * CH + D
W96 = W_G + 2 * E
K_PATCH, K_REAL, K_REV, K_BASE = 0, TILES, 2 * TILES, 2 * TILES + E
KCON = K_BASE + E
XB, XC, XDT = 0, 2 * NS, 4 * NS
XROWS = XDT + 2 * R


def vit_mamba_moe(nc, a):
    with ExitStack() as ctx:
        def sb(name, shape, dt=F32):
            return ctx.enter_context(nc.sbuf_tensor(name, shape, dt))

        def sem(name):
            return ctx.enter_context(nc.semaphore(name))

        xT = sb("xT", [P, PK, NP_])
        tokW = sb("tokW", [P, PK, D])
        chanp = sb("chanp", [P, CC, CPAR])
        rowp = sb("rowp", [P, RPAR])
        base = sb("base", [P, TILES, D])
        kcon = sb("kcon", [P, KCON])
        brow = sb("brow", [1, NP_ + D])
        col96 = sb("col96", [BN, 3])
        w96 = sb("w96", [BN, W96])
        xpw = sb("xpw", [P, CC, XROWS])
        dtw = sb("dtw", [P, CH])
        outw = sb("outw", [P, CC, BN])
        sel = sb("sel", [3 * 2 * NS, SEL, P], BF16)
        ident = sb("ident", [P, P])
        tri = sb("tri", [P, P], BF16)
        ones = sb("ones", [P, P], BF16)
        iota = sb("iota", [P, KSLOTS], F16)
        w1s = [sb(f"w1_{i}", [DK, 2, 2 * H]) for i in range(2)]
        w2s = [sb(f"w2_{i}", [P, HC, D]) for i in range(2)]

        stats = sb("stats", [P, TILES, 2, 6])
        mv = sb("mv", [P, TILES, 2, 2])
        lnv = sb("lnv", [P, TILES, 2])
        rst = sb("rst", [P, TILES, 2])
        nt = sb("nt", [P, TILES, 2])
        h0 = sb("h0", [P, TILES, D])
        zn = sb("zn", [P, TILES, D])
        znT = sb("znT", [DK, 2 * NP_])
        hF = sb("hF", [BN, N])
        hR = sb("hR", [BN, N])
        halfw = sb("halfw", [P, CC, TAPS + 1])
        xs = sb("xs", [P, CC, N])
        xc = sb("xc", [P, CC, N])
        th = sb("th", [P, CC, N])
        pix = xT[:].rearrange("p k n -> p (k n)")
        zs = pix[:, 0:CC * N].rearrange("p (c n) -> p c n", c=CC)
        sz = sb("sz", [P, CC, N])
        mix = sb("mix", [P, 4, CC, N])
        u, uD, dt, du = (mix[:, i] for i in range(4))
        ab, ex, lg = xs, th, xc
        xdt = sb("xdt", [P, N])
        bcr = sb("bcr", [4 * NS, N])
        bparts = sb("bparts", [6 * NS, N], BF16)
        cparts = sb("cparts", [6 * NS, N], BF16)
        negA = sb("negA", [P, CC * NS])
        dA = [sb(f"dA{i}", [P, N]) for i in range(2)]
        Bs = [sb(f"Bs{i}", [P, N]) for i in range(2)]
        dBu = [sb(f"dBu{i}", [P, N])[:] for i in range(2)] + [pix[:, (CC + i) * N:(CC + i + 1) * N] for i in range(2)]
        hs = [sb(f"hs{i}", [P, N]) for i in range(2)]
        hc = [sb(f"hc{i}", [P, N]) for i in range(2)]
        g = sb("g", [P, 2, NP_])
        ysb = xc[:, 0, :]
        gR = xs[:].rearrange("p c n -> p (c n)")[:, 0:2 * NP_].rearrange("p (c n) -> p c n", c=2)
        yn = zn
        yT = sb("yT", [BN, NP_])
        bsum = sb("bsum", [BN, 1])
        xfT = znT
        xhi = sb("xhi", [P, TILES, D], F16)
        xlo = sb("xlo", [P, TILES, D], F16)
        xr = sb("xr", [P, TILES, D])
        lgt = sb("lgt", [P, TILES, E])
        lg2 = sb("lg2", [P, TILES, E])
        key = sb("key", [P, TILES, E])
        oh = sb("oh", [P, TOP, TILES, E])
        ohm = sb("ohm", [P, TOP, TILES, E])
        ohb = sb("ohb", [P, TILES, TOP, E], BF16)
        mx = sb("mx", [P, TOP, TILES])
        km = sb("km", [P, TILES])
        dm = sb("dm", [P, TILES])
        em = sb("em", [P, TILES])
        wts = sb("wts", [P, TOP, TILES])
        psel = sb("psel", [P, TILES, TOP, E])
        pos = sb("pos", [P, TILES, TOP])
        eb = sb("eb", [P, TILES, TOP])
        over = sb("over", [P, TILES, TOP])
        slot = sb("slot", [P, TILES, TOP])
        row = sb("row", [P, TILES, TOP])
        rowu = sb("rowu", [P, TILES, TOP], U32)
        disp = pix.bitcast(BF16)[:, 0:TILES * SLOTS].rearrange("p (t s) -> p t s", t=TILES)
        flat = mix[:].rearrange("p a c n -> p (a c n)")
        xgT = flat[0:DK, 0:2 * SLOTS].rearrange("p (k s) -> p k s", k=2)
        back = flat[:, 2 * CC * N:2 * CC * N + TILES * TOP * D].rearrange("p (t k d) -> p t k d", t=TILES, k=TOP)
        thg = [dA[i][:, 0:4 * CAP].rearrange("p (q s) -> p q s", q=2) for i in range(2)]
        gt = [dBu[i][:, 0:4 * CAP].rearrange("p (q s) -> p q s", q=2) for i in range(2)]
        act_t = [sb(f"act{i}", [P, HC, 2 * CAP]) for i in range(2)]
        ye = [sb(f"ye{i}", [CAP, TOP, D]) for i in range(2)]
        zrow = sb("zrow", [1, D])
        ybuf = nc.dram_tensor("ybuf", (SLOTS + 1, D), F32, kind="Internal").ap()
        ps = ctx.enter_context(nc.psum_tensor("ps", [P, 8, 512], F32))

        def halves(b):
            return ps[:, b:b + 2, 0:HALF]

        def split(ap):
            return ap.rearrange("p (s c) -> p s c", s=2)

        def img(ap, lo, hi):
            return ap.rearrange("p (i t) -> p i t", t=SEQ)[:, :, lo:hi]

        s_px = [sem(f"pixels_loaded{k}") for k in range(PK)]
        s_par = sem("token_params_loaded")
        s_id = sem("identity_loaded")
        s_w96 = sem("w96_loaded")
        s_chp = sem("channel_params_loaded")
        s_xpw = sem("xproj_loaded")
        s_dtw = sem("dtw_loaded")
        s_sel = sem("selectors_loaded")
        s_late = sem("late_weights_loaded")
        s_route = sem("routing_constants_loaded")
        s_y = sem("embedding_in_psum")
        s_v = sem("vector_chain")
        s_a = sem("scalar_chain")
        s_var = sem("variance_ready")
        s_lnv = sem("log_variance_done")
        s_rs = sem("rstd_guess_ready")
        s_zn = sem("normalised_tiles")
        s_zt = sem("transposed_in_psum")
        s_ztc = sem("transposed_copied")
        s_h = sem("down_in_psum")
        s_hf = sem("hF_ready")
        s_hr = sem("hR_ready")
        s_xs = sem("xs_in_psum")
        s_xsc = sem("xs_copied")
        s_xc0 = sem("conv_first_tap")
        s_hw = sem("halved_weights")
        s_xc = sem("conv_done")
        s_th = sem("tanh_done")
        s_u = sem("u_ready")
        s_zp = sem("z_in_psum")
        s_zth = sem("z_tanh_done")
        s_sz = sem("silu_z_ready")
        s_xp = sem("xproj_in_psum")
        s_xdt = sem("dt_rows_copied")
        s_hi = sem("high_parts")
        s_r1 = sem("first_rests")
        s_mid = sem("middle_parts")
        s_lo = sem("low_parts")
        s_dtp = sem("dt_in_psum")
        s_ab = sem("abs_done")
        s_lg = sem("log_done")
        s_relu = sem("relu_done")
        s_dt = sem("dt_ready")
        s_midc = sem("middle_part_of_C")
        s_loc = sem("low_part_of_C")
        s_du = sem("du_ready")
        s_aexp = sem("A_exponential")
        s_nA = sem("negA_ready")
        s_zero = sem("borders_zeroed")
        s_uD = sem("uD_ready")
        s_zs = sem("z_copied")
        s_szh = sem("z_times_tanh")
        s_ysb = sem("y_copied")
        s_brow = sem("bias_row_loaded")
        s_B = [sem(f"B_in_psum{i}") for i in range(2)]
        s_C = [sem(f"C_in_psum{i}") for i in range(2)]
        s_Bs = [sem(f"B_copied{i}") for i in range(2)]
        s_dA = [sem(f"dA_ready{i}") for i in range(2)]
        s_dbu = [sem(f"dBu_ready{i}") for i in range(4)]
        s_scan = [sem(f"scan_done{i}") for i in range(2)]
        s_hc = [sem(f"hC_ready{i}") for i in range(2)]
        s_acc = [sem(f"hC_summed{i}") for i in range(2)]
        s_gate = sem("y_gated")
        s_gr = sem("y_reversed")
        s_o = sem("mixer_out_in_psum")
        s_yn = sem("mixer_normed")
        s_yt = sem("y_transposed")
        s_ytc = sem("yT_ready")
        s_up = sem("up_in_psum")
        s_x2 = sem("ffn_input_ready")
        s_xt = sem("ffn_input_transposed")
        s_xtc = sem("ffn_input_T_ready")
        s_lgp = sem("logits_in_psum")
        s_m = sem("score_gap_ready")
        s_em = sem("score_exp_ready")
        s_oh = sem("onehot_ready")
        s_pos = sem("positions_in_psum")
        s_row = sem("rows_ready")
        s_disp = sem("dispatch_tiles")
        s_xh = sem("xhi_ready")
        s_xrr = sem("xrest_ready")
        s_xl = sem("xlo_ready")
        s_g = sem("gathered_in_psum")
        s_gc = [sem(f"gathered_copied{k}") for k in range(2)]
        s_w1 = [sem(f"up_weights{i}") for i in range(2)]
        s_w2 = [sem(f"down_weights{i}") for i in range(2)]
        s_hp = [sem(f"hidden_in_psum{i}") for i in range(2)]
        s_ht = [sem(f"gate_tanh{i}") for i in range(2)]
        s_hg = [sem(f"gate_product{i}") for i in range(2)]
        s_act = [sem(f"hidden_ready{i}") for i in range(2)]
        s_ye = [sem(f"expert_out_in_psum{i}") for i in range(2)]
        s_yec = [sem(f"expert_out_copied{i}") for i in range(2)]
        s_yst = [sem(f"expert_out_stored{i}") for i in range(2)]
        s_zs = sem("zero_row_stored")
        s_zr = sem("zero_row_ready")
        s_back = [sem(f"rows_gathered{t}") for t in range(TILES)]
        s_out = sem("result_ready")
        s_fin = sem("result_stored")


        block = ctx.enter_context(nc.Block())

        @block.sync
        def _(sp):
            sp.dma_start(brow[:], a["brow"]).then_inc(s_brow, 16)
            for k in range(PK):
                sp.dma_start(xT[:, k, :], a["xT"][:, k, :]).then_inc(s_px[k], 16)
            sp.dma_start(base[:], a["base"]).then_inc(s_par, 16)
            sp.dma_start(ident[:], a["ident"]).then_inc(s_id, 16)
            sp.dma_start(xpw[:], a["xpw"]).then_inc(s_xpw, 16)
            sp.dma_start(sel[:], a["sel"]).then_inc(s_sel, 16)
            sp.dma_start(outw[:], a["outw"]).then_inc(s_late, 16)
            sp.dma_start(tri[:], a["tri"]).then_inc(s_route, 16)
            sp.dma_start(ones[:], a["ones"]).then_inc(s_route, 16)
            sp.dma_start(iota[:], a["iota"]).then_inc(s_route, 16)
            for i in range(2):
                sp.dma_start(w1s[i][:], a["W1"][i]).then_inc(s_w1[i], 16)
                sp.dma_start(w2s[i][:], a["W2"][i]).then_inc(s_w2[i], 16)
            sp.wait_ge(s_zr, 1)
            sp.dma_start(ybuf[SLOTS:SLOTS + 1, :], zrow[:]).then_inc(s_zs, 16)
            for i in range(2):
                sp.sem_inc(s_yst[i], 16)
            yv = ybuf[0:SLOTS, :].rearrange("(k e c) d -> e c k d", k=TOP, e=E)

            def load_up(e, slot, done):
                sp.wait_ge(s_hp[1], done)
                sp.dma_start(w1s[slot][:], a["W1"][bass.ds(e, 1)].rearrange("o p k h -> (o p) k h")).then_inc(s_w1[slot], 16)

            def load_down(e, slot):
                sp.dma_start(w2s[slot][:], a["W2"][bass.ds(e, 1)].rearrange("o p k h -> (o p) k h")).then_inc(s_w2[slot], 16)

            def store(e, slot, uses):
                sp.wait_ge(s_yec[slot], uses + 1)
                sp.dma_start(yv[bass.ds(e, 1)].rearrange("o c k d -> (o c) k d"), ye[slot][:]).then_inc(s_yst[slot], 16)

            load_up(2, 0, 1)
            with sp.Fori(0, E // 2 - 2) as j:
                for i in range(2):
                    load_up(j * 2 + (i + 3), 1 - i, j * 2 + (i + 2))
                    store(j * 2 + i, i, j + 1)
                    load_down(j * 2 + (i + 2), i)
            load_up(E - 1, 1, E - 2)
            for i in range(2):
                store(E - 4 + i, i, E // 2 - 1)
                load_down(E - 2 + i, i)
            for i in range(2):
                store(E - 2 + i, i, E // 2)
            for t in range(TILES):
                rows = min(P, N - t * P)
                sp.wait_ge(s_out, t + 1)
                sp.dma_start(a["out"][t * P:t * P + rows, :], back[0:rows, t, 0, :]).then_inc(s_fin, 16)
            sp.wait_ge(s_fin, 16 * TILES)

        @block.gpsimd
        def _(pool):
            nc.gpsimd.memset(dA[0][:], 0.0).then_inc(s_zero, 1)
            nc.gpsimd.memset(dA[1][:], 0.0).then_inc(s_zero, 1)
            nc.gpsimd.memset(g[:, :, N:], 0.0).then_inc(s_zero, 1)
            nc.gpsimd.memset(zrow[:], 0.0).then_inc(s_zr, 1)
            for c in range(CC):
                pool.wait_ge(s_u, c + 1)
                nc.gpsimd.tensor_scalar(uD[:, c, :], u[:, c, :], chanp[:, c, C_D:C_D + 1], None, ALU.mult).then_inc(s_uD, 1)
            pool.wait_ge(s_r1, 2)
            pool.wait_ge(s_uD, CC)
            nc.gpsimd.tensor_copy(cparts[2 * NS:4 * NS, :], bcr[XC:XDT, :]).then_inc(s_midc, 1)
            pool.wait_ge(s_midc, 1)
            nc.gpsimd.tensor_tensor(cparts[4 * NS:6 * NS, :], bcr[XC:XDT, :], cparts[2 * NS:4 * NS, :], ALU.subtract).then_inc(s_loc, 1)
            pool.wait_ge(s_loc, 1)
            for c in range(CC):
                pool.wait_ge(s_zth, c + 1)
                nc.gpsimd.tensor_tensor(sz[:, c, :], sz[:, c, :], zs[:, c, :], ALU.mult).then_inc(s_szh, 1)
                pool.wait_ge(s_szh, c + 1)
                nc.gpsimd.tensor_tensor(sz[:, c, :], sz[:, c, :], zs[:, c, :], ALU.add).then_inc(s_sz, 1)

            def pool_quad(c, q):
                for i in range(4):
                    pool.wait_ge(s_Bs[i % 2], q * 2 + (c * 8 + i // 2 + 1))
                    nc.gpsimd.tensor_tensor(dBu[i], du[:, c, :], Bs[i % 2][:], ALU.mult).then_inc(s_dbu[i], 1)

            for i in range(4):
                pool.sem_inc(s_dbu[i], 1)
            for c in range(CC):
                pool.wait_ge(s_du, c + 1)
                if c == 0:
                    with pool.Fori(0, QUADS) as q:
                        pool_quad(c, q)
                    pool.wait_ge(s_lg, CC)
                    nc.gpsimd.memset(gR[:, :, N:], 0.0).then_inc(s_zero, 1)
                else:
                    with pool.Fori(0, QUADS - 1) as q:
                        pool_quad(c, q)
                    pool.wait_ge(s_ysb, c)
                    if c == 1:
                        nc.gpsimd.tensor_tensor(g[:, 0, 0:N], ysb, sz[:, 0, :], ALU.mult).then_inc(s_gate, 1)
                    else:
                        nc.gpsimd.tensor_tensor(g[:, 1, 0:N], ysb, sz[:, 1, :], ALU.mult).then_inc(s_gate, 1)
                        nc.gpsimd.tensor_tensor(gR[:, 0, 0:N][:, ::-1], ysb, sz[:, 1, :], ALU.mult).then_inc(s_gate, 1)
                    pool_quad(c, QUADS - 1)
            pool.wait_ge(s_row, 1)
            pool.wait_ge(s_zs, 16)
            for i in range(2):
                pool.wait_ge(s_yst[i], 16 * (E // 2 + 1))
            for t in range(TILES):
                for k in range(TOP):
                    pool.indirect_dma_start(
                        out=back[:, t, k, :], out_offset=None, in_=ybuf,
                        in_offset=bass.IndirectOffsetOnAxis(ap=rowu[:, t, k:k + 1], axis=0)
                    ).then_inc(s_back[t], 16)

        @block.scalar
        def _(act):
            chain = [0]

            def link(ins):
                chain[0] += 1
                ins.then_inc(s_a, 1)
                act.wait_ge(s_a, chain[0])

            def log_rstd(n, cols):
                act.wait_ge(s_var, n)
                link(nc.scalar.activation(lnv[:, :, 0:cols], mv[:, :, 0:cols, 1], ACT.Ln))
                nc.scalar.activation(rst[:, :, 0:cols], lnv[:, :, 0:cols], ACT.Exp, scale=-0.5).then_inc(s_rs, 1)

            for k in range(PK):
                act.dma_start(tokW[:, k, :], a["tokW"][:, k, :]).then_inc(s_px[k], 16)
            act.dma_start(rowp[:], a["rowp"].broadcast_to([P, RPAR])).then_inc(s_par, 16)
            act.dma_start(kcon[:], a["kcon"]).then_inc(s_par, 16)
            act.dma_start(w96[:], a["w96"]).then_inc(s_w96, 16)
            act.dma_start(col96[:], a["col96"]).then_inc(s_w96, 16)
            act.dma_start(chanp[:], a["chanp"]).then_inc(s_chp, 16)
            act.dma_start(dtw[XDT:XROWS, :], a["dtw"]).then_inc(s_dtw, 16)
            act.preload_act_table_set("natural_log_exp_and_others")
            log_rstd(1, 1)
            log_rstd(2, 1)
            act.preload_act_table_set("exp_and_others")
            act.wait_ge(s_zt, 3)
            nc.scalar.activation(znT[:, 512:1024], ps[0:DK, 6, :], ACT.Copy).then_inc(s_ztc, 1)
            nc.scalar.activation(znT[:, 1024:1280], ps[0:DK, 7, 0:256], ACT.Copy).then_inc(s_ztc, 1)
            act.wait_ge(s_hf, 1)
            nc.scalar.activation(hR[:], hF[:, ::-1], ACT.Copy).then_inc(s_hr, 1)
            act.wait_ge(s_hw, 1)
            for c in range(CC):
                act.wait_ge(s_xs, c + 1)
                link(nc.scalar.activation(split(xs[:, c, :]), halves(2 * c + 2), ACT.Copy))
                nc.scalar.activation(xc[:, c, :], xs[:, c, :], ACT.Identity, bias=halfw[:, c, TAPS:TAPS + 1],
                                     scale=halfw[:, c, TAPS - 1:TAPS]).then_inc(s_xc0, 1)
            for c in range(CC):
                act.wait_ge(s_xc, c + 1)
                nc.scalar.activation(th[:, c, :], xc[:, c, :], ACT.Tanh).then_inc(s_th, 1)
                act.wait_ge(s_zp, c + 1)
                nc.scalar.activation(split(sz[:, c, :]), halves(2 * c), ACT.Tanh, scale=0.5)
                nc.scalar.activation(split(zs[:, c, :]), halves(2 * c), ACT.Copy).then_inc(s_zth, 1)
            act.preload_act_table_set("natural_log_exp_and_others")
            nc.scalar.activation(negA[:].rearrange("p (c n) -> p c n", c=CC), chanp[:, :, C_A:C_A + NS], ACT.Exp).then_inc(s_aexp, 1)
            act.wait_ge(s_xp, 1)
            nc.scalar.activation(split(xdt[XDT:XROWS, :]), ps[XDT:XROWS, 6:8, 0:HALF], ACT.Copy).then_inc(s_xdt, 1)
            nc.scalar.activation(split(bparts[2 * NS:4 * NS, :]), ps[XB:XC, 6:8, 0:HALF], ACT.Copy).then_inc(s_hi, 1)
            nc.scalar.activation(split(cparts[0:2 * NS, :]), ps[XC:XDT, 6:8, 0:HALF], ACT.Copy).then_inc(s_hi, 1)
            for c in range(CC):
                act.wait_ge(s_dtp, c + 1)
                nc.scalar.activation(split(ab[:, c, :]), halves(2 * c), ACT.Abs, bias=chanp[:, c, C_DTB:C_DTB + 1]).then_inc(s_ab, 1)
                if c == 0:
                    act.wait_ge(s_r1, 1)
                    nc.scalar.activation(bparts[0:2 * NS, :], bcr[XB:XC, :], ACT.Copy).then_inc(s_mid, 1)
            for c in range(CC):
                act.wait_ge(s_ab, c + 1)
                link(nc.scalar.activation(ex[:, c, :], ab[:, c, :], ACT.Exp, scale=-1.0))
                nc.scalar.activation(lg[:, c, :], ex[:, c, :], ACT.Ln, bias=1.0).then_inc(s_lg, 1)
            act.wait_ge(s_zero, 3)
            act.wait_ge(s_nA, 1)

            def copy_b(slot, uses):
                act.wait_ge(s_B[slot], uses)
                nc.scalar.activation(split(Bs[slot][:]), halves(2), ACT.Copy).then_inc(s_Bs[slot], 1)

            def act_quad(c, q, copies, mid=None):
                for pair in range(2):
                    for i in range(2):
                        act.wait_ge(s_scan[i], q * 2 + (c * 8 + pair + 1))
                        nc.scalar.activation(img(dA[i][:], 1, SEQ), img(dt[:, c, :], 1, SEQ), ACT.Exp,
                                             scale=negA[:, bass.ds(q * 4 + (c * NS + 2 * pair + i), 1)]).then_inc(s_dA[i], 1)
                    for i in range(2):
                        if 2 * pair + i < copies:
                            act.wait_ge(s_dbu[2 * pair + i], q + (c * QUADS + 2))
                            copy_b(i, q * 2 + (c * 8 + pair + 2))
                    if pair == 0 and mid:
                        mid()

            def copy_y(c):
                for i in range(2):
                    act.wait_ge(s_acc[i], 8 * (c + 1) + 1)
                if c > 0:
                    act.wait_ge(s_gate, c)
                nc.scalar.activation(split(ysb), halves(0), ACT.Copy, scale=0.5).then_inc(s_ysb, 1)

            copy_b(0, 1)
            copy_b(1, 1)
            for c in range(CC):
                act.wait_ge(s_dt, c + 1)
                if c > 0:
                    act_quad(c, 0, 4, lambda: copy_y(c - 1))
                with act.Fori(min(c, 1), QUADS - (c == CC - 1)) as q:
                    act_quad(c, q, 4)
            act_quad(CC - 1, QUADS - 1, 2)
            log_rstd(3, 2)
            act.wait_ge(s_yt, TILES)
            nc.scalar.activation(yT[:, 0:512], ps[0:BN, 3, :], ACT.Identity, bias=bsum[:, 0:1]).then_inc(s_ytc, 1)
            nc.scalar.activation(yT[:, 512:640], ps[0:BN, 4, 0:128], ACT.Identity, bias=bsum[:, 0:1]).then_inc(s_ytc, 1)
            log_rstd(4, 1)
            act.preload_act_table_set("exp_and_others")
            act.wait_ge(s_xt, 3)
            nc.scalar.activation(xfT[:, 512:1024], ps[0:DK, 6, :], ACT.Copy).then_inc(s_xtc, 1)
            nc.scalar.activation(xfT[:, 1024:1280], ps[0:DK, 7, 0:256], ACT.Copy).then_inc(s_xtc, 1)
            nc.scalar.activation(xhi[:], zn[:], ACT.Copy, scale=SPLIT).then_inc(s_xh, 1)
            act.wait_ge(s_m, 1)
            nc.scalar.activation(em[:], dm[:], ACT.Exp).then_inc(s_em, 1)
            act.wait_ge(s_xrr, 1)
            nc.scalar.activation(xlo[:], xr[:], ACT.Copy).then_inc(s_xl, 1)
            for q in range(4):
                act.wait_ge(s_g, 2 * q + 1)
                cols = slice(q * SLOTS // 4, (q + 1) * SLOTS // 4)
                nc.scalar.activation(xgT[:, 0, cols], ps[0:DK, 4 + 2 * (q % 2), 0:SLOTS // 4], ACT.Copy,
                                     scale=1.0 / SPLIT).then_inc(s_gc[0], 1)
            for i in range(2):
                act.sem_inc(s_yec[i], 1)
            def gate_tanh(j, i):
                for s in range(2):
                    act.wait_ge(s_hp[s], j * 2 + (i + 1))
                    act.wait_ge(s_hg[s], j * 2 + (i + 1))
                    nc.scalar.activation(thg[s][:], ps[:, 2 * s:2 * s + 2, 2 * CAP:4 * CAP], ACT.Tanh,
                                         scale=0.5).then_inc(s_ht[s], 1)

            def copy_out(j, i):
                act.wait_ge(s_ye[i], j + 2)
                act.wait_ge(s_yst[i], j * 16 + 16)
                nc.scalar.activation(ye[i][:], ps[0:CAP, 4 + i, 0:TOP * D].rearrange("p (k d) -> p k d", k=TOP),
                                     ACT.Copy).then_inc(s_yec[i], 1)

            gate_tanh(0, 0)
            with act.Fori(0, E // 2 - 1) as j:
                gate_tanh(j, 1)
                copy_out(j, 0)
                gate_tanh(j + 1, 0)
                copy_out(j, 1)
            gate_tanh(E // 2 - 1, 1)
            copy_out(E // 2 - 1, 0)
            copy_out(E // 2 - 1, 1)

        @block.vector
        def _(dve):
            chain = [0]
            V = nc.vector

            def link(ins):
                chain[0] += 1
                ins.then_inc(s_v, 1)
                dve.wait_ge(s_v, chain[0])

            def step(ins):
                chain[0] += 1
                ins.then_inc(s_v, 1)

            def settle():
                dve.wait_ge(s_v, chain[0])

            def moments(n, cols, src):
                for t in range(TILES):
                    for d in range(cols):
                        step(V.bn_stats(stats[:, t, d, :], src(t, d)))
                settle()
                for t in range(TILES):
                    for d in range(cols):
                        step(V.bn_aggr(mv[:, t, d, :], stats[:, t, d, :]))
                settle()
                V.tensor_scalar(mv[:, :, 0:cols, 1], mv[:, :, 0:cols, 1], EPS, None, ALU.add).then_inc(s_var, 1)

            def newton(n, cols):
                r, w, v = rst[:, :, 0:cols], nt[:, :, 0:cols], mv[:, :, 0:cols, 1]
                dve.wait_ge(s_var, n)
                dve.wait_ge(s_rs, n)
                link(V.tensor_tensor(w, r, r, ALU.mult))
                link(V.scalar_tensor_tensor(w, w, -0.5, v, ALU.mult, ALU.mult))
                link(V.scalar_tensor_tensor(r, w, 1.5, r, ALU.add, ALU.mult))

            dve.wait_ge(s_y, TILES)
            moments(1, 1, lambda t, d: ps[:, t, 0:D])
            newton(1, 1)
            for t in range(TILES):
                step(V.tensor_scalar(h0[:, t, :], ps[:, t, 0:D], mv[:, t, 0, 0:1], rst[:, t, 0:1], ALU.subtract, ALU.mult))
            settle()
            dve.wait_ge(s_par, 48)
            link(V.tensor_tensor(h0[:], h0[:], rowp[:, None, R_LW:R_LW + D].broadcast_to([P, TILES, D]), ALU.mult))
            link(V.tensor_tensor(h0[:], h0[:], base[:], ALU.add))
            moments(2, 1, lambda t, d: h0[:, t, :])
            newton(2, 1)
            for t in range(TILES):
                V.tensor_scalar(zn[:, t, :], h0[:, t, :], mv[:, t, 0, 0:1], rst[:, t, 0:1],
                                ALU.subtract, ALU.mult).then_inc(s_zn, 1)
            dve.wait_ge(s_zn, TILES)
            step(V.tensor_tensor(h0[:], h0[:], rowp[:, None, R_UB:R_UB + D].broadcast_to([P, TILES, D]), ALU.add))
            dve.wait_ge(s_zt, 1)
            V.tensor_copy(znT[:, 0:512], ps[0:DK, 5, :]).then_inc(s_ztc, 1)
            dve.wait_ge(s_chp, 16)
            V.tensor_scalar(halfw[:], chanp[:, :, 0:TAPS + 1], 0.5, None, ALU.mult).then_inc(s_hw, 1)
            dve.wait_ge(s_w96, 32)
            step(V.tensor_tensor(bsum[:], col96[:, 1:2], col96[:, 2:3], ALU.add))
            dve.wait_ge(s_h, 1)
            V.tensor_scalar(split(hF[:]), ps[0:BN, 0:2, 0:HALF], col96[:, 0:1], None, ALU.add).then_inc(s_hf, 1)
            dve.wait_ge(s_hw, 1)
            for c in range(CC):
                dve.wait_ge(s_xc0, c + 1)
                for k in range(1, TAPS):
                    o = img(xc[:, c, :], k, SEQ)
                    ins = V.scalar_tensor_tensor(o, img(xs[:, c, :], 0, SEQ - k), halfw[:, c, TAPS - 1 - k:TAPS - k], o,
                                                 ALU.mult, ALU.add)
                    if k < TAPS - 1:
                        link(ins)
                    else:
                        ins.then_inc(s_xc, 1)
            for c in range(CC):
                dve.wait_ge(s_th, c + 1)
                V.scalar_tensor_tensor(u[:, c, :], th[:, c, :], 1.0, xc[:, c, :], ALU.add, ALU.mult).then_inc(s_u, 1)
            dve.wait_ge(s_hi, 1)
            V.tensor_tensor(split(bcr[XB:XC, :]), ps[XB:XC, 6:8, 0:HALF], split(bparts[2 * NS:4 * NS, :]), ALU.subtract).then_inc(s_r1, 1)
            dve.wait_ge(s_hi, 2)
            V.tensor_tensor(split(bcr[XC:XDT, :]), ps[XC:XDT, 6:8, 0:HALF], split(cparts[0:2 * NS, :]), ALU.subtract).then_inc(s_r1, 1)
            dve.wait_ge(s_aexp, 1)
            V.tensor_scalar(negA[:], negA[:], -1.0, None, ALU.mult).then_inc(s_nA, 1)
            for c in range(CC):
                dve.wait_ge(s_ab, c + 1)
                V.tensor_scalar(split(dt[:, c, :]), halves(2 * c), chanp[:, c, C_DTB:C_DTB + 1], 0.0, ALU.add, ALU.max).then_inc(s_relu, 1)
                if c == 0:
                    dve.wait_ge(s_mid, 1)
                    V.tensor_tensor(bparts[4 * NS:6 * NS, :], bcr[XB:XC, :], bparts[0:2 * NS, :], ALU.subtract).then_inc(s_lo, 1)
            for c in range(CC):
                dve.wait_ge(s_relu, c + 1)
                dve.wait_ge(s_lg, c + 1)
                V.tensor_tensor(dt[:, c, :], dt[:, c, :], lg[:, c, :], ALU.add).then_inc(s_dt, 1)
                dve.wait_ge(s_dt, c + 1)
                V.tensor_tensor(du[:, c, :], dt[:, c, :], u[:, c, :], ALU.mult).then_inc(s_du, 1)
            dve.wait_ge(s_zero, 3)
            for i in range(2):
                dve.sem_inc(s_scan[i], 1)
                dve.sem_inc(s_hc[i], 1)

            def dve_quad(c, q):
                for pair in range(2):
                    uses = q * 2 + (c * 8 + pair)
                    for i in range(2):
                        dve.wait_ge(s_dA[i], uses + 1)
                        dve.wait_ge(s_dbu[2 * pair + i], q + (c * QUADS + 2))
                        dve.wait_ge(s_hc[i], uses + 1)
                        V.tensor_tensor_scan(hs[i][:], dA[i][:], dBu[2 * pair + i], 0.0, ALU.mult, ALU.add).then_inc(s_scan[i], 1)
                    for i in range(2):
                        dve.wait_ge(s_C[i], uses + 1)
                        dve.wait_ge(s_acc[i], uses + 1)
                        dve.wait_ge(s_scan[i], uses + 2)
                        V.tensor_tensor(split(hc[i][:]), split(hs[i][:]), halves(4 + 2 * i), ALU.mult).then_inc(s_hc[i], 1)

            for c in range(CC):
                with dve.Fori(0, QUADS) as q:
                    dve_quad(c, q)
            dve.wait_ge(s_sz, CC)
            dve.wait_ge(s_zero, 4)
            for i in range(2):
                dve.wait_ge(s_acc[i], 8 * CC + 1)
            V.scalar_tensor_tensor(split(gR[:, 1, 0:N][:, ::-1]), halves(0), 0.5, split(sz[:, 2, :]),
                                   ALU.mult, ALU.mult).then_inc(s_gr, 1)
            dve.wait_ge(s_o, TILES)
            o_of = lambda t, d: ps[:, d, t * BN:(t + 1) * BN]
            moments(3, 2, o_of)
            newton(3, 2)
            for t in range(TILES):
                for d in range(2):
                    step(V.tensor_scalar(yn[:, t, d * BN:(d + 1) * BN], o_of(t, d), mv[:, t, d, 0:1], rst[:, t, d:d + 1],
                                         ALU.subtract, ALU.mult))
            settle()
            link(V.tensor_tensor(yn[:], yn[:], rowp[:, None, R_G:R_G + 2 * BN].broadcast_to([P, TILES, 2 * BN]), ALU.mult))
            V.tensor_tensor(yn[:, :, 0:BN], yn[:, :, 0:BN], yn[:, :, BN:2 * BN], ALU.add).then_inc(s_yn, 1)
            for t in range(TILES):
                dve.wait_ge(s_up, min(t // 2 * 2 + 2, TILES))
                step(V.tensor_tensor(h0[:, t, :], h0[:, t, :], ps[:, t // 2, (t % 2) * D:(t % 2 + 1) * D], ALU.add))
            settle()
            moments(4, 1, lambda t, d: h0[:, t, :])
            newton(4, 1)
            for t in range(TILES):
                V.tensor_scalar(zn[:, t, :], h0[:, t, :], mv[:, t, 0, 0:1], rst[:, t, 0:1],
                                ALU.subtract, ALU.mult).then_inc(s_x2, 1)
            dve.wait_ge(s_xt, 1)
            V.tensor_copy(xfT[:, 0:512], ps[0:DK, 5, :]).then_inc(s_xtc, 1)
            dve.wait_ge(s_xh, 1)
            V.scalar_tensor_tensor(xr[:], zn[:], SPLIT, xhi[:], ALU.mult, ALU.subtract).then_inc(s_xrr, 1)
            rev = kcon[:, None, K_REV:K_REV + E].broadcast_to([P, TILES, E])
            real = kcon[:, K_REAL:K_REAL + TILES].rearrange("p (t o) -> p t o", o=1).broadcast_to([P, TILES, E])
            dve.wait_ge(s_lgp, 1)
            link(V.tensor_copy(lgt[:], ps[:, 4, 0:TILES * E].rearrange("p (t e) -> p t e", e=E)))
            for k in range(TOP):
                src = (lgt, lg2)[k]
                link(V.tensor_reduce(mx[:, k, :], src[:], AX.X, ALU.max))
                link(V.tensor_tensor(key[:], src[:], mx[:, k, :].rearrange("p (t o) -> p t o", o=1).broadcast_to([P, TILES, E]), ALU.is_equal))
                link(V.tensor_tensor(key[:], key[:], rev, ALU.mult))
                link(V.tensor_reduce(km[:], key[:], AX.X, ALU.max))
                link(V.tensor_tensor(oh[:, k], rev, km[:].rearrange("p (t o) -> p t o", o=1).broadcast_to([P, TILES, E]), ALU.is_equal))
                if k == 0:
                    link(V.scalar_tensor_tensor(lg2[:], oh[:, 0], -3.0e38, lgt[:], ALU.mult, ALU.add))
            V.tensor_tensor(dm[:], mx[:, 1, :], mx[:, 0, :], ALU.subtract).then_inc(s_m, 1)
            for k in range(TOP):
                step(V.tensor_tensor(ohm[:, k], oh[:, k], real, ALU.mult))
            settle()
            V.tensor_copy(ohb[:].rearrange("p t k e -> p k t e"), ohm[:]).then_inc(s_oh, 1)
            dve.wait_ge(s_em, 1)
            link(V.tensor_scalar(wts[:, 1, :], em[:], 1.0, None, ALU.add))
            link(V.reciprocal(wts[:, 0, :], wts[:, 1, :]))
            step(V.tensor_tensor(wts[:, 1, :], em[:], wts[:, 0, :], ALU.mult))
            dve.wait_ge(s_pos, 1)
            link(V.tensor_tensor(psel[:], ps[:, 5, 0:TILES * TOP * E].rearrange("p (t k e) -> p t k e", k=TOP, e=E), ohb[:], ALU.mult))
            link(V.tensor_reduce(pos[:], psel[:], AX.X, ALU.add))
            for k in range(TOP):
                link(V.tensor_tensor(psel[:, :, k, :], ohm[:, k], kcon[:, None, K_BASE:K_BASE + E].broadcast_to([P, TILES, E]), ALU.mult))
            link(V.tensor_reduce(eb[:], psel[:], AX.X, ALU.add))
            link(V.scalar_tensor_tensor(slot[:], pos[:], -1.0, eb[:], ALU.add, ALU.add))
            link(V.tensor_scalar(over[:], pos[:], float(CAP), DROP, ALU.is_gt, ALU.mult))
            link(V.tensor_tensor(slot[:], slot[:], over[:], ALU.add))
            dve.wait_ge(s_route, 48)
            for k in range(TOP):
                for t in range(TILES):
                    V.tensor_scalar(disp[:, t, k * KSLOTS:(k + 1) * KSLOTS], iota[:], slot[:, t, k:k + 1], None,
                                    ALU.is_equal).then_inc(s_disp, 1)
            link(V.tensor_scalar(row[:], slot[:], 0.0, None, ALU.max))
            link(V.tensor_scalar(row[:, :, 1], row[:, :, 1], float(KSLOTS), None, ALU.add))
            link(V.tensor_scalar(row[:], row[:], float(SLOTS), None, ALU.min))
            V.tensor_copy(rowu[:], row[:]).then_inc(s_row, 1)
            for q in range(4):
                dve.wait_ge(s_g, 2 * q + 2)
                cols = slice(q * SLOTS // 4, (q + 1) * SLOTS // 4)
                V.tensor_scalar(xgT[:, 1, cols], ps[0:DK, 5 + 2 * (q % 2), 0:SLOTS // 4], 1.0 / SPLIT, None,
                                ALU.mult).then_inc(s_gc[1], 1)
            for i in range(2):
                dve.sem_inc(s_hg[i], 1)
                dve.sem_inc(s_act[i], 1)
            with dve.Fori(0, E // 2) as j:
                for i in range(2):
                    for s in range(2):
                        dve.wait_ge(s_ht[s], j * 2 + i + 1)
                        V.scalar_tensor_tensor(gt[s][:], thg[s][:], 1.0, ps[:, 2 * s:2 * s + 2, 2 * CAP:4 * CAP],
                                               ALU.add, ALU.mult).then_inc(s_hg[s], 1)
                        dve.wait_ge(s_hg[s], j * 2 + i + 2)
                        dve.wait_ge(s_ye[i], j + 1)
                        V.scalar_tensor_tensor(act_t[i][:, 2 * s:2 * s + 2, :], gt[s][:], 0.5,
                                               ps[:, 2 * s:2 * s + 2, 0:2 * CAP], ALU.mult, ALU.mult).then_inc(s_act[s], 1)
            for t in range(TILES):
                dve.wait_ge(s_back[t], 16 * TOP)
                link(V.scalar_tensor_tensor(h0[:, t, :], back[:, t, 0, :], wts[:, 0, t:t + 1], h0[:, t, :], ALU.mult, ALU.add))
                V.scalar_tensor_tensor(back[:, t, 0, :], back[:, t, 1, :], wts[:, 1, t:t + 1], h0[:, t, :],
                                       ALU.mult, ALU.add).then_inc(s_out, 1)

        @block.tensor
        def _(pe):
            mm = nc.tensor.matmul

            pe.wait_ge(s_brow, 16)
            for t in range(TILES):
                mm(ps[:, t, 0:D], brow[:, t * P:(t + 1) * P], brow[:, NP_:NP_ + D], start=True, stop=False)
            for k in range(PK):
                pe.wait_ge(s_px[k], 32)
                for t in range(TILES):
                    last = mm(ps[:, t, 0:D], xT[:, k, t * P:(t + 1) * P], tokW[:, k, :], start=False, stop=k == PK - 1)
                    if k == PK - 1:
                        last.then_inc(s_y, 1)

            def transpose_rows(ready, done):
                for q in range(2 * TILES):
                    k, t = divmod(q, TILES)
                    pe.wait_ge(ready, t + 1 if k == 0 else TILES)
                    last = nc.tensor.transpose(ps[0:DK, 5 + q // 4, (q % 4) * P:(q % 4 + 1) * P],
                                               zn[:, t, k * DK:(k + 1) * DK], ident[:])
                    if q % 4 == 3 or q == 2 * TILES - 1:
                        last.then_inc(done, 1)

            pe.wait_ge(s_id, 16)
            transpose_rows(s_zn, s_zt)
            pe.wait_ge(s_w96, 32)
            pe.wait_ge(s_ztc, 3)
            for h in range(2):
                for k in range(2):
                    last = mm(ps[0:BN, h, 0:HALF], w96[:, W_DOWN + k * BN:W_DOWN + (k + 1) * BN],
                              znT[:, k * NP_ + h * HALF:k * NP_ + (h + 1) * HALF], start=k == 0, stop=k == 1)
            last.then_inc(s_h, 1)
            parts = [[(0, P, hF)], [(0, 64, hF), (64, P, hR)], [(0, P, hR)]]

            def in_proj(col, bank, c, done):
                for lo, hi, src in parts[c]:
                    for h in range(2):
                        last = mm(ps[lo:hi, bank + h, 0:HALF], w96[:, col + c * P + lo:col + c * P + hi],
                                  src[:, h * HALF:(h + 1) * HALF], start=True, stop=True)
                last.then_inc(done, 1)

            pe.wait_ge(s_hf, 1)
            in_proj(W_XS, 2, 0, s_xs)
            pe.wait_ge(s_hr, 1)
            in_proj(W_XS, 4, 1, s_xs)
            in_proj(W_XS, 6, 2, s_xs)
            for c in range(CC):
                if c > 0:
                    pe.wait_ge(s_xc0, c)
                in_proj(W_Z, 2 * c, c, s_zp)
            pe.wait_ge(s_xpw, 16)
            pe.wait_ge(s_xc0, 3)
            for c in range(CC):
                pe.wait_ge(s_u, c + 1)
                for h in range(2):
                    last = mm(ps[0:XROWS, 6 + h, 0:HALF], xpw[:, c, :], u[:, c, h * HALF:(h + 1) * HALF],
                              start=c == 0, stop=c == CC - 1)
            last.then_inc(s_xp, 1)
            pe.wait_ge(s_dtw, 16)
            pe.wait_ge(s_xdt, 1)
            for c in range(CC):
                pe.wait_ge(s_zth, c + 1)
                for h in range(2):
                    last = mm(ps[:, 2 * c + h, 0:HALF], dtw[XDT:XROWS, c * P:(c + 1) * P],
                              xdt[XDT:XROWS, h * HALF:(h + 1) * HALF], start=True, stop=True)
                last.then_inc(s_dtp, 1)

            def bcast(bank, parts, idx, done):
                for h in range(2):
                    last = mm(ps[:, bank + h, 0:HALF], sel[:, idx, :].rearrange("p o m -> p (o m)"),
                              parts[:, h * HALF:(h + 1) * HALF], start=True, stop=True)
                last.then_inc(done, 1)

            pe.wait_ge(s_sel, 16)
            pe.wait_ge(s_lo, 1)
            pe.wait_ge(s_relu, 2)
            bcast(2, bparts, slice(0, 1), s_B[0])
            pe.wait_ge(s_relu, CC)
            pe.wait_ge(s_loc, 1)
            for k in range(1, 4):
                pe.wait_ge(s_Bs[(k - 1) % 2], (k - 1) // 2 + 1)
                bcast(2, bparts, slice(k, k + 1), s_B[k % 2])
                if k < 3:
                    bcast(2 + 2 * k, cparts, slice(k - 1, k), s_C[k - 1])
            pe.wait_ge(s_uD, CC)
            for i in range(2):
                pe.sem_inc(s_acc[i], 1)

            def pe_quad(c, q, ahead=4):
                for i in range(4):
                    if ahead:
                        pe.wait_ge(s_Bs[(i + 1) % 2], q * 2 + (c * 8 + (i + 3) // 2 + 1))
                        bcast(2, bparts, bass.ds(q * 4 + (c * NS + i + 4), 1), s_B[i % 2])
                    pe.wait_ge(s_hc[i % 2], q * 2 + (c * 8 + i // 2 + 2))
                    for h in range(2):
                        last = mm(ps[:, h, 0:HALF], ident[:], hc[i % 2][:, h * HALF:(h + 1) * HALF],
                                  start=False, stop=False, skip_group_check=True)
                    last.then_inc(s_acc[i % 2], 1)
                    if i < 2 + ahead // 2:
                        bcast(4 + 2 * (i % 2), cparts, bass.ds(q * 4 + (c * NS + i + 2), 1), s_C[i % 2])

            for c in range(CC):
                if c > 0:
                    pe.wait_ge(s_ysb, c)
                for h in range(2):
                    mm(ps[:, h, 0:HALF], ident[:], uD[:, c, h * HALF:(h + 1) * HALF],
                       start=True, stop=False, skip_group_check=True)
                with pe.Fori(0, QUADS - (c == CC - 1)) as q:
                    pe_quad(c, q)
            pe_quad(CC - 1, QUADS - 1, ahead=0)
            pe.wait_ge(s_late, 16)
            pe.wait_ge(s_gate, 3)
            pe.wait_ge(s_zero, 4)
            pe.wait_ge(s_gr, 1)
            for t in range(TILES):
                rows = slice(t * P, (t + 1) * P)
                of, ob = (ps[:, d, t * BN:(t + 1) * BN] for d in range(2))
                mm(of, g[:, 0, rows], outw[:, 0, :], start=True, stop=False)
                mm(of, g[0:64, 1, rows], outw[0:64, 1, :], start=False, stop=True)
                mm(ob, gR[:, 1, rows], outw[:, 2, :], start=True, stop=False)
                mm(ob, gR[64:P, 0, rows], outw[64:P, 1, :], start=False, stop=True).then_inc(s_o, 1)
            pe.wait_ge(s_yn, 1)
            for t in range(TILES):
                nc.tensor.transpose(ps[0:BN, 3 + t // 4, (t % 4) * P:(t % 4 + 1) * P], yn[:, t, 0:BN],
                                    ident[:]).then_inc(s_yt, 1)
            pe.wait_ge(s_ytc, 2)
            for t in range(TILES):
                mm(ps[:, t // 2, (t % 2) * D:(t % 2 + 1) * D], yT[:, t * P:(t + 1) * P], w96[:, W_UP:W_UP + D],
                   start=True, stop=True).then_inc(s_up, 1)
            transpose_rows(s_x2, s_xt)
            pe.wait_ge(s_xtc, 3)
            for t in range(TILES):
                for k in range(2):
                    last = mm(ps[:, 4, t * E:(t + 1) * E], xfT[:, k * NP_ + t * P:k * NP_ + (t + 1) * P],
                              w96[:, W_G + k * E:W_G + (k + 1) * E], start=k == 0, stop=k == 1)
            last.then_inc(s_lgp, 1)
            pe.wait_ge(s_route, 48)
            pe.wait_ge(s_oh, 1)
            for t in range(TILES):
                for b in range(t + 1):
                    last = mm(ps[:, 5, t * TOP * E:(t + 1) * TOP * E], tri[:] if b == t else ones[:],
                              ohb[:, b].rearrange("p k e -> p (k e)"), start=b == 0, stop=b == t)
            last.then_inc(s_pos, 1)
            pe.wait_ge(s_xl, 1)
            for q in range(4):
                pe.wait_ge(s_disp, TILES if q < 2 else TILES * TOP)
                if q == 0:
                    pe.wait_ge(s_row, 1)
                for k in range(2):
                    if q >= 2:
                        pe.wait_ge(s_gc[k], q - 1)
                    n = 0
                    for t in range(TILES):
                        for part in (xhi, xlo):
                            last = mm(ps[0:DK, 4 + 2 * (q % 2) + k, 0:SLOTS // 4], part[:, t, k * DK:(k + 1) * DK],
                                      disp[:, t, q * SLOTS // 4:(q + 1) * SLOTS // 4], start=n == 0, stop=n == 2 * TILES - 1)
                            n += 1
                    last.then_inc(s_g, 1)
            for k in range(2):
                pe.wait_ge(s_gc[k], 4)
            for i in range(2):
                pe.sem_inc(s_ye[i], 1)

            def up(j, i):
                pe.wait_ge(s_w1[i], j * 16 + 16)
                for s in range(2):
                    pe.wait_ge(s_act[s], j * 2 + (i + 1))
                    for q in range(2 * s, 2 * s + 2):
                        for half in range(2):
                            for k in range(2):
                                src = xgT[:, k, :].rearrange("p (k e c) -> p e k c", k=TOP, e=E)[:, bass.ds(j * 2 + i, 1)]
                                col = half * H + q * P
                                last = mm(ps[:, q, half * 2 * CAP:(half + 1) * 2 * CAP].rearrange("p (k c) -> p k c", k=TOP),
                                          w1s[i][:, k, col:col + P], src.rearrange("p o k c -> p (o k) c"),
                                          start=k == 0, stop=k == 1)
                    last.then_inc(s_hp[s], 1)

            def down(j, i):
                pe.wait_ge(s_w2[i], j * 16 + 16)
                pe.wait_ge(s_yec[i], j + 1)
                for s in range(2):
                    pe.wait_ge(s_act[s], j * 2 + (i + 2))
                for k in range(TOP):
                    for q in range(HC):
                        last = mm(ps[0:CAP, 4 + i, k * D:(k + 1) * D], act_t[i][:, q, k * CAP:(k + 1) * CAP],
                                  w2s[i][:, q, :], start=q == 0, stop=q == HC - 1)
                last.then_inc(s_ye[i], 1)

            up(0, 0)
            with pe.Fori(0, E // 2 - 1) as j:
                up(j, 1)
                down(j, 0)
                up(j + 1, 0)
                down(j, 1)
            up(E // 2 - 1, 1)
            down(E // 2 - 1, 0)
            down(E // 2 - 1, 1)


def kernel(**inputs):
    import concourse.bacc as bacc
    import ml_dtypes
    from concourse.bass_utils import run_bass_kernel_spmd

    I = {k: np.asarray(v) for k, v in inputs.items()}
    f32 = np.float32

    def both(name):
        v = np.concatenate([I["L0_attn_f_" + name], I["L0_attn_b_" + name]], axis=0)
        return v.reshape((CC, P) + v.shape[1:]).swapaxes(0, 1)

    x = I["x"].reshape(IMAGES, 3, SIDE, PATCH, SIDE, PATCH).transpose(1, 3, 5, 0, 2, 4).reshape(PIX, IMAGES, SEQ - 1)
    xT = np.zeros((PIX, NP_), f32)
    xT[:, :N].reshape(PIX, IMAGES, SEQ)[:, :, 1:] = x
    base = np.zeros((NP_, D), f32)
    base[:N].reshape(IMAGES, SEQ, D)[:, 1:] = I["L0_tok_ln_b"]
    base[:N].reshape(IMAGES, SEQ, D)[:, 0] = I["cls_tok"].reshape(D)
    chanp = np.concatenate([both("conv_w"), both("conv_b")[..., None], both("dt_b")[..., None], both("D")[..., None],
                            both("A_log")], axis=2)
    rowp = np.concatenate([I["L0_tok_b"], I["L0_tok_ln_w"], I["L0_attn_up_b"], I["L0_attn_f_ln_g"],
                           I["L0_attn_b_ln_g"]])[None]
    col96 = np.stack([I["L0_attn_down_b"], I["L0_attn_f_ln_b"], I["L0_attn_b_ln_b"]], axis=1)

    def rows96(w):
        return w.reshape(2, DK, -1).transpose(1, 0, 2).reshape(DK, -1)

    brow = np.concatenate([((np.arange(NP_) < N) & (np.arange(NP_) % SEQ > 0)).astype(f32), I["L0_tok_b"]])[None]
    fi, bi = I["L0_attn_f_in_W"], I["L0_attn_b_in_W"]
    w96 = np.concatenate([rows96(I["L0_attn_down_W"]), fi[:, :DI], bi[:, :DI], fi[:, DI:], bi[:, DI:],
                          I["L0_attn_up_W"], rows96(I["L0_ffn_Wg"])], axis=1)
    xpw = np.zeros((CH, XROWS), f32)
    dtw = np.zeros((2 * R, CH), f32)
    sel = np.zeros((3, 2, NS, SEL, P), ml_dtypes.bfloat16)
    for d, w in enumerate("fb"):
        xw = I[f"L0_attn_{w}_xproj_W"]
        mine = slice(d * DI, (d + 1) * DI)
        xpw[mine, XB + d * NS:XB + (d + 1) * NS] = xw[:, R:R + NS]
        xpw[mine, XC + d * NS:XC + (d + 1) * NS] = xw[:, R + NS:]
        xpw[mine, XDT + d * R:XDT + (d + 1) * R] = xw[:, :R]
        dtw[d * R:(d + 1) * R, mine] = I[f"L0_attn_{w}_dt_W"]
        for i in range(SEL):
            c, n = divmod(i, NS)
            ch = np.arange(c * P, (c + 1) * P)
            sel[:, d, n, i, (ch >= d * DI) & (ch < (d + 1) * DI)] = 1
    tok = np.arange(NP_).reshape(TILES, P).T
    kcon = np.concatenate([((tok < N) & (tok % SEQ > 0)), tok < N, np.tile(E - np.arange(E), (P, 1)),
                           np.tile(CAP * np.arange(E), (P, 1))], axis=1).astype(f32)
    at = np.arange(P)
    arrays = {
        "xT": xT.reshape(PK, P, NP_).transpose(1, 0, 2),
        "tokW": I["L0_tok_W"].T.reshape(PK, P, D).transpose(1, 0, 2),
        "base": base.reshape(TILES, P, D).transpose(1, 0, 2),
        "chanp": chanp, "rowp": rowp, "col96": col96, "w96": w96, "kcon": kcon, "brow": brow,
        "xpw": xpw.reshape(CC, P, XROWS).transpose(1, 0, 2), "dtw": dtw,
        "outw": both("out_W"),
        "sel": sel.reshape(6 * NS, SEL, P),
        "ident": np.eye(P, dtype=f32),
        "tri": (at[:, None] <= at[None, :]).astype(ml_dtypes.bfloat16),
        "ones": np.ones((P, P), ml_dtypes.bfloat16),
        "iota": np.tile(np.arange(KSLOTS), (P, 1)).astype(np.float16),
        "W1": I["L0_ffn_W1"].reshape(E, 2, DK, 2 * H).transpose(0, 2, 1, 3),
        "W2": I["L0_ffn_W2"].reshape(E, HC, P, D).transpose(0, 2, 1, 3),
    }
    arrays = {k: np.ascontiguousarray(v) for k, v in arrays.items()}
    nc = bacc.Bacc("TRN2", target_bir_lowering=False, num_devices=1)
    aps = {k: nc.dram_tensor(k + "_dram", v.shape, mybir.dt.from_np(v.dtype), kind="ExternalInput").ap()
           for k, v in arrays.items()}
    aps["out"] = nc.dram_tensor("out_dram", (N, D), F32, kind="ExternalOutput").ap()
    vit_mamba_moe(nc, aps)
    r = run_bass_kernel_spmd(nc, [{k + "_dram": v for k, v in arrays.items()}], core_ids=[0])
    return r.results[0]["out_dram"].reshape(IMAGES, SEQ, D)
```

```python
from contextlib import ExitStack

import numpy as np

import concourse.bass as bass
from concourse import mybir

ALU = mybir.AluOpType
ACT = mybir.ActivationFunctionType
AX = mybir.AxisListType
F32 = mybir.dt.float32
BF16 = mybir.dt.bfloat16
F16 = mybir.dt.float16
U32 = mybir.dt.uint32

P = 128
IMAGES, PATCH, SIDE = 16, 16, 6
SEQ = SIDE * SIDE + 1
N = IMAGES * SEQ
HALF = N // 2
TILES = -(-N // P)
NP_ = TILES * P
D = 192
DK = D // 2
PIX = 3 * PATCH * PATCH
PK = PIX // P
BN = 96
DI = 192
CH = 2 * DI
CC = CH // P
NS, TAPS, R = 16, 4, 24
E, TOP, H = 8, 2, 512
CAP = int(1.2 * N / E)
HC = H // P
KSLOTS = E * CAP
SLOTS = TOP * KSLOTS
EPS = 1e-5
SPLIT = 1024.0
QUADS = NS // 4
SEL = CC * NS
DT_BANK = (2, 0, 4)
DROP = 4096.0

C_W, C_B, C_DTB, C_D, C_A = 0, TAPS, TAPS + 1, TAPS + 2, TAPS + 3
CPAR = C_A + NS
R_TB, R_LW, R_UB, R_G = 0, D, 2 * D, 3 * D
RPAR = R_G + 2 * BN
W_DOWN, W_XS, W_Z, W_UP, W_G = 0, 2 * BN, 2 * BN + CH, 2 * BN + 2 * CH, 2 * BN + 2 * CH + D
W96 = W_G + 2 * E
K_PATCH, K_REAL, K_REV, K_BASE, K_TOK = 0, TILES, 2 * TILES, 2 * TILES + E, 2 * TILES + 2 * E
KCON = K_TOK + TILES
EXT = 3
WARM = [7, 44, 2, 2, 12, 8, 20, 4, 24, 8, 16, 20, 4, 4]
XB, XC, XDT = 0, 2 * NS, 4 * NS
XROWS = XDT + 2 * R


def vit_mamba_moe(nc, a):
    with ExitStack() as ctx:
        def sb(name, shape, dt=F32):
            return ctx.enter_context(nc.sbuf_tensor(name, shape, dt))

        def sem(name):
            return ctx.enter_context(nc.semaphore(name))

        xT = sb("xT", [P, PK, NP_])
        tokW = sb("tokW", [P, PK, D])
        chanp = sb("chanp", [P, CC, CPAR])
        rowp = sb("rowp", [P, RPAR])
        base = sb("base", [P, TILES, D])
        kcon = sb("kcon", [P, KCON])
        col96 = sb("col96", [BN, 3])
        w96 = sb("w96", [BN, W96])
        xpw = sb("xpw", [P, CC, XROWS])
        dtw = sb("dtw", [P, CH])
        outw = sb("outw", [P, CC, BN])
        sel = sb("sel", [3 * 2 * NS, SEL, P], BF16)
        ident = sb("ident", [P, P])
        tri = sb("tri", [P, P], BF16)
        ones = sb("ones", [P, P], BF16)
        iota = sb("iota", [P, KSLOTS], F16)
        w1s = [sb(f"w1_{i}", [DK, 2, 2 * H]) for i in range(2)]
        w2s = [sb(f"w2_{i}", [P, HC, D]) for i in range(2)]

        stats = sb("stats", [P, TILES, 2, 6])
        mv = sb("mv", [P, TILES, 2, 2])
        veps = sb("veps", [P, TILES, 2])
        halfpow = sb("halfpow", [P, TILES, 2])
        rst = sb("rst", [P, TILES, 2])
        h0 = sb("h0", [P, TILES, D])
        zn = sb("zn", [P, TILES, D])
        znT = sb("znT", [DK, 2 * NP_])
        hF = sb("hF", [BN, N])
        hR = sb("hR", [BN, N])
        halfw = sb("halfw", [P, CC, TAPS + 1])
        xs = sb("xs", [P, CC, N])
        xc = sb("xc", [P, CC, N])
        th = sb("th", [P, CC, N])
        pix = xT[:].rearrange("p k n -> p (k n)")
        zs = pix[:, 0:CC * N].rearrange("p (c n) -> p c n", c=CC)
        sz = sb("sz", [P, CC, N])
        mix = sb("mix", [P, 4, CC, N])
        u, uD, dt, du = (mix[:, i] for i in range(4))
        ab, ex, lg = xs, th, xc
        xdt = sb("xdt", [P, N])
        bcr = sb("bcr", [4 * NS, N])
        bparts = sb("bparts", [6 * NS, N], BF16)
        cparts = sb("cparts", [6 * NS, N], BF16)
        negA = sb("negA", [P, CC * NS])
        dA = [sb(f"dA{i}", [P, N]) for i in range(2)]
        Bs = [sb(f"Bs{i}", [P, N]) for i in range(2)]
        dBu = [sb(f"dBu{i}", [P, N])[:] for i in range(2)] + [pix[:, (CC + i) * N:(CC + i + 1) * N] for i in range(2)]
        hs = [sb(f"hs{i}", [P, N]) for i in range(2)]
        hc = [sb(f"hc{i}", [P, N]) for i in range(2)]
        g = sb("g", [P, 2, NP_])
        ysb = xc[:, 0, :]
        gR = xs[:].rearrange("p c n -> p (c n)")[:, 0:2 * NP_].rearrange("p (c n) -> p c n", c=2)
        yn = zn
        yT = sb("yT", [BN, NP_])
        bsum = sb("bsum", [BN, 1])
        xfT = znT
        xhi = sb("xhi", [P, TILES, D + EXT], F16)
        xlo = sb("xlo", [P, TILES, D + EXT], F16)
        xr = sb("xr", [P, TILES, D])
        lgt = sb("lgt", [P, TILES, E])
        lg2 = sb("lg2", [P, TILES, E])
        key = sb("key", [P, TILES, E])
        oh = sb("oh", [P, TOP, TILES, E])
        ohm = sb("ohm", [P, TOP, TILES, E])
        ohb = sb("ohb", [P, TILES, TOP, E], BF16)
        mx = sb("mx", [P, TOP, TILES])
        km = sb("km", [P, TILES])
        dm = sb("dm", [P, TILES])
        em = sb("em", [P, TILES])
        wts = sb("wts", [P, TOP, TILES])
        psel = sb("psel", [P, TILES, TOP, E])
        pos = sb("pos", [P, TILES, TOP])
        eb = sb("eb", [P, TILES, TOP])
        over = sb("over", [P, TILES, TOP])
        slot = sb("slot", [P, TILES, TOP])
        disp = pix.bitcast(BF16)[:, 0:TILES * SLOTS].rearrange("p (t s) -> p t s", t=TILES)
        flat = mix[:].rearrange("p a c n -> p (a c n)")
        xgT = flat[0:DK + EXT, 0:2 * SLOTS].rearrange("p (k s) -> p k s", k=2)
        thg = [dA[i][:, 0:4 * CAP].rearrange("p (q s) -> p q s", q=2) for i in range(2)]
        gt = [dBu[i][:, 0:4 * CAP].rearrange("p (q s) -> p q s", q=2) for i in range(2)]
        act_t = [sb(f"act{i}", [P, HC, 2 * CAP]) for i in range(2)]
        ye = [sb(f"ye{i}", [CAP, TOP, D]) for i in range(2)]
        idle = sb("idle", [P, 512], BF16)
        zrow = sb("zrow", [CAP, TOP * D])
        info = sb("info", [CAP, TOP * E * EXT])
        dump = sb("dump", [CAP, TOP * E])
        empty = sb("empty", [CAP, TOP * E])
        dest = sb("dest", [CAP, TOP * E])
        destu = sb("destu", [CAP, TOP * E], U32)
        ps = ctx.enter_context(nc.psum_tensor("ps", [P, 8, 512], F32))

        def halves(b):
            return ps[:, b:b + 2, 0:HALF]

        def split(ap):
            return ap.rearrange("p (s c) -> p s c", s=2)

        def img(ap, lo, hi):
            return ap.rearrange("p (i t) -> p i t", t=SEQ)[:, :, lo:hi]

        s_px = [sem(f"pixels_loaded{k}") for k in range(PK)]
        s_par = sem("token_params_loaded")
        s_id = sem("identity_loaded")
        s_w96 = sem("w96_loaded")
        s_chp = sem("channel_params_loaded")
        s_xpw = sem("xproj_loaded")
        s_dtw = sem("dtw_loaded")
        s_sel = sem("selectors_loaded")
        s_late = sem("late_weights_loaded")
        s_route = sem("routing_constants_loaded")
        s_y = sem("embedding_in_psum")
        s_v = sem("vector_chain")
        s_a = sem("scalar_chain")
        s_idle = sem("idle_operand_ready")
        s_var = sem("variance_ready")
        s_ve = sem("variance_plus_eps")
        s_hp5 = sem("exponent_ready")
        s_rs = sem("rstd_ready")
        s_zn = sem("normalised_tiles")
        s_zt = sem("transposed_in_psum")
        s_ztc = sem("transposed_copied")
        s_h = sem("down_in_psum")
        s_hf = sem("hF_ready")
        s_hr = sem("hR_ready")
        s_xs = sem("xs_in_psum")
        s_xsc = sem("xs_copied")
        s_xc0 = sem("conv_first_tap")
        s_hw = sem("halved_weights")
        s_xc = sem("conv_done")
        s_th = sem("tanh_done")
        s_u = sem("u_ready")
        s_zp = sem("z_in_psum")
        s_zth = sem("z_tanh_done")
        s_sz = sem("silu_z_ready")
        s_xp = sem("xproj_in_psum")
        s_xdt = sem("dt_rows_copied")
        s_hi = sem("high_parts")
        s_r1 = sem("first_rests")
        s_mid = sem("middle_parts")
        s_lo = sem("low_parts")
        s_dtp = sem("dt_in_psum")
        s_ab = sem("abs_done")
        s_lg = sem("log_done")
        s_relu = sem("relu_done")
        s_dt = sem("dt_ready")
        s_midc = sem("middle_part_of_C")
        s_loc = sem("low_part_of_C")
        s_du = sem("du_ready")
        s_aexp = sem("A_exponential")
        s_nA = sem("negA_ready")
        s_zero = sem("borders_zeroed")
        s_uD = sem("uD_ready")
        s_zs = sem("z_copied")
        s_ysb = sem("y_copied")
        s_B = [sem(f"B_in_psum{i}") for i in range(2)]
        s_C = [sem(f"C_in_psum{i}") for i in range(2)]
        s_Bs = [sem(f"B_copied{i}") for i in range(2)]
        s_dA = [sem(f"dA_ready{i}") for i in range(2)]
        s_dbu = [sem(f"dBu_ready{i}") for i in range(4)]
        s_scan = [sem(f"scan_done{i}") for i in range(2)]
        s_hc = [sem(f"hC_ready{i}") for i in range(2)]
        s_acc = [sem(f"hC_summed{i}") for i in range(2)]
        s_gate = sem("y_gated")
        s_gr = sem("y_reversed")
        s_o = sem("mixer_out_in_psum")
        s_yc = sem("backward_centred")
        s_yb = sem("backward_scaled")
        s_yn = sem("mixer_normed")
        s_yt = sem("y_transposed")
        s_ytc = sem("yT_ready")
        s_up = sem("up_in_psum")
        s_x2 = sem("ffn_input_ready")
        s_xt = sem("ffn_input_transposed")
        s_xtc = sem("ffn_input_T_ready")
        s_lgp = sem("logits_in_psum")
        s_m = sem("score_gap_ready")
        s_em = sem("score_exp_ready")
        s_oh = sem("onehot_ready")
        s_pos = sem("positions_in_psum")
        s_disp = sem("dispatch_tiles")
        s_xh = sem("xhi_ready")
        s_xrr = sem("xrest_ready")
        s_xl = sem("xlo_ready")
        s_g = sem("gathered_in_psum")
        s_gc = [sem(f"gathered_copied{k}") for k in range(2)]
        s_w1 = [sem(f"up_weights{i}") for i in range(2)]
        s_w2 = [sem(f"down_weights{i}") for i in range(2)]
        s_hp = [sem(f"hidden_in_psum{i}") for i in range(2)]
        s_ht = [sem(f"gate_tanh{i}") for i in range(2)]
        s_hg = [sem(f"gate_product{i}") for i in range(2)]
        s_act = [sem(f"hidden_ready{i}") for i in range(2)]
        s_ye = [sem(f"expert_out_in_psum{i}") for i in range(2)]
        s_yec = [sem(f"expert_out_copied{i}") for i in range(2)]
        s_yst = [sem(f"expert_out_stored{i}") for i in range(2)]
        s_yfree = [sem(f"expert_out_slot_free{i}") for i in range(2)]
        s_zr = sem("zero_rows_ready")
        s_dump = sem("dump_rows_loaded")
        s_fill = sem("result_holds_residual")
        s_ext = sem("slot_extras_ready")
        s_info = sem("slot_info_in_psum")
        s_ic = sem("slot_info_copied")
        s_dest = sem("destination_steps")


        block = ctx.enter_context(nc.Block())

        @block.sync
        def _(sp):
            for k in range(PK):
                sp.dma_start(xT[:, k, :], a["xT"][:, k, :]).then_inc(s_px[k], 16)
            sp.dma_start(base[:], a["base"]).then_inc(s_par, 16)
            sp.dma_start(ident[:], a["ident"]).then_inc(s_id, 16)
            sp.dma_start(xpw[:], a["xpw"]).then_inc(s_xpw, 16)
            sp.dma_start(sel[:], a["sel"]).then_inc(s_sel, 16)
            sp.dma_start(outw[:], a["outw"]).then_inc(s_late, 16)
            sp.dma_start(tri[:], a["tri"]).then_inc(s_route, 16)
            sp.dma_start(ones[:], a["ones"]).then_inc(s_route, 16)
            sp.dma_start(iota[:], a["iota"]).then_inc(s_route, 16)
            for i in range(2):
                sp.dma_start(w1s[i][:], a["W1"][i]).then_inc(s_w1[i], 16)
                sp.dma_start(w2s[i][:], a["W2"][i]).then_inc(s_w2[i], 16)
            sp.dma_start(dump[:], a["dump"]).then_inc(s_dump, 16)
            sp.wait_ge(s_zr, 1)
            sp.dma_start(a["out"][N:, :].rearrange("(k c) d -> c k d", k=TOP), zrow[:].rearrange("c (k d) -> c k d", k=TOP)).then_inc(s_fill, 16)
            sp.wait_ge(s_var, 4)
            for t in range(TILES):
                rows = min(P, N - t * P)
                sp.dma_start(a["out"][t * P:t * P + rows, :], h0[0:rows, t, :]).then_inc(s_fill, 16)

            def load_up(e, slot, done):
                sp.wait_ge(s_hp[1], done)
                sp.dma_start(w1s[slot][:], a["W1"][bass.ds(e, 1)].rearrange("o p k h -> (o p) k h")).then_inc(s_w1[slot], 16)

            def load_down(e, slot, uses):
                sp.wait_ge(s_yec[slot], uses + 1)
                sp.dma_start(w2s[slot][:], a["W2"][bass.ds(e, 1)].rearrange("o p k h -> (o p) k h")).then_inc(s_w2[slot], 16)

            load_up(2, 0, 1)
            with sp.Fori(0, E // 2 - 2) as j:
                for i in range(2):
                    load_up(j * 2 + (i + 3), 1 - i, j * 2 + (i + 2))
                    load_down(j * 2 + (i + 2), i, j + 1)
            load_up(E - 1, 1, E - 2)
            for i in range(2):
                load_down(E - 2 + i, i, E // 2 - 1)

        @block.gpsimd
        def _(pool):
            nc.gpsimd.memset(dA[0][:], 0.0).then_inc(s_zero, 1)
            nc.gpsimd.memset(dA[1][:], 0.0).then_inc(s_zero, 1)
            nc.gpsimd.memset(g[:, :, N:], 0.0).then_inc(s_zero, 1)
            nc.gpsimd.memset(zrow[:], 0.0).then_inc(s_zr, 1)
            nc.gpsimd.memset(xlo[:, :, D:D + 1], 0.0).then_inc(s_ext, 1)

            def rstd(n, cols):
                pool.wait_ge(s_var, n)
                nc.gpsimd.tensor_scalar(veps[:, :, 0:cols], mv[:, :, 0:cols, 1], EPS, None, ALU.add).then_inc(s_ve, 1)
                pool.wait_ge(s_ve, n)
                nc.gpsimd.tensor_tensor(rst[:, :, 0:cols], veps[:, :, 0:cols], halfpow[:, :, 0:cols], ALU.pow).then_inc(s_rs, 1)

            nc.gpsimd.memset(halfpow[:], -0.5).then_inc(s_hp5, 1)
            pool.wait_ge(s_hp5, 1)
            rstd(1, 1)
            rstd(2, 1)
            for c in range(CC):
                pool.wait_ge(s_u, c + 1)
                nc.gpsimd.tensor_scalar(uD[:, c, :], u[:, c, :], chanp[:, c, C_D:C_D + 1], None, ALU.mult).then_inc(s_uD, 1)
            pool.wait_ge(s_uD, CC)
            pool.wait_ge(s_midc, 1)
            nc.gpsimd.tensor_tensor(cparts[4 * NS:6 * NS, :], bcr[XC:XDT, :], cparts[2 * NS:4 * NS, :], ALU.subtract).then_inc(s_loc, 1)
            pool.wait_ge(s_loc, 1)

            def pool_quad(c, q):
                for i in range(4):
                    pool.wait_ge(s_Bs[i % 2], q * 2 + (c * 8 + i // 2 + 1))
                    nc.gpsimd.tensor_tensor(dBu[i], du[:, c, :], Bs[i % 2][:], ALU.mult).then_inc(s_dbu[i], 1)

            for i in range(4):
                pool.sem_inc(s_dbu[i], 1)
            for c in range(CC):
                pool.wait_ge(s_du, c + 1)
                if c == 0:
                    with pool.Fori(0, QUADS) as q:
                        pool_quad(c, q)
                    pool.wait_ge(s_lg, CC)
                    nc.gpsimd.memset(gR[:, :, N:], 0.0).then_inc(s_zero, 1)
                else:
                    with pool.Fori(0, QUADS - 1) as q:
                        pool_quad(c, q)
                    pool.wait_ge(s_sz, CC)
                    pool.wait_ge(s_ysb, c)
                    if c == 1:
                        nc.gpsimd.tensor_tensor(g[:, 0, 0:N], ysb, sz[:, 0, :], ALU.mult).then_inc(s_gate, 1)
                    else:
                        nc.gpsimd.tensor_tensor(g[:, 1, 0:N], ysb, sz[:, 1, :], ALU.mult).then_inc(s_gate, 1)
                        nc.gpsimd.tensor_tensor(gR[:, 0, 0:N][:, ::-1], ysb, sz[:, 1, :], ALU.mult).then_inc(s_gate, 1)
                    pool_quad(c, QUADS - 1)
            rstd(3, 2)
            rstd(4, 1)
            for i in range(2):
                pool.sem_inc(s_yfree[i], 1)
            pool.wait_ge(s_ic, 1)
            number = info[:].rearrange("c (b x) -> c b x", x=EXT)[:, :, 0]
            nc.gpsimd.tensor_scalar(empty[:], number, 0.0, None, ALU.is_equal).then_inc(s_dest, 1)
            nc.gpsimd.tensor_scalar(dest[:], number, SPLIT, -1.0, ALU.mult, ALU.add).then_inc(s_dest, 1)
            pool.wait_ge(s_dump, 16)
            pool.wait_ge(s_dest, 2)
            nc.gpsimd.tensor_tensor(empty[:], empty[:], dump[:], ALU.mult).then_inc(s_dest, 1)
            pool.wait_ge(s_dest, 3)
            nc.gpsimd.tensor_tensor(dest[:], dest[:], empty[:], ALU.add).then_inc(s_dest, 1)
            pool.wait_ge(s_dest, 4)
            nc.gpsimd.tensor_copy(destu[:], dest[:]).then_inc(s_dest, 1)
            pool.wait_ge(s_dest, 5)
            pool.wait_ge(s_fill, 16 * (TILES + 1))
            for e in range(E):
                if e > 0:
                    pool.wait_ge(s_yst[(e - 1) % 2], 16 * TOP * ((e - 1) // 2 + 1))
                    pool.sem_inc(s_yfree[(e - 1) % 2], 1)
                pool.wait_ge(s_yec[e % 2], e // 2 + 2)
                for k in range(TOP):
                    pool.indirect_dma_start(
                        out=a["out"], out_offset=bass.IndirectOffsetOnAxis(ap=destu[:, k * E + e:k * E + e + 1], axis=0),
                        in_=ye[e % 2][:, k, :], in_offset=None, compute_op=ALU.add
                    ).then_inc(s_yst[e % 2], 16)
            pool.wait_ge(s_yst[(E - 1) % 2], 16 * TOP * (E // 2))

        @block.scalar
        def _(act):
            chain = [0]

            def link(ins):
                chain[0] += 1
                ins.then_inc(s_a, 1)
                act.wait_ge(s_a, chain[0])

            for k in range(PK):
                act.dma_start(tokW[:, k, :], a["tokW"][:, k, :]).then_inc(s_px[k], 16)
            act.dma_start(rowp[:], a["rowp"].broadcast_to([P, RPAR])).then_inc(s_par, 16)
            act.dma_start(kcon[:], a["kcon"]).then_inc(s_par, 16)
            act.dma_start(w96[:], a["w96"]).then_inc(s_w96, 16)
            act.dma_start(col96[:], a["col96"]).then_inc(s_w96, 16)
            act.dma_start(chanp[:], a["chanp"]).then_inc(s_chp, 16)
            act.dma_start(dtw[XDT:XROWS, :], a["dtw"]).then_inc(s_dtw, 16)
            act.preload_act_table_set("exp_and_others")
            act.wait_ge(s_zt, 3)
            nc.scalar.activation(znT[:, 512:1024], ps[0:DK, 6, :], ACT.Copy).then_inc(s_ztc, 1)
            nc.scalar.activation(znT[:, 1024:1280], ps[0:DK, 7, 0:256], ACT.Copy).then_inc(s_ztc, 1)
            act.wait_ge(s_hf, 1)
            nc.scalar.activation(hR[:], hF[:, ::-1], ACT.Copy).then_inc(s_hr, 1)
            act.wait_ge(s_hw, 1)
            for c in range(CC):
                act.wait_ge(s_xs, c + 1)
                link(nc.scalar.activation(split(xs[:, c, :]), halves(2 * c + 2), ACT.Copy))
                nc.scalar.activation(xc[:, c, :], xs[:, c, :], ACT.Identity, bias=halfw[:, c, TAPS:TAPS + 1],
                                     scale=halfw[:, c, TAPS - 1:TAPS]).then_inc(s_xc0, 1)
            for c in range(CC):
                act.wait_ge(s_xc, c + 1)
                nc.scalar.activation(th[:, c, :], xc[:, c, :], ACT.Tanh).then_inc(s_th, 1)
                act.wait_ge(s_zp, c + 1)
                nc.scalar.activation(split(sz[:, c, :]), halves(2 * c), ACT.Tanh, scale=0.5)
                nc.scalar.activation(split(zs[:, c, :]), halves(2 * c), ACT.Copy).then_inc(s_zth, 1)
            act.preload_act_table_set("natural_log_exp_and_others")
            nc.scalar.activation(negA[:].rearrange("p (c n) -> p c n", c=CC), chanp[:, :, C_A:C_A + NS], ACT.Exp).then_inc(s_aexp, 1)
            act.wait_ge(s_xp, 1)
            nc.scalar.activation(split(xdt[XDT:XROWS, :]), ps[XDT:XROWS, 6:8, 0:HALF], ACT.Copy).then_inc(s_xdt, 1)
            nc.scalar.activation(split(bparts[2 * NS:4 * NS, :]), ps[XB:XC, 6:8, 0:HALF], ACT.Copy).then_inc(s_hi, 1)
            nc.scalar.activation(split(cparts[0:2 * NS, :]), ps[XC:XDT, 6:8, 0:HALF], ACT.Copy).then_inc(s_hi, 1)
            def log1p_exp(c):
                act.wait_ge(s_ab, c + 1)
                link(nc.scalar.activation(ex[:, c, :], ab[:, c, :], ACT.Exp, scale=-1.0))
                nc.scalar.activation(lg[:, c, :], ex[:, c, :], ACT.Ln, bias=1.0).then_inc(s_lg, 1)

            for c in range(CC):
                act.wait_ge(s_dtp, c + 1)
                nc.scalar.activation(split(ab[:, c, :]), halves(DT_BANK[c]), ACT.Abs, bias=chanp[:, c, C_DTB:C_DTB + 1]).then_inc(s_ab, 1)
                if c == 0:
                    act.wait_ge(s_r1, 1)
                    nc.scalar.activation(bparts[0:2 * NS, :], bcr[XB:XC, :], ACT.Copy).then_inc(s_mid, 1)
                    log1p_exp(0)
            for c in range(1, CC):
                log1p_exp(c)
            act.wait_ge(s_zero, 3)
            act.wait_ge(s_nA, 1)

            def copy_b(slot, uses):
                act.wait_ge(s_B[slot], uses)
                nc.scalar.activation(split(Bs[slot][:]), halves(2), ACT.Copy).then_inc(s_Bs[slot], 1)

            def act_quad(c, q, copies, mid=None):
                for pair in range(2):
                    for i in range(2):
                        act.wait_ge(s_scan[i], q * 2 + (c * 8 + pair + 1))
                        nc.scalar.activation(img(dA[i][:], 1, SEQ), img(dt[:, c, :], 1, SEQ), ACT.Exp,
                                             scale=negA[:, bass.ds(q * 4 + (c * NS + 2 * pair + i), 1)]).then_inc(s_dA[i], 1)
                        if 2 * pair + i < copies:
                            act.wait_ge(s_dbu[2 * pair + i], q + (c * QUADS + 2))
                            copy_b(i, q * 2 + (c * 8 + pair + 2))
                    if pair == 0 and mid:
                        mid()

            def copy_y(c):
                for i in range(2):
                    act.wait_ge(s_acc[i], 8 * (c + 1) + 1)
                if c > 0:
                    act.wait_ge(s_gate, c)
                nc.scalar.activation(split(ysb), halves(0), ACT.Copy, scale=0.5).then_inc(s_ysb, 1)

            copy_b(0, 1)
            copy_b(1, 1)
            for c in range(CC):
                act.wait_ge(s_dt, c + 1)
                if c > 0:
                    act_quad(c, 0, 4, lambda: copy_y(c - 1))
                with act.Fori(min(c, 1), QUADS - (c == CC - 1)) as q:
                    act_quad(c, q, 4)
            act_quad(CC - 1, QUADS - 1, 2)
            act.preload_act_table_set("exp_and_others")
            act.wait_ge(s_rs, 3)
            act.wait_ge(s_yc, 1)
            for t in range(TILES):
                nc.scalar.activation(yn[:, t, BN:2 * BN], yn[:, t, BN:2 * BN], ACT.Copy, scale=rst[:, t, 1:2]).then_inc(s_yb, 1)
            act.wait_ge(s_yt, 4)
            nc.scalar.activation(yT[:, 0:512], ps[0:BN, 6, :], ACT.Identity, bias=bsum[:, 0:1]).then_inc(s_ytc, 1)
            act.wait_ge(s_yt, TILES)
            nc.scalar.activation(yT[:, 512:640], ps[0:BN, 7, 0:128], ACT.Identity, bias=bsum[:, 0:1]).then_inc(s_ytc, 1)
            act.wait_ge(s_xt, 3)
            nc.scalar.activation(xfT[:, 512:1024], ps[0:DK, 6, :], ACT.Copy).then_inc(s_xtc, 1)
            nc.scalar.activation(xfT[:, 1024:1280], ps[0:DK, 7, 0:256], ACT.Copy).then_inc(s_xtc, 1)
            nc.scalar.activation(xhi[:, :, 0:D], zn[:], ACT.Copy, scale=SPLIT).then_inc(s_xh, 1)
            act.wait_ge(s_m, 1)
            nc.scalar.activation(em[:], dm[:], ACT.Exp).then_inc(s_em, 1)
            act.wait_ge(s_xrr, 1)
            nc.scalar.activation(xlo[:, :, 0:D], xr[:], ACT.Copy).then_inc(s_xl, 1)
            for q in range(4):
                act.wait_ge(s_g, 2 * q + 1)
                cols = slice(q * SLOTS // 4, (q + 1) * SLOTS // 4)
                nc.scalar.activation(xgT[0:DK, 0, cols], ps[0:DK, 4 + 2 * (q % 2), 0:SLOTS // 4], ACT.Copy,
                                     scale=1.0 / SPLIT).then_inc(s_gc[0], 1)
            for i in range(2):
                act.sem_inc(s_yec[i], 1)
            def gate_tanh(j, i):
                for s in range(2):
                    act.wait_ge(s_hp[s], j * 2 + (i + 1))
                    act.wait_ge(s_hg[s], j * 2 + (i + 1))
                    nc.scalar.activation(thg[s][:], ps[:, 2 * s:2 * s + 2, 2 * CAP:4 * CAP], ACT.Tanh,
                                         scale=0.5).then_inc(s_ht[s], 1)

            def copy_out(j, i):
                act.wait_ge(s_ye[i], j + 2)
                act.wait_ge(s_yfree[i], j + 1)
                for k in range(TOP):
                    last = nc.scalar.activation(ye[i][:, k, :], ps[0:CAP, 4 + i, k * D:(k + 1) * D], ACT.Copy,
                                                scale=info[:, bass.ds(j * (2 * EXT) + ((k * E + i) * EXT + 1 + k), 1)])
                last.then_inc(s_yec[i], 1)

            gate_tanh(0, 0)
            act.wait_ge(s_info, 1)
            nc.scalar.activation(info[:], ps[0:CAP, 6, 0:TOP * E * EXT], ACT.Copy).then_inc(s_ic, 1)
            act.wait_ge(s_ic, 1)
            with act.Fori(0, E // 2 - 1) as j:
                gate_tanh(j, 1)
                copy_out(j, 0)
                gate_tanh(j + 1, 0)
                copy_out(j, 1)
            gate_tanh(E // 2 - 1, 1)
            copy_out(E // 2 - 1, 0)
            copy_out(E // 2 - 1, 1)

        @block.vector
        def _(dve):
            chain = [0]
            V = nc.vector
            V.memset(idle[:], 0.0).then_inc(s_idle, 1)

            def link(ins):
                chain[0] += 1
                ins.then_inc(s_v, 1)
                dve.wait_ge(s_v, chain[0])

            def step(ins):
                chain[0] += 1
                ins.then_inc(s_v, 1)
                return chain[0]

            def settle():
                dve.wait_ge(s_v, chain[0])

            def moments(cols, src, ready):
                for t in range(TILES):
                    ready(t)
                    for d in range(cols):
                        step(V.bn_stats(stats[:, t, d, :], src(t, d)))
                settle()
                for t in range(TILES):
                    for d in range(cols):
                        last = V.bn_aggr(mv[:, t, d, :], stats[:, t, d, :])
                last.then_inc(s_var, 1)

            dve.wait_ge(s_par, 48)
            done = []
            for t in range(TILES):
                dve.wait_ge(s_y, t + 1)
                done.append(step(V.scalar_tensor_tensor(h0[:, t, :], rowp[:, R_TB:R_TB + D], kcon[:, K_PATCH + t:K_PATCH + t + 1],
                                                        ps[:, t, 0:D], ALU.mult, ALU.add)))
            moments(1, lambda t, d: h0[:, t, :], lambda t: dve.wait_ge(s_v, done[t]))
            dve.wait_ge(s_var, 1)
            for t in range(TILES):
                step(V.scalar_tensor_tensor(h0[:, t, :], h0[:, t, :], mv[:, t, 0, 0:1], rowp[:, R_LW:R_LW + D], ALU.subtract, ALU.mult))
            settle()
            dve.wait_ge(s_rs, 1)
            done = [step(V.scalar_tensor_tensor(h0[:, t, :], h0[:, t, :], rst[:, t, 0:1], base[:, t, :], ALU.mult, ALU.add))
                    for t in range(TILES)]
            moments(1, lambda t, d: h0[:, t, :], lambda t: dve.wait_ge(s_v, done[t]))
            dve.wait_ge(s_var, 2)
            dve.wait_ge(s_rs, 2)
            for t in range(TILES):
                V.tensor_scalar(zn[:, t, :], h0[:, t, :], mv[:, t, 0, 0:1], rst[:, t, 0:1],
                                ALU.subtract, ALU.mult).then_inc(s_zn, 1)
            dve.wait_ge(s_zn, TILES)
            step(V.tensor_tensor(h0[:], h0[:], rowp[:, None, R_UB:R_UB + D].broadcast_to([P, TILES, D]), ALU.add))
            dve.wait_ge(s_zt, 1)
            V.tensor_copy(znT[:, 0:512], ps[0:DK, 5, :]).then_inc(s_ztc, 1)
            dve.wait_ge(s_chp, 16)
            V.tensor_scalar(halfw[:], chanp[:, :, 0:TAPS + 1], 0.5, None, ALU.mult).then_inc(s_hw, 1)
            dve.wait_ge(s_w96, 32)
            step(V.tensor_tensor(bsum[:], col96[:, 1:2], col96[:, 2:3], ALU.add))
            dve.wait_ge(s_h, 1)
            V.tensor_scalar(split(hF[:]), ps[0:BN, 0:2, 0:HALF], col96[:, 0:1], None, ALU.add).then_inc(s_hf, 1)
            dve.wait_ge(s_hw, 1)
            def silu_u(c):
                dve.wait_ge(s_th, c + 1)
                V.scalar_tensor_tensor(u[:, c, :], th[:, c, :], 1.0, xc[:, c, :], ALU.add, ALU.mult).then_inc(s_u, 1)

            done = [0] * CC
            for c, k in ((0, 1), (0, 2), (1, 1), (0, 3), (1, 2), (2, 1), (1, 3), (2, 2), (2, 3)):
                if k == 1:
                    dve.wait_ge(s_xc0, c + 1)
                else:
                    dve.wait_ge(s_v, done[c])
                o = img(xc[:, c, :], k, SEQ)
                ins = V.scalar_tensor_tensor(o, img(xs[:, c, :], 0, SEQ - k), halfw[:, c, TAPS - 1 - k:TAPS - k], o,
                                             ALU.mult, ALU.add)
                if k < TAPS - 1:
                    done[c] = step(ins)
                else:
                    ins.then_inc(s_xc, 1)
            for c in range(CC):
                silu_u(c)
            for c in range(CC):
                dve.wait_ge(s_zth, c + 1)
                V.scalar_tensor_tensor(sz[:, c, :], sz[:, c, :], 1.0, zs[:, c, :], ALU.add, ALU.mult).then_inc(s_sz, 1)
            dve.wait_ge(s_hi, 1)
            V.tensor_tensor(split(bcr[XB:XC, :]), ps[XB:XC, 6:8, 0:HALF], split(bparts[2 * NS:4 * NS, :]), ALU.subtract).then_inc(s_r1, 1)
            dve.wait_ge(s_hi, 2)
            V.tensor_tensor(split(bcr[XC:XDT, :]), ps[XC:XDT, 6:8, 0:HALF], split(cparts[0:2 * NS, :]), ALU.subtract).then_inc(s_r1, 1)
            dve.wait_ge(s_aexp, 1)
            V.tensor_scalar(negA[:], negA[:], -1.0, None, ALU.mult).then_inc(s_nA, 1)
            dve.wait_ge(s_r1, 2)
            V.tensor_copy(cparts[2 * NS:4 * NS, :], bcr[XC:XDT, :]).then_inc(s_midc, 1)

            def step_size(c):
                dve.wait_ge(s_relu, c + 1)
                dve.wait_ge(s_lg, c + 1)
                V.tensor_tensor(dt[:, c, :], dt[:, c, :], lg[:, c, :], ALU.add).then_inc(s_dt, 1)
                dve.wait_ge(s_dt, c + 1)
                V.tensor_tensor(du[:, c, :], dt[:, c, :], u[:, c, :], ALU.mult).then_inc(s_du, 1)

            for c in range(CC):
                dve.wait_ge(s_ab, c + 1)
                V.tensor_scalar(split(dt[:, c, :]), halves(DT_BANK[c]), chanp[:, c, C_DTB:C_DTB + 1], 0.0, ALU.add, ALU.max).then_inc(s_relu, 1)
                if c == 0:
                    dve.wait_ge(s_mid, 1)
                    V.tensor_tensor(bparts[4 * NS:6 * NS, :], bcr[XB:XC, :], bparts[0:2 * NS, :], ALU.subtract).then_inc(s_lo, 1)
                    step_size(0)
            for c in range(1, CC):
                step_size(c)
            dve.wait_ge(s_zero, 3)
            for i in range(2):
                dve.sem_inc(s_scan[i], 1)
                dve.sem_inc(s_hc[i], 1)

            def dve_quad(c, q):
                for pair in range(2):
                    uses = q * 2 + (c * 8 + pair)
                    for i in range(2):
                        dve.wait_ge(s_dA[i], uses + 1)
                        dve.wait_ge(s_dbu[2 * pair + i], q + (c * QUADS + 2))
                        dve.wait_ge(s_hc[i], uses + 1)
                        V.tensor_tensor_scan(hs[i][:], dA[i][:], dBu[2 * pair + i], 0.0, ALU.mult, ALU.add).then_inc(s_scan[i], 1)
                    for i in range(2):
                        dve.wait_ge(s_C[i], uses + 1)
                        dve.wait_ge(s_acc[i], uses + 1)
                        dve.wait_ge(s_scan[i], uses + 2)
                        V.tensor_tensor(split(hc[i][:]), split(hs[i][:]), halves(4 + 2 * i), ALU.mult).then_inc(s_hc[i], 1)

            for c in range(CC):
                with dve.Fori(0, QUADS) as q:
                    dve_quad(c, q)
            dve.wait_ge(s_sz, CC)
            dve.wait_ge(s_zero, 4)
            for i in range(2):
                dve.wait_ge(s_acc[i], 8 * CC + 1)
            V.scalar_tensor_tensor(split(gR[:, 1, 0:N][:, ::-1]), halves(0), 0.5, split(sz[:, 2, :]),
                                   ALU.mult, ALU.mult).then_inc(s_gr, 1)
            o_of = lambda t, d: ps[:, t // 2 * 2 + d, (t % 2) * BN:(t % 2 + 1) * BN]
            moments(2, o_of, lambda t: dve.wait_ge(s_o, min(t // 2 * 2 + 2, TILES)))
            dve.wait_ge(s_var, 3)
            for d in (1, 0):
                for t in range(TILES):
                    ins = V.scalar_tensor_tensor(yn[:, t, d * BN:(d + 1) * BN], o_of(t, d), mv[:, t, d, 0:1],
                                                 rowp[:, R_G + d * BN:R_G + (d + 1) * BN], ALU.subtract, ALU.mult)
                    if d == 0 or t < TILES - 1:
                        step(ins)
                    else:
                        ins.then_inc(s_yc, 1)
            settle()
            dve.wait_ge(s_rs, 3)
            for t in range(TILES):
                dve.wait_ge(s_yb, t + 1)
                V.scalar_tensor_tensor(yn[:, t, 0:BN], yn[:, t, 0:BN], rst[:, t, 0:1], yn[:, t, BN:2 * BN],
                                       ALU.mult, ALU.add).then_inc(s_yn, 1)
            done = []
            for t in range(TILES):
                dve.wait_ge(s_up, min(t // 2 * 2 + 2, TILES))
                done.append(step(V.tensor_tensor(h0[:, t, :], h0[:, t, :], ps[:, t // 2, (t % 2) * D:(t % 2 + 1) * D], ALU.add)))
            moments(1, lambda t, d: h0[:, t, :], lambda t: dve.wait_ge(s_v, done[t]))
            dve.wait_ge(s_var, 4)
            dve.wait_ge(s_rs, 4)
            for t in range(TILES):
                V.tensor_scalar(zn[:, t, :], h0[:, t, :], mv[:, t, 0, 0:1], rst[:, t, 0:1],
                                ALU.subtract, ALU.mult).then_inc(s_x2, 1)
            dve.wait_ge(s_xt, 1)
            V.tensor_copy(xfT[:, 0:512], ps[0:DK, 5, :]).then_inc(s_xtc, 1)
            dve.wait_ge(s_xh, 1)
            V.scalar_tensor_tensor(xr[:], zn[:], SPLIT, xhi[:, :, 0:D], ALU.mult, ALU.subtract).then_inc(s_xrr, 1)
            rev = kcon[:, None, K_REV:K_REV + E].broadcast_to([P, TILES, E])
            real = kcon[:, K_REAL:K_REAL + TILES].rearrange("p (t o) -> p t o", o=1).broadcast_to([P, TILES, E])
            dve.wait_ge(s_lgp, 1)
            link(V.tensor_copy(lgt[:], ps[:, 4, 0:TILES * E].rearrange("p (t e) -> p t e", e=E)))
            for k in range(TOP):
                src = (lgt, lg2)[k]
                link(V.tensor_reduce(mx[:, k, :], src[:], AX.X, ALU.max))
                link(V.tensor_tensor(key[:], src[:], mx[:, k, :].rearrange("p (t o) -> p t o", o=1).broadcast_to([P, TILES, E]), ALU.is_equal))
                link(V.tensor_tensor(key[:], key[:], rev, ALU.mult))
                link(V.tensor_reduce(km[:], key[:], AX.X, ALU.max))
                link(V.tensor_tensor(oh[:, k], rev, km[:].rearrange("p (t o) -> p t o", o=1).broadcast_to([P, TILES, E]), ALU.is_equal))
                if k == 0:
                    link(V.scalar_tensor_tensor(lg2[:], oh[:, 0], -3.0e38, lgt[:], ALU.mult, ALU.add))
            V.tensor_tensor(dm[:], mx[:, 1, :], mx[:, 0, :], ALU.subtract).then_inc(s_m, 1)
            for k in range(TOP):
                step(V.tensor_tensor(ohm[:, k], oh[:, k], real, ALU.mult))
            settle()
            V.tensor_copy(ohb[:].rearrange("p t k e -> p k t e"), ohm[:]).then_inc(s_oh, 1)
            dve.wait_ge(s_em, 1)
            link(V.tensor_scalar(wts[:, 1, :], em[:], 1.0, None, ALU.add))
            link(V.reciprocal(wts[:, 0, :], wts[:, 1, :]))
            link(V.tensor_tensor(wts[:, 1, :], em[:], wts[:, 0, :], ALU.mult))
            wtk = wts[:].rearrange("p k t -> p t k")
            V.tensor_copy(xhi[:, :, D], kcon[:, K_TOK:K_TOK + TILES]).then_inc(s_ext, 1)
            V.tensor_scalar(xhi[:, :, D + 1:D + EXT], wtk, SPLIT, None, ALU.mult).then_inc(s_ext, 1)
            dve.wait_ge(s_ext, 3)
            V.scalar_tensor_tensor(xlo[:, :, D + 1:D + EXT], wtk, SPLIT, xhi[:, :, D + 1:D + EXT], ALU.mult, ALU.subtract).then_inc(s_ext, 1)
            dve.wait_ge(s_pos, 1)
            link(V.tensor_tensor(psel[:], ps[:, 5, 0:TILES * TOP * E].rearrange("p (t k e) -> p t k e", k=TOP, e=E), ohb[:], ALU.mult))
            link(V.tensor_reduce(pos[:], psel[:], AX.X, ALU.add))
            for k in range(TOP):
                link(V.tensor_tensor(psel[:, :, k, :], ohm[:, k], kcon[:, None, K_BASE:K_BASE + E].broadcast_to([P, TILES, E]), ALU.mult))
            link(V.tensor_reduce(eb[:], psel[:], AX.X, ALU.add))
            link(V.scalar_tensor_tensor(slot[:], pos[:], -1.0, eb[:], ALU.add, ALU.add))
            link(V.tensor_scalar(over[:], pos[:], float(CAP), DROP, ALU.is_gt, ALU.mult))
            link(V.tensor_tensor(slot[:], slot[:], over[:], ALU.add))
            dve.wait_ge(s_route, 48)
            for k in range(TOP):
                for t in range(TILES):
                    V.tensor_scalar(disp[:, t, k * KSLOTS:(k + 1) * KSLOTS], iota[:], slot[:, t, k:k + 1], None,
                                    ALU.is_equal).then_inc(s_disp, 1)
            for q in range(4):
                dve.wait_ge(s_g, 2 * q + 2)
                cols = slice(q * SLOTS // 4, (q + 1) * SLOTS // 4)
                V.tensor_scalar(xgT[:, 1, cols], ps[0:DK + EXT, 5 + 2 * (q % 2), 0:SLOTS // 4], 1.0 / SPLIT, None,
                                ALU.mult).then_inc(s_gc[1], 1)
            for i in range(2):
                dve.sem_inc(s_hg[i], 1)
                dve.sem_inc(s_act[i], 1)
            with dve.Fori(0, E // 2) as j:
                for i in range(2):
                    for s in range(2):
                        dve.wait_ge(s_ht[s], j * 2 + i + 1)
                        V.scalar_tensor_tensor(gt[s][:], thg[s][:], 1.0, ps[:, 2 * s:2 * s + 2, 2 * CAP:4 * CAP],
                                               ALU.add, ALU.mult).then_inc(s_hg[s], 1)
                        dve.wait_ge(s_hg[s], j * 2 + i + 2)
                        dve.wait_ge(s_ye[i], j + 1)
                        V.scalar_tensor_tensor(act_t[i][:, 2 * s:2 * s + 2, :], gt[s][:], 0.5,
                                               ps[:, 2 * s:2 * s + 2, 0:2 * CAP], ALU.mult, ALU.mult).then_inc(s_act[s], 1)

        @block.tensor
        def _(pe):
            mm = nc.tensor.matmul

            def keep_warm(count, bank):
                with pe.Fori(0, -(-count // 4)) as _:
                    for _ in range(min(count, 4)):
                        mm(ps[:, bank, :], idle[:, 0:P], idle[:], start=True, stop=True)

            pe.wait_ge(s_idle, 1)
            keep_warm(WARM[0], 7)
            for k in range(PK):
                pe.wait_ge(s_px[k], 32)
                for t in range(TILES):
                    last = mm(ps[:, t, 0:D], xT[:, k, t * P:(t + 1) * P], tokW[:, k, :], start=k == 0, stop=k == PK - 1)
                    if k == PK - 1:
                        last.then_inc(s_y, 1)

            def transpose_rows(ready, done):
                for q in range(2 * TILES):
                    k, t = divmod(q, TILES)
                    pe.wait_ge(ready, t + 1 if k == 0 else TILES)
                    last = nc.tensor.transpose(ps[0:DK, 5 + q // 4, (q % 4) * P:(q % 4 + 1) * P],
                                               zn[:, t, k * DK:(k + 1) * DK], ident[:])
                    if q % 4 == 3 or q == 2 * TILES - 1:
                        last.then_inc(done, 1)

            pe.wait_ge(s_id, 16)
            keep_warm(WARM[1], 7)
            transpose_rows(s_zn, s_zt)
            keep_warm(WARM[2], 4)
            pe.wait_ge(s_w96, 32)
            pe.wait_ge(s_ztc, 3)
            for h in range(2):
                for k in range(2):
                    last = mm(ps[0:BN, h, 0:HALF], w96[:, W_DOWN + k * BN:W_DOWN + (k + 1) * BN],
                              znT[:, k * NP_ + h * HALF:k * NP_ + (h + 1) * HALF], start=k == 0, stop=k == 1)
            last.then_inc(s_h, 1)
            parts = [[(0, P, hF)], [(0, 64, hF), (64, P, hR)], [(0, P, hR)]]

            def in_proj(col, bank, c, done):
                for lo, hi, src in parts[c]:
                    for h in range(2):
                        last = mm(ps[lo:hi, bank + h, 0:HALF], w96[:, col + c * P + lo:col + c * P + hi],
                                  src[:, h * HALF:(h + 1) * HALF], start=True, stop=True)
                last.then_inc(done, 1)

            keep_warm(WARM[3], 4)
            pe.wait_ge(s_hf, 1)
            in_proj(W_XS, 2, 0, s_xs)
            pe.wait_ge(s_hr, 1)
            in_proj(W_XS, 4, 1, s_xs)
            in_proj(W_XS, 6, 2, s_xs)
            for c in range(CC):
                if c > 0:
                    pe.wait_ge(s_xc0, c)
                in_proj(W_Z, 2 * c, c, s_zp)
            pe.wait_ge(s_xpw, 16)
            pe.wait_ge(s_xc0, 3)
            keep_warm(WARM[4], 6)
            for c in range(CC):
                pe.wait_ge(s_u, c + 1)
                for h in range(2):
                    last = mm(ps[0:XROWS, 6 + h, 0:HALF], xpw[:, c, :], u[:, c, h * HALF:(h + 1) * HALF],
                              start=c == 0, stop=c == CC - 1)
            last.then_inc(s_xp, 1)
            pe.wait_ge(s_zth, 2)
            keep_warm(WARM[5], 2)
            pe.wait_ge(s_dtw, 16)
            pe.wait_ge(s_xdt, 1)
            for c in range(CC):
                pe.wait_ge(s_zth, max(DT_BANK[c] // 2, c - 1) + 1)
                for h in range(2):
                    last = mm(ps[:, DT_BANK[c] + h, 0:HALF], dtw[XDT:XROWS, c * P:(c + 1) * P],
                              xdt[XDT:XROWS, h * HALF:(h + 1) * HALF], start=True, stop=True)
                last.then_inc(s_dtp, 1)

            def bcast(bank, parts, idx, done):
                for h in range(2):
                    last = mm(ps[:, bank + h, 0:HALF], sel[:, idx, :].rearrange("p o m -> p (o m)"),
                              parts[:, h * HALF:(h + 1) * HALF], start=True, stop=True)
                last.then_inc(done, 1)

            pe.wait_ge(s_sel, 16)
            pe.wait_ge(s_lo, 1)
            pe.wait_ge(s_relu, 1)
            bcast(2, bparts, slice(0, 1), s_B[0])
            pe.wait_ge(s_relu, CC)
            pe.wait_ge(s_loc, 1)
            for k in range(1, 4):
                if k == 3:
                    keep_warm(WARM[13], 0)
                pe.wait_ge(s_Bs[(k - 1) % 2], (k - 1) // 2 + 1)
                bcast(2, bparts, slice(k, k + 1), s_B[k % 2])
                if k < 3:
                    bcast(2 + 2 * k, cparts, slice(k - 1, k), s_C[k - 1])
            pe.wait_ge(s_uD, CC)
            for i in range(2):
                pe.sem_inc(s_acc[i], 1)

            def pe_quad(c, q, ahead=4):
                for i in range(4):
                    if ahead:
                        pe.wait_ge(s_Bs[(i + 1) % 2], q * 2 + (c * 8 + (i + 3) // 2 + 1))
                        bcast(2, bparts, bass.ds(q * 4 + (c * NS + i + 4), 1), s_B[i % 2])
                    pe.wait_ge(s_hc[i % 2], q * 2 + (c * 8 + i // 2 + 2))
                    for h in range(2):
                        last = mm(ps[:, h, 0:HALF], ident[:], hc[i % 2][:, h * HALF:(h + 1) * HALF],
                                  start=False, stop=False, skip_group_check=True)
                    last.then_inc(s_acc[i % 2], 1)
                    if i < 2 + ahead // 2:
                        bcast(4 + 2 * (i % 2), cparts, bass.ds(q * 4 + (c * NS + i + 2), 1), s_C[i % 2])

            for c in range(CC):
                if c > 0:
                    pe.wait_ge(s_ysb, c)
                for h in range(2):
                    mm(ps[:, h, 0:HALF], ident[:], uD[:, c, h * HALF:(h + 1) * HALF],
                       start=True, stop=False, skip_group_check=True)
                with pe.Fori(0, QUADS - (c == CC - 1)) as q:
                    pe_quad(c, q)
            pe_quad(CC - 1, QUADS - 1, ahead=0)
            keep_warm(WARM[12], 2)
            pe.wait_ge(s_late, 16)
            pe.wait_ge(s_gate, 3)
            pe.wait_ge(s_zero, 4)
            pe.wait_ge(s_gr, 1)
            for t in range(TILES):
                rows = slice(t * P, (t + 1) * P)
                of, ob = (ps[:, t // 2 * 2 + d, (t % 2) * BN:(t % 2 + 1) * BN] for d in range(2))
                mm(of, g[:, 0, rows], outw[:, 0, :], start=True, stop=False)
                mm(of, g[0:64, 1, rows], outw[0:64, 1, :], start=False, stop=True)
                mm(ob, gR[:, 1, rows], outw[:, 2, :], start=True, stop=False)
                mm(ob, gR[64:P, 0, rows], outw[64:P, 1, :], start=False, stop=True).then_inc(s_o, 1)
            keep_warm(WARM[6], 6)
            for t in range(TILES):
                pe.wait_ge(s_yn, t + 1)
                nc.tensor.transpose(ps[0:BN, 6 + t // 4, (t % 4) * P:(t % 4 + 1) * P], yn[:, t, 0:BN],
                                    ident[:]).then_inc(s_yt, 1)
            keep_warm(WARM[7], 5)
            pe.wait_ge(s_ytc, 2)
            for t in range(TILES):
                mm(ps[:, t // 2, (t % 2) * D:(t % 2 + 1) * D], yT[:, t * P:(t + 1) * P], w96[:, W_UP:W_UP + D],
                   start=True, stop=True).then_inc(s_up, 1)
            keep_warm(WARM[8], 5)
            transpose_rows(s_x2, s_xt)
            keep_warm(WARM[9], 3)
            pe.wait_ge(s_xtc, 3)
            for t in range(TILES):
                for k in range(2):
                    last = mm(ps[:, 4, t * E:(t + 1) * E], xfT[:, k * NP_ + t * P:k * NP_ + (t + 1) * P],
                              w96[:, W_G + k * E:W_G + (k + 1) * E], start=k == 0, stop=k == 1)
            last.then_inc(s_lgp, 1)
            keep_warm(WARM[10], 3)
            pe.wait_ge(s_route, 48)
            pe.wait_ge(s_oh, 1)
            for t in range(TILES):
                for b in range(t + 1):
                    last = mm(ps[:, 5, t * TOP * E:(t + 1) * TOP * E], tri[:] if b == t else ones[:],
                              ohb[:, b].rearrange("p k e -> p (k e)"), start=b == 0, stop=b == t)
            last.then_inc(s_pos, 1)
            keep_warm(WARM[11], 3)
            pe.wait_ge(s_xl, 1)
            pe.wait_ge(s_ext, 4)
            for q in range(4):
                for k in range(2):
                    if q >= 2:
                        pe.wait_ge(s_gc[k], q - 1)
                    n = 0
                    width = DK + k * EXT
                    for t in range(TILES):
                        pe.wait_ge(s_disp, t + 1 if q < 2 else TILES + t + 1)
                        for part in (xhi, xlo):
                            last = mm(ps[0:width, 4 + 2 * (q % 2) + k, 0:SLOTS // 4], part[:, t, k * DK:k * DK + width],
                                      disp[:, t, q * SLOTS // 4:(q + 1) * SLOTS // 4], start=n == 0, stop=n == 2 * TILES - 1)
                            n += 1
                    last.then_inc(s_g, 1)
            for k in range(2):
                pe.wait_ge(s_gc[k], 4)
            for i in range(2):
                pe.sem_inc(s_ye[i], 1)

            def up(j, i):
                pe.wait_ge(s_w1[i], j * 16 + 16)
                for s in range(2):
                    pe.wait_ge(s_act[s], j * 2 + (i + 1))
                    for q in range(2 * s, 2 * s + 2):
                        for half in range(2):
                            for k in range(2):
                                src = xgT[0:DK, k, :].rearrange("p (k e c) -> p e k c", k=TOP, e=E)[:, bass.ds(j * 2 + i, 1)]
                                col = half * H + q * P
                                last = mm(ps[:, q, half * 2 * CAP:(half + 1) * 2 * CAP].rearrange("p (k c) -> p k c", k=TOP),
                                          w1s[i][:, k, col:col + P], src.rearrange("p o k c -> p (o k) c"),
                                          start=k == 0, stop=k == 1)
                    last.then_inc(s_hp[s], 1)

            def down(j, i):
                pe.wait_ge(s_w2[i], j * 16 + 16)
                pe.wait_ge(s_yec[i], j + 1)
                for s in range(2):
                    pe.wait_ge(s_act[s], j * 2 + (i + 2))
                for k in range(TOP):
                    for q in range(HC):
                        last = mm(ps[0:CAP, 4 + i, k * D:(k + 1) * D], act_t[i][:, q, k * CAP:(k + 1) * CAP],
                                  w2s[i][:, q, :], start=q == 0, stop=q == HC - 1)
                last.then_inc(s_ye[i], 1)

            up(0, 0)
            for b in range(TOP * E):
                last = nc.tensor.transpose(ps[0:CAP, 6, b * EXT:(b + 1) * EXT], xgT[DK:DK + EXT, 1, b * CAP:(b + 1) * CAP],
                                           ident[DK:DK + EXT, DK:DK + EXT])
            last.then_inc(s_info, 1)
            with pe.Fori(0, E // 2 - 1) as j:
                up(j, 1)
                down(j, 0)
                up(j + 1, 0)
                down(j, 1)
            up(E // 2 - 1, 1)
            down(E // 2 - 1, 0)
            down(E // 2 - 1, 1)


def kernel(**inputs):
    import concourse.bacc as bacc
    import ml_dtypes
    from concourse.bass_utils import run_bass_kernel_spmd

    I = {k: np.asarray(v) for k, v in inputs.items()}
    f32 = np.float32

    def both(name):
        v = np.concatenate([I["L0_attn_f_" + name], I["L0_attn_b_" + name]], axis=0)
        return v.reshape((CC, P) + v.shape[1:]).swapaxes(0, 1)

    x = I["x"].reshape(IMAGES, 3, SIDE, PATCH, SIDE, PATCH).transpose(1, 3, 5, 0, 2, 4).reshape(PIX, IMAGES, SEQ - 1)
    xT = np.zeros((PIX, NP_), f32)
    xT[:, :N].reshape(PIX, IMAGES, SEQ)[:, :, 1:] = x
    base = np.zeros((NP_, D), f32)
    base[:N].reshape(IMAGES, SEQ, D)[:, 1:] = I["L0_tok_ln_b"]
    base[:N].reshape(IMAGES, SEQ, D)[:, 0] = I["cls_tok"].reshape(D)
    chanp = np.concatenate([both("conv_w"), both("conv_b")[..., None], both("dt_b")[..., None], both("D")[..., None],
                            both("A_log")], axis=2)
    rowp = np.concatenate([I["L0_tok_b"], I["L0_tok_ln_w"], I["L0_attn_up_b"], I["L0_attn_f_ln_g"],
                           I["L0_attn_b_ln_g"]])[None]
    col96 = np.stack([I["L0_attn_down_b"], I["L0_attn_f_ln_b"], I["L0_attn_b_ln_b"]], axis=1)

    def rows96(w):
        return w.reshape(2, DK, -1).transpose(1, 0, 2).reshape(DK, -1)

    fi, bi = I["L0_attn_f_in_W"], I["L0_attn_b_in_W"]
    w96 = np.concatenate([rows96(I["L0_attn_down_W"]), fi[:, :DI], bi[:, :DI], fi[:, DI:], bi[:, DI:],
                          I["L0_attn_up_W"], rows96(I["L0_ffn_Wg"])], axis=1)
    xpw = np.zeros((CH, XROWS), f32)
    dtw = np.zeros((2 * R, CH), f32)
    sel = np.zeros((3, 2, NS, SEL, P), ml_dtypes.bfloat16)
    for d, w in enumerate("fb"):
        xw = I[f"L0_attn_{w}_xproj_W"]
        mine = slice(d * DI, (d + 1) * DI)
        xpw[mine, XB + d * NS:XB + (d + 1) * NS] = xw[:, R:R + NS]
        xpw[mine, XC + d * NS:XC + (d + 1) * NS] = xw[:, R + NS:]
        xpw[mine, XDT + d * R:XDT + (d + 1) * R] = xw[:, :R]
        dtw[d * R:(d + 1) * R, mine] = I[f"L0_attn_{w}_dt_W"]
        for i in range(SEL):
            c, n = divmod(i, NS)
            ch = np.arange(c * P, (c + 1) * P)
            sel[:, d, n, i, (ch >= d * DI) & (ch < (d + 1) * DI)] = 1
    tok = np.arange(NP_).reshape(TILES, P).T
    kcon = np.concatenate([((tok < N) & (tok % SEQ > 0)), tok < N, np.tile(E - np.arange(E), (P, 1)),
                           np.tile(CAP * np.arange(E), (P, 1)), tok + 1], axis=1).astype(f32)
    at = np.arange(P)
    arrays = {
        "xT": xT.reshape(PK, P, NP_).transpose(1, 0, 2),
        "tokW": I["L0_tok_W"].T.reshape(PK, P, D).transpose(1, 0, 2),
        "base": base.reshape(TILES, P, D).transpose(1, 0, 2),
        "chanp": chanp, "rowp": rowp, "col96": col96, "w96": w96, "kcon": kcon,
        "xpw": xpw.reshape(CC, P, XROWS).transpose(1, 0, 2), "dtw": dtw,
        "outw": both("out_W"),
        "sel": sel.reshape(6 * NS, SEL, P),
        "ident": np.eye(P, dtype=f32),
        "tri": (at[:, None] <= at[None, :]).astype(ml_dtypes.bfloat16),
        "ones": np.ones((P, P), ml_dtypes.bfloat16),
        "iota": np.tile(np.arange(KSLOTS), (P, 1)).astype(np.float16),
        "dump": np.repeat(1 + N + np.arange(TOP)[None, :] * CAP + np.arange(CAP)[:, None], E, axis=1).astype(f32),
        "W1": I["L0_ffn_W1"].reshape(E, 2, DK, 2 * H).transpose(0, 2, 1, 3),
        "W2": I["L0_ffn_W2"].reshape(E, HC, P, D).transpose(0, 2, 1, 3),
    }
    arrays = {k: np.ascontiguousarray(v) for k, v in arrays.items()}
    nc = bacc.Bacc("TRN2", target_bir_lowering=False, num_devices=1)
    aps = {k: nc.dram_tensor(k + "_dram", v.shape, mybir.dt.from_np(v.dtype), kind="ExternalInput").ap()
           for k, v in arrays.items()}
    aps["out"] = nc.dram_tensor("out_dram", (N + TOP * CAP, D), F32, kind="ExternalOutput").ap()
    vit_mamba_moe(nc, aps)
    r = run_bass_kernel_spmd(nc, [{k + "_dram": v for k, v in arrays.items()}], core_ids=[0])
    return r.results[0]["out_dram"][:N].reshape(IMAGES, SEQ, D)
```

```python
from contextlib import ExitStack

import numpy as np

import concourse.bass as bass
from concourse import mybir

ALU = mybir.AluOpType
ACT = mybir.ActivationFunctionType
AX = mybir.AxisListType
F32 = mybir.dt.float32
BF16 = mybir.dt.bfloat16
F16 = mybir.dt.float16
U32 = mybir.dt.uint32

P = 128
IMAGES, PATCH, SIDE = 16, 16, 6
SEQ = SIDE * SIDE + 1
N = IMAGES * SEQ
HALF = N // 2
TILES = -(-N // P)
NP_ = TILES * P
D = 192
DK = D // 2
PIX = 3 * PATCH * PATCH
PK = PIX // P
BN = 96
DI = 192
CH = 2 * DI
CC = CH // P
NS, TAPS, R = 16, 4, 24
E, TOP, H = 8, 2, 512
CAP = int(1.2 * N / E)
HC = H // P
KSLOTS = E * CAP
SLOTS = TOP * KSLOTS
EPS = 1e-5
SPLIT = 1024.0
QUADS = NS // 4
SEL = CC * NS
DT_BANK = (2, 0, 4)
DROP = 4096.0

C_W, C_B, C_DTB, C_D, C_A = 0, TAPS, TAPS + 1, TAPS + 2, TAPS + 3
CPAR = C_A + NS
R_TB, R_LW, R_UB, R_G = 0, D, 2 * D, 3 * D
RPAR = R_G + 2 * BN
W_DOWN, W_XS, W_Z, W_UP, W_G = 0, 2 * BN, 2 * BN + CH, 2 * BN + 2 * CH, 2 * BN + 2 * CH + D
W96 = W_G + 2 * E
K_PATCH, K_REV, K_CMP, K_BASE, K_TOK = np.cumsum([0, TILES, E, TILES * E, TILES]).tolist()
KCON = K_TOK + TILES
EXT = 3
XB, XC, XDT = 0, 2 * NS, 4 * NS
XROWS = XDT + 2 * R


def vit_mamba_moe(nc, a):
    with ExitStack() as ctx:
        def sb(name, shape, dt=F32):
            return ctx.enter_context(nc.sbuf_tensor(name, shape, dt))

        def sem(name):
            return ctx.enter_context(nc.semaphore(name))

        xT = sb("xT", [P, PK, NP_])
        tokW = sb("tokW", [P, PK, D])
        chanp = sb("chanp", [P, CC, CPAR])
        rowp = sb("rowp", [P, RPAR])
        base = sb("base", [P, TILES, D])
        kcon = sb("kcon", [P, KCON])
        col96 = sb("col96", [BN, 3])
        w96 = sb("w96", [BN, W96])
        xpw = sb("xpw", [P, CC, XROWS])
        dtw = sb("dtw", [P, CH])
        outw = sb("outw", [P, CC, BN])
        sel = sb("sel", [3 * 2 * NS, SEL, P], BF16)
        ident = sb("ident", [P, P])
        tri = sb("tri", [P, P], BF16)
        ones = sb("ones", [P, P], BF16)
        iota = sb("iota", [P, KSLOTS], F16)
        w1s = [sb(f"w1_{i}", [DK, 2, 2 * H]) for i in range(2)]
        w2s = [sb(f"w2_{i}", [P, HC, D]) for i in range(2)]

        stats = sb("stats", [P, TILES, 2, 6])
        mv = sb("mv", [P, TILES, 2, 2])
        veps = sb("veps", [P, TILES, 2])
        halfpow = sb("halfpow", [P, TILES, 2])
        rst = sb("rst", [P, TILES, 2])
        h0 = sb("h0", [P, TILES, D])
        zn = sb("zn", [P, TILES, D])
        znT = sb("znT", [DK, 2 * NP_])
        hF = sb("hF", [BN, N])
        hR = sb("hR", [BN, N])
        halfw = sb("halfw", [P, CC, TAPS + 1])
        xs = sb("xs", [P, CC, N])
        xc = sb("xc", [P, CC, N])
        th = sb("th", [P, CC, N])
        pix = xT[:].rearrange("p k n -> p (k n)")
        zs = pix[:, 0:CC * N].rearrange("p (c n) -> p c n", c=CC)
        sz = sb("sz", [P, CC, N])
        mix = sb("mix", [P, 4, CC, N])
        u, uD, dt, du = (mix[:, i] for i in range(4))
        ab, ex, lg = xs, th, xc
        xdt = sb("xdt", [P, N])
        bcr = sb("bcr", [4 * NS, N])
        bparts = sb("bparts", [6 * NS, N], BF16)
        cparts = sb("cparts", [6 * NS, N], BF16)
        negA = sb("negA", [P, CC * NS])
        dA = [sb(f"dA{i}", [P, N]) for i in range(2)]
        Bs = [sb(f"Bs{i}", [P, N]) for i in range(2)]
        dBu = [sb(f"dBu{i}", [P, N])[:] for i in range(2)] + [pix[:, (CC + i) * N:(CC + i + 1) * N] for i in range(2)]
        hs = [sb(f"hs{i}", [P, N]) for i in range(2)]
        hc = [sb(f"hc{i}", [P, N]) for i in range(2)]
        g = sb("g", [P, 2, NP_])
        ysb = xc[:, 0, :]
        gR = xs[:].rearrange("p c n -> p (c n)")[:, 0:2 * NP_].rearrange("p (c n) -> p c n", c=2)
        yn = zn
        yT = sb("yT", [BN, NP_])
        bsum = sb("bsum", [BN, 1])
        xfT = znT
        xhi = sb("xhi", [P, TILES, D + EXT], F16)
        xlo = sb("xlo", [P, TILES, D + EXT], F16)
        xr = sb("xr", [P, TILES, D])
        lg2 = sb("lg2", [P, TILES, E])
        key = sb("key", [P, TILES, E])
        ohb = sb("ohb", [P, TILES, TOP, E], BF16)
        mx = sb("mx", [P, TOP, TILES])
        km = sb("km", [P, TILES, TOP])
        dm = sb("dm", [P, TILES])
        em = sb("em", [P, TILES])
        wts = sb("wts", [P, TOP, TILES])
        psel = sb("psel", [P, TILES, TOP, E])
        pos = sb("pos", [P, TILES, TOP])
        eb = sb("eb", [P, TILES, TOP])
        over = sb("over", [P, TILES, TOP])
        slot = sb("slot", [P, TILES, TOP])
        disp = pix.bitcast(BF16)[:, 0:TILES * SLOTS].rearrange("p (t s) -> p t s", t=TILES)
        flat = mix[:].rearrange("p a c n -> p (a c n)")
        xgT = flat[0:DK + EXT, 0:2 * SLOTS].rearrange("p (k s) -> p k s", k=2)
        thg = [dA[i][:, 0:4 * CAP].rearrange("p (q s) -> p q s", q=2) for i in range(2)]
        gt = [dBu[i][:, 0:4 * CAP].rearrange("p (q s) -> p q s", q=2) for i in range(2)]
        act_t = [sb(f"act{i}", [P, HC, 2 * CAP]) for i in range(2)]
        ye = [sb(f"ye{i}", [CAP, TOP, D]) for i in range(2)]
        idle = sb("idle", [P, 512], BF16)
        zrow = sb("zrow", [CAP, TOP * D])
        info = sb("info", [CAP, TOP * E * EXT])
        dump = sb("dump", [CAP, TOP * E])
        empty = sb("empty", [CAP, TOP * E])
        dest = sb("dest", [CAP, TOP * E])
        destu = sb("destu", [CAP, TOP * E], U32)
        ps = ctx.enter_context(nc.psum_tensor("ps", [P, 8, 512], F32))

        def halves(b):
            return ps[:, b:b + 2, 0:HALF]

        def split(ap):
            return ap.rearrange("p (s c) -> p s c", s=2)

        def img(ap, lo, hi):
            return ap.rearrange("p (i t) -> p i t", t=SEQ)[:, :, lo:hi]

        s_px = [sem(f"pixels_loaded{k}") for k in range(PK)]
        s_par = sem("token_params_loaded")
        s_id = sem("identity_loaded")
        s_w96 = sem("w96_loaded")
        s_chp = sem("channel_params_loaded")
        s_xpw = sem("xproj_loaded")
        s_dtw = sem("dtw_loaded")
        s_sel = sem("selectors_loaded")
        s_late = sem("late_weights_loaded")
        s_route = sem("routing_constants_loaded")
        s_y = sem("embedding_in_psum")
        s_v = sem("vector_chain")
        s_a = sem("scalar_chain")
        s_idle = sem("idle_operand_ready")
        s_var = sem("variance_ready")
        s_ve = sem("variance_plus_eps")
        s_hp5 = sem("exponent_ready")
        s_rs = sem("rstd_ready")
        s_zn = sem("normalised_tiles")
        s_zt = sem("transposed_in_psum")
        s_ztc = sem("transposed_copied")
        s_h = sem("down_in_psum")
        s_hf = sem("hF_ready")
        s_hr = sem("hR_ready")
        s_xs = sem("xs_in_psum")
        s_xc0 = sem("conv_first_tap")
        s_hw = sem("halved_weights")
        s_xc = sem("conv_done")
        s_th = sem("tanh_done")
        s_u = sem("u_ready")
        s_zp = sem("z_in_psum")
        s_zth = sem("z_tanh_done")
        s_sz = sem("silu_z_ready")
        s_xp = sem("xproj_in_psum")
        s_xdt = sem("dt_rows_copied")
        s_hi = sem("high_parts")
        s_r1 = sem("first_rests")
        s_mid = sem("middle_parts")
        s_lo = sem("low_parts")
        s_dtp = sem("dt_in_psum")
        s_ab = sem("abs_done")
        s_lg = sem("log_done")
        s_relu = sem("relu_done")
        s_dt = sem("dt_ready")
        s_midc = sem("middle_part_of_C")
        s_loc = sem("low_part_of_C")
        s_du = sem("du_ready")
        s_aexp = sem("A_exponential")
        s_nA = sem("negA_ready")
        s_zero = sem("borders_zeroed")
        s_uD = sem("uD_ready")
        s_ysb = sem("y_copied")
        s_B = [sem(f"B_in_psum{i}") for i in range(2)]
        s_C = [sem(f"C_in_psum{i}") for i in range(2)]
        s_Bs = [sem(f"B_copied{i}") for i in range(2)]
        s_dA = [sem(f"dA_ready{i}") for i in range(2)]
        s_dbu = [sem(f"dBu_ready{i}") for i in range(4)]
        s_scan = [sem(f"scan_done{i}") for i in range(2)]
        s_hc = [sem(f"hC_ready{i}") for i in range(2)]
        s_acc = [sem(f"hC_summed{i}") for i in range(2)]
        s_gate = sem("y_gated")
        s_gr = sem("y_reversed")
        s_o = sem("backward_out_in_psum")
        s_of = sem("forward_out_in_psum")
        s_yc = sem("directions_centred")
        s_yf = sem("forward_scaled")
        s_yn = sem("mixer_normed")
        s_yt = sem("y_transposed")
        s_ytc = sem("yT_ready")
        s_up = sem("up_in_psum")
        s_x2 = sem("ffn_input_ready")
        s_xt = sem("ffn_input_transposed")
        s_xtc = sem("ffn_input_T_ready")
        s_lgp = sem("logits_in_psum")
        s_m = sem("score_gap_ready")
        s_em = sem("score_exp_ready")
        s_oh = sem("onehot_ready")
        s_pos = sem("positions_in_psum")
        s_disp = sem("dispatch_tiles")
        s_xh = sem("xhi_ready")
        s_xrr = sem("xrest_ready")
        s_xl = sem("xlo_ready")
        s_g = [sem(f"gathered_in_psum{k}") for k in range(2)]
        s_gc = [sem(f"gathered_copied{k}") for k in range(2)]
        s_w1 = [sem(f"up_weights{i}") for i in range(2)]
        s_w2 = [sem(f"down_weights{i}") for i in range(2)]
        s_hp = [sem(f"hidden_in_psum{i}") for i in range(2)]
        s_ht = [sem(f"gate_tanh{i}") for i in range(2)]
        s_hg = [sem(f"gate_product{i}") for i in range(2)]
        s_act = [sem(f"hidden_ready{i}") for i in range(2)]
        s_ye = [sem(f"expert_out_in_psum{i}") for i in range(2)]
        s_yec = [sem(f"expert_out_copied{i}") for i in range(2)]
        s_yst = [sem(f"expert_out_stored{i}") for i in range(2)]
        s_yfree = [sem(f"expert_out_slot_free{i}") for i in range(2)]
        s_zr = sem("zero_rows_ready")
        s_dump = sem("dump_rows_loaded")
        s_fill = sem("result_holds_residual")
        s_ext = sem("slot_extras_ready")
        s_info = sem("slot_info_in_psum")
        s_ic = sem("slot_info_copied")
        s_dest = sem("destination_steps")


        block = ctx.enter_context(nc.Block())

        @block.sync
        def _(sp):
            for k in range(PK):
                sp.dma_start(xT[:, k, :], a["xT"][:, k, :]).then_inc(s_px[k], 16)
            sp.dma_start(base[:], a["base"]).then_inc(s_par, 16)
            sp.dma_start(ident[:], a["ident"]).then_inc(s_id, 16)
            sp.dma_start(xpw[:], a["xpw"]).then_inc(s_xpw, 16)
            sp.dma_start(sel[:], a["sel"]).then_inc(s_sel, 16)
            sp.dma_start(outw[:], a["outw"]).then_inc(s_late, 16)
            sp.dma_start(tri[:], a["tri"]).then_inc(s_route, 16)
            sp.dma_start(ones[:], a["ones"]).then_inc(s_route, 16)
            sp.dma_start(iota[:], a["iota"]).then_inc(s_route, 16)
            for i in range(2):
                sp.dma_start(w1s[i][:], a["W1"][i]).then_inc(s_w1[i], 16)
                sp.dma_start(w2s[i][:], a["W2"][i]).then_inc(s_w2[i], 16)
            sp.dma_start(dump[:], a["dump"]).then_inc(s_dump, 16)
            sp.wait_ge(s_zr, 1)
            sp.dma_start(a["out"][N:, :].rearrange("(k c) d -> c k d", k=TOP), zrow[:].rearrange("c (k d) -> c k d", k=TOP)).then_inc(s_fill, 16)
            sp.wait_ge(s_var, 5)
            for t in range(TILES):
                rows = min(P, N - t * P)
                sp.dma_start(a["out"][t * P:t * P + rows, :], h0[0:rows, t, :]).then_inc(s_fill, 16)

            def load_up(e, slot, done):
                sp.wait_ge(s_hp[1], done)
                sp.dma_start(w1s[slot][:], a["W1"][bass.ds(e, 1)].rearrange("o p k h -> (o p) k h")).then_inc(s_w1[slot], 16)

            def load_down(e, slot, uses):
                sp.wait_ge(s_yec[slot], (uses + 1) * TOP)
                sp.dma_start(w2s[slot][:], a["W2"][bass.ds(e, 1)].rearrange("o p k h -> (o p) k h")).then_inc(s_w2[slot], 16)

            load_up(2, 0, 1)
            with sp.Fori(0, E // 2 - 2) as j:
                for i in range(2):
                    load_up(j * 2 + (i + 3), 1 - i, j * 2 + (i + 2))
                    load_down(j * 2 + (i + 2), i, j + 1)
            load_up(E - 1, 1, E - 2)
            for i in range(2):
                load_down(E - 2 + i, i, E // 2 - 1)

        @block.gpsimd
        def _(pool):
            nc.gpsimd.memset(dA[0][:], 0.0).then_inc(s_zero, 1)
            nc.gpsimd.memset(dA[1][:], 0.0).then_inc(s_zero, 1)
            nc.gpsimd.memset(g[:, :, N:], 0.0).then_inc(s_zero, 1)
            nc.gpsimd.memset(zrow[:], 0.0).then_inc(s_zr, 1)
            nc.gpsimd.memset(xlo[:, :, D:D + 1], 0.0).then_inc(s_ext, 1)

            def rstd(n, d=0):
                pool.wait_ge(s_var, n)
                nc.gpsimd.tensor_scalar(veps[:, :, d], mv[:, :, d, 1], EPS, None, ALU.add).then_inc(s_ve, 1)
                pool.wait_ge(s_ve, n)
                nc.gpsimd.tensor_tensor(rst[:, :, d], veps[:, :, d], halfpow[:, :, d], ALU.pow).then_inc(s_rs, 1)

            nc.gpsimd.memset(halfpow[:], -0.5).then_inc(s_hp5, 1)
            pool.wait_ge(s_hp5, 1)
            rstd(1)
            rstd(2)
            for c in range(CC):
                pool.wait_ge(s_u, c + 1)
                nc.gpsimd.tensor_scalar(uD[:, c, :], u[:, c, :], chanp[:, c, C_D:C_D + 1], None, ALU.mult).then_inc(s_uD, 1)
            pool.wait_ge(s_uD, CC)
            pool.wait_ge(s_midc, 1)
            nc.gpsimd.tensor_tensor(cparts[4 * NS:6 * NS, :], bcr[XC:XDT, :], cparts[2 * NS:4 * NS, :], ALU.subtract).then_inc(s_loc, 1)
            pool.wait_ge(s_loc, 1)

            def pool_quad(c, q):
                for i in range(4):
                    pool.wait_ge(s_Bs[i % 2], q * 2 + (c * 8 + i // 2 + 1))
                    nc.gpsimd.tensor_tensor(dBu[i], du[:, c, :], Bs[i % 2][:], ALU.mult).then_inc(s_dbu[i], 1)

            for i in range(4):
                pool.sem_inc(s_dbu[i], 1)
            for c in range(CC):
                pool.wait_ge(s_du, c + 1)
                if c == 0:
                    with pool.Fori(0, QUADS) as q:
                        pool_quad(c, q)
                    pool.wait_ge(s_lg, CC)
                    nc.gpsimd.memset(gR[:, :, N:], 0.0).then_inc(s_zero, 1)
                else:
                    with pool.Fori(0, QUADS - 1) as q:
                        pool_quad(c, q)
                    if c == 1:
                        pool.wait_ge(s_sz, CC)
                        pool.wait_ge(s_ysb, 1)
                        nc.gpsimd.tensor_tensor(g[:, 0, 0:N], ysb, sz[:, 0, :], ALU.mult).then_inc(s_gate, 1)
                    pool_quad(c, QUADS - 1)
            pool.wait_ge(s_ysb, 2)
            nc.gpsimd.tensor_tensor(g[:, 1, 0:N], ysb, sz[:, 1, :], ALU.mult).then_inc(s_gate, 1)
            nc.gpsimd.tensor_tensor(gR[:, 0, 0:N][:, ::-1], ysb, sz[:, 1, :], ALU.mult).then_inc(s_gate, 1)
            rstd(3, 0)
            rstd(4, 1)
            rstd(5)
            for i in range(2):
                pool.sem_inc(s_yfree[i], 1)
            pool.wait_ge(s_ic, 1)
            number = info[:].rearrange("c (b x) -> c b x", x=EXT)[:, :, 0]
            nc.gpsimd.tensor_scalar(empty[:], number, 0.0, None, ALU.is_equal).then_inc(s_dest, 1)
            nc.gpsimd.tensor_scalar(dest[:], number, SPLIT, -1.0, ALU.mult, ALU.add).then_inc(s_dest, 1)
            pool.wait_ge(s_dump, 16)
            pool.wait_ge(s_dest, 2)
            nc.gpsimd.tensor_tensor(empty[:], empty[:], dump[:], ALU.mult).then_inc(s_dest, 1)
            pool.wait_ge(s_dest, 3)
            nc.gpsimd.tensor_tensor(dest[:], dest[:], empty[:], ALU.add).then_inc(s_dest, 1)
            pool.wait_ge(s_dest, 4)
            nc.gpsimd.tensor_copy(destu[:], dest[:]).then_inc(s_dest, 1)
            pool.wait_ge(s_dest, 5)
            pool.wait_ge(s_fill, 16 * (TILES + 1))
            for e in range(E):
                if e > 0:
                    pool.wait_ge(s_yst[(e - 1) % 2], 16 * TOP * ((e - 1) // 2 + 1))
                    pool.sem_inc(s_yfree[(e - 1) % 2], 1)
                for k in range(TOP):
                    pool.wait_ge(s_yec[e % 2], TOP * (e // 2 + 1) + k + 1)
                    pool.indirect_dma_start(
                        out=a["out"], out_offset=bass.IndirectOffsetOnAxis(ap=destu[:, k * E + e:k * E + e + 1], axis=0),
                        in_=ye[e % 2][:, k, :], in_offset=None, compute_op=ALU.add
                    ).then_inc(s_yst[e % 2], 16)
            pool.wait_ge(s_yst[(E - 1) % 2], 16 * TOP * (E // 2))

        @block.scalar
        def _(act):
            chain = [0]

            def link(ins):
                chain[0] += 1
                ins.then_inc(s_a, 1)
                act.wait_ge(s_a, chain[0])

            for k in range(PK):
                act.dma_start(tokW[:, k, :], a["tokW"][:, k, :]).then_inc(s_px[k], 16)
            act.dma_start(rowp[:], a["rowp"].broadcast_to([P, RPAR])).then_inc(s_par, 16)
            act.dma_start(kcon[:], a["kcon"]).then_inc(s_par, 16)
            act.dma_start(w96[:], a["w96"]).then_inc(s_w96, 16)
            act.dma_start(col96[:], a["col96"]).then_inc(s_w96, 16)
            act.dma_start(chanp[:], a["chanp"]).then_inc(s_chp, 16)
            act.dma_start(dtw[XDT:XROWS, :], a["dtw"]).then_inc(s_dtw, 16)
            act.preload_act_table_set("exp_and_others")
            act.wait_ge(s_zt, 2)
            nc.scalar.activation(znT[:, 512:1024], ps[0:DK, 6, :], ACT.Copy).then_inc(s_ztc, 1)
            act.wait_ge(s_zt, 3)
            nc.scalar.activation(znT[:, 1024:1280], ps[0:DK, 7, 0:256], ACT.Copy).then_inc(s_ztc, 1)
            act.wait_ge(s_hf, 1)
            nc.scalar.activation(hR[:], hF[:, ::-1], ACT.Copy).then_inc(s_hr, 1)
            act.wait_ge(s_hw, 1)
            for c in range(CC):
                act.wait_ge(s_xs, c + 1)
                link(nc.scalar.activation(split(xs[:, c, :]), halves(2 * c + 2), ACT.Copy))
                nc.scalar.activation(xc[:, c, :], xs[:, c, :], ACT.Identity, bias=halfw[:, c, TAPS:TAPS + 1],
                                     scale=halfw[:, c, TAPS - 1:TAPS]).then_inc(s_xc0, 1)
            for c in range(CC):
                act.wait_ge(s_xc, c + 1)
                nc.scalar.activation(th[:, c, :], xc[:, c, :], ACT.Tanh).then_inc(s_th, 1)
                act.wait_ge(s_zp, c + 1)
                nc.scalar.activation(split(sz[:, c, :]), halves(2 * c), ACT.Tanh, scale=0.5)
                nc.scalar.activation(split(zs[:, c, :]), halves(2 * c), ACT.Copy).then_inc(s_zth, 1)
            act.preload_act_table_set("natural_log_exp_and_others")
            nc.scalar.activation(negA[:].rearrange("p (c n) -> p c n", c=CC), chanp[:, :, C_A:C_A + NS], ACT.Exp).then_inc(s_aexp, 1)
            act.wait_ge(s_xp, 1)
            nc.scalar.activation(split(xdt[XDT:XROWS, :]), ps[XDT:XROWS, 6:8, 0:HALF], ACT.Copy).then_inc(s_xdt, 1)
            nc.scalar.activation(split(bparts[2 * NS:4 * NS, :]), ps[XB:XC, 6:8, 0:HALF], ACT.Copy).then_inc(s_hi, 1)
            nc.scalar.activation(split(cparts[0:2 * NS, :]), ps[XC:XDT, 6:8, 0:HALF], ACT.Copy).then_inc(s_hi, 1)
            def log1p_exp(c):
                act.wait_ge(s_ab, c + 1)
                link(nc.scalar.activation(ex[:, c, :], ab[:, c, :], ACT.Exp, scale=-1.0))
                nc.scalar.activation(lg[:, c, :], ex[:, c, :], ACT.Ln, bias=1.0).then_inc(s_lg, 1)

            for c in range(CC):
                act.wait_ge(s_dtp, c + 1)
                nc.scalar.activation(split(ab[:, c, :]), halves(DT_BANK[c]), ACT.Abs, bias=chanp[:, c, C_DTB:C_DTB + 1]).then_inc(s_ab, 1)
                if c == 0:
                    act.wait_ge(s_r1, 1)
                    nc.scalar.activation(bparts[0:2 * NS, :], bcr[XB:XC, :], ACT.Copy).then_inc(s_mid, 1)
                    log1p_exp(0)
            for c in range(1, CC):
                log1p_exp(c)
            act.wait_ge(s_zero, 3)
            act.wait_ge(s_nA, 1)

            def copy_b(slot, uses):
                act.wait_ge(s_B[slot], uses)
                nc.scalar.activation(split(Bs[slot][:]), halves(2), ACT.Copy).then_inc(s_Bs[slot], 1)

            def act_quad(c, q, copies, mid=None):
                for pair in range(2):
                    for i in range(2):
                        act.wait_ge(s_scan[i], q * 2 + (c * 8 + pair + 1))
                        nc.scalar.activation(img(dA[i][:], 1, SEQ), img(dt[:, c, :], 1, SEQ), ACT.Exp,
                                             scale=negA[:, bass.ds(q * 4 + (c * NS + 2 * pair + i), 1)]).then_inc(s_dA[i], 1)
                        if 2 * pair + i < copies:
                            act.wait_ge(s_dbu[2 * pair + i], q + (c * QUADS + 2))
                            copy_b(i, q * 2 + (c * 8 + pair + 2))
                    if pair == 0 and mid:
                        mid()

            def copy_y(c):
                for i in range(2):
                    act.wait_ge(s_acc[i], 8 * (c + 1) + 1)
                if c > 0:
                    act.wait_ge(s_gate, c)
                nc.scalar.activation(split(ysb), halves(0), ACT.Copy, scale=0.5).then_inc(s_ysb, 1)

            copy_b(0, 1)
            copy_b(1, 1)
            for c in range(CC):
                act.wait_ge(s_dt, c + 1)
                if c > 0:
                    act_quad(c, 0, 4, lambda: copy_y(c - 1))
                with act.Fori(min(c, 1), QUADS - (c == CC - 1)) as q:
                    act_quad(c, q, 4)
            act_quad(CC - 1, QUADS - 1, 2)
            act.preload_act_table_set("exp_and_others")
            act.wait_ge(s_rs, 3)
            act.wait_ge(s_yc, 1)
            for t in range(TILES):
                nc.scalar.activation(yn[:, t, 0:BN], yn[:, t, 0:BN], ACT.Copy, scale=rst[:, t, 0:1]).then_inc(s_yf, 1)
            act.wait_ge(s_yt, 4)
            nc.scalar.activation(yT[:, 0:512], ps[0:BN, 6, :], ACT.Identity, bias=bsum[:, 0:1]).then_inc(s_ytc, 1)
            act.wait_ge(s_yt, TILES)
            nc.scalar.activation(yT[:, 512:640], ps[0:BN, 7, 0:128], ACT.Identity, bias=bsum[:, 0:1]).then_inc(s_ytc, 1)
            act.wait_ge(s_xt, 2)
            nc.scalar.activation(xfT[:, 512:1024], ps[0:DK, 6, :], ACT.Copy).then_inc(s_xtc, 1)
            act.wait_ge(s_xt, 3)
            nc.scalar.activation(xfT[:, 1024:1280], ps[0:DK, 7, 0:256], ACT.Copy).then_inc(s_xtc, 1)
            nc.scalar.activation(xhi[:, :, 0:D], zn[:], ACT.Copy, scale=SPLIT).then_inc(s_xh, 1)
            act.wait_ge(s_m, 1)
            nc.scalar.activation(em[:], dm[:], ACT.Exp).then_inc(s_em, 1)
            act.wait_ge(s_xrr, 1)
            nc.scalar.activation(xlo[:, :, 0:D], xr[:], ACT.Copy).then_inc(s_xl, 1)
            for q in range(4):
                act.wait_ge(s_g[0], q + 1)
                cols = slice(q * SLOTS // 4, (q + 1) * SLOTS // 4)
                nc.scalar.activation(xgT[0:DK, 0, cols], ps[0:DK, 4 + 2 * (q % 2), 0:SLOTS // 4], ACT.Copy,
                                     scale=1.0 / SPLIT).then_inc(s_gc[0], 1)
            for i in range(2):
                act.sem_inc(s_yec[i], TOP)
            def gate_tanh(j, i):
                for s in range(2):
                    act.wait_ge(s_hp[s], j * 2 + (i + 1))
                    act.wait_ge(s_hg[s], j * 2 + (i + 1))
                    nc.scalar.activation(thg[s][:], ps[:, 2 * s:2 * s + 2, 2 * CAP:4 * CAP], ACT.Tanh,
                                         scale=0.5).then_inc(s_ht[s], 1)

            def copy_out(j, i):
                act.wait_ge(s_yfree[i], j + 1)
                for k in range(TOP):
                    act.wait_ge(s_ye[i], j * TOP + (TOP + k + 1))
                    nc.scalar.activation(ye[i][:, k, :], ps[0:CAP, 4 + 2 * k + i, 0:D], ACT.Copy,
                                         scale=info[:, bass.ds(j * (2 * EXT) + ((k * E + i) * EXT + 1 + k), 1)]).then_inc(s_yec[i], 1)

            gate_tanh(0, 0)
            act.wait_ge(s_info, 1)
            nc.scalar.activation(info[:], ps[0:CAP, 6, 0:TOP * E * EXT], ACT.Copy).then_inc(s_ic, 1)
            act.wait_ge(s_ic, 1)
            with act.Fori(0, E // 2 - 1) as j:
                gate_tanh(j, 1)
                copy_out(j, 0)
                gate_tanh(j + 1, 0)
                copy_out(j, 1)
            gate_tanh(E // 2 - 1, 1)
            copy_out(E // 2 - 1, 0)
            copy_out(E // 2 - 1, 1)

        @block.vector
        def _(dve):
            chain = [0]
            V = nc.vector
            V.memset(idle[:], 0.0).then_inc(s_idle, 1)

            def link(ins):
                chain[0] += 1
                ins.then_inc(s_v, 1)
                dve.wait_ge(s_v, chain[0])

            def step(ins):
                chain[0] += 1
                ins.then_inc(s_v, 1)
                return chain[0]

            def settle():
                dve.wait_ge(s_v, chain[0])

            def moments(src, ready, d=0):
                for t in range(TILES):
                    ready(t)
                    step(V.bn_stats(stats[:, t, d, :], src(t)))
                settle()
                for t in range(TILES):
                    last = V.bn_aggr(mv[:, t, d, :], stats[:, t, d, :])
                last.then_inc(s_var, 1)

            dve.wait_ge(s_par, 48)
            done = []
            for t in range(TILES):
                dve.wait_ge(s_y, t + 1)
                done.append(step(V.scalar_tensor_tensor(h0[:, t, :], rowp[:, R_TB:R_TB + D], kcon[:, K_PATCH + t:K_PATCH + t + 1],
                                                        ps[:, t, 0:D], ALU.mult, ALU.add)))
            moments(lambda t: h0[:, t, :], lambda t: dve.wait_ge(s_v, done[t]))
            dve.wait_ge(s_var, 1)
            for t in range(TILES):
                step(V.scalar_tensor_tensor(h0[:, t, :], h0[:, t, :], mv[:, t, 0, 0:1], rowp[:, R_LW:R_LW + D], ALU.subtract, ALU.mult))
            settle()
            dve.wait_ge(s_rs, 1)
            done = [step(V.scalar_tensor_tensor(h0[:, t, :], h0[:, t, :], rst[:, t, 0:1], base[:, t, :], ALU.mult, ALU.add))
                    for t in range(TILES)]
            moments(lambda t: h0[:, t, :], lambda t: dve.wait_ge(s_v, done[t]))
            dve.wait_ge(s_var, 2)
            dve.wait_ge(s_rs, 2)
            for t in range(TILES):
                V.tensor_scalar(zn[:, t, :], h0[:, t, :], mv[:, t, 0, 0:1], rst[:, t, 0:1],
                                ALU.subtract, ALU.mult).then_inc(s_zn, 1)
            dve.wait_ge(s_zt, 1)
            V.tensor_copy(znT[:, 0:512], ps[0:DK, 5, :]).then_inc(s_ztc, 1)
            dve.wait_ge(s_chp, 16)
            V.tensor_scalar(halfw[:], chanp[:, :, 0:TAPS + 1], 0.5, None, ALU.mult).then_inc(s_hw, 1)
            dve.wait_ge(s_w96, 32)
            step(V.tensor_tensor(bsum[:], col96[:, 1:2], col96[:, 2:3], ALU.add))
            dve.wait_ge(s_h, 1)
            V.tensor_scalar(split(hF[:]), ps[0:BN, 0:2, 0:HALF], col96[:, 0:1], None, ALU.add).then_inc(s_hf, 1)
            dve.wait_ge(s_zn, TILES)
            step(V.tensor_tensor(h0[:], h0[:], rowp[:, None, R_UB:R_UB + D].broadcast_to([P, TILES, D]), ALU.add))
            dve.wait_ge(s_hw, 1)
            def silu_u(c):
                dve.wait_ge(s_th, c + 1)
                V.scalar_tensor_tensor(u[:, c, :], th[:, c, :], 1.0, xc[:, c, :], ALU.add, ALU.mult).then_inc(s_u, 1)

            done = [0] * CC
            for c, k in ((0, 1), (0, 2), (1, 1), (0, 3), (1, 2), (2, 1), (1, 3), (2, 2), (2, 3)):
                if k == 1:
                    dve.wait_ge(s_xc0, c + 1)
                else:
                    dve.wait_ge(s_v, done[c])
                o = img(xc[:, c, :], k, SEQ)
                ins = V.scalar_tensor_tensor(o, img(xs[:, c, :], 0, SEQ - k), halfw[:, c, TAPS - 1 - k:TAPS - k], o,
                                             ALU.mult, ALU.add)
                if k < TAPS - 1:
                    done[c] = step(ins)
                else:
                    ins.then_inc(s_xc, 1)
            for c in range(CC):
                silu_u(c)
            for c in range(CC):
                dve.wait_ge(s_zth, c + 1)
                V.scalar_tensor_tensor(sz[:, c, :], sz[:, c, :], 1.0, zs[:, c, :], ALU.add, ALU.mult).then_inc(s_sz, 1)
            dve.wait_ge(s_hi, 1)
            V.tensor_tensor(split(bcr[XB:XC, :]), ps[XB:XC, 6:8, 0:HALF], split(bparts[2 * NS:4 * NS, :]), ALU.subtract).then_inc(s_r1, 1)
            dve.wait_ge(s_hi, 2)
            V.tensor_tensor(split(bcr[XC:XDT, :]), ps[XC:XDT, 6:8, 0:HALF], split(cparts[0:2 * NS, :]), ALU.subtract).then_inc(s_r1, 1)
            dve.wait_ge(s_aexp, 1)
            V.tensor_scalar(negA[:], negA[:], -1.0, None, ALU.mult).then_inc(s_nA, 1)
            dve.wait_ge(s_r1, 2)
            V.tensor_copy(cparts[2 * NS:4 * NS, :], bcr[XC:XDT, :]).then_inc(s_midc, 1)

            def step_size(c):
                dve.wait_ge(s_relu, c + 1)
                dve.wait_ge(s_lg, c + 1)
                V.tensor_tensor(dt[:, c, :], dt[:, c, :], lg[:, c, :], ALU.add).then_inc(s_dt, 1)
                dve.wait_ge(s_dt, c + 1)
                V.tensor_tensor(du[:, c, :], dt[:, c, :], u[:, c, :], ALU.mult).then_inc(s_du, 1)

            for c in range(CC):
                dve.wait_ge(s_ab, c + 1)
                V.tensor_scalar(split(dt[:, c, :]), halves(DT_BANK[c]), chanp[:, c, C_DTB:C_DTB + 1], 0.0, ALU.add, ALU.max).then_inc(s_relu, 1)
                if c == 0:
                    dve.wait_ge(s_mid, 1)
                    V.tensor_tensor(bparts[4 * NS:6 * NS, :], bcr[XB:XC, :], bparts[0:2 * NS, :], ALU.subtract).then_inc(s_lo, 1)
                    step_size(0)
            for c in range(1, CC):
                step_size(c)
            dve.wait_ge(s_zero, 3)
            for i in range(2):
                dve.sem_inc(s_scan[i], 1)
                dve.sem_inc(s_hc[i], 1)

            def dve_quad(c, q):
                for pair in range(2):
                    uses = q * 2 + (c * 8 + pair)
                    for i in range(2):
                        dve.wait_ge(s_dA[i], uses + 1)
                        dve.wait_ge(s_dbu[2 * pair + i], q + (c * QUADS + 2))
                        dve.wait_ge(s_hc[i], uses + 1)
                        V.tensor_tensor_scan(hs[i][:], dA[i][:], dBu[2 * pair + i], 0.0, ALU.mult, ALU.add).then_inc(s_scan[i], 1)
                    for i in range(2):
                        dve.wait_ge(s_C[i], uses + 1)
                        dve.wait_ge(s_acc[i], uses + 1)
                        dve.wait_ge(s_scan[i], uses + 2)
                        V.tensor_tensor(split(hc[i][:]), split(hs[i][:]), halves(4 + 2 * i), ALU.mult).then_inc(s_hc[i], 1)

            for c in range(CC):
                with dve.Fori(0, QUADS) as q:
                    dve_quad(c, q)
            dve.wait_ge(s_sz, CC)
            dve.wait_ge(s_zero, 4)
            for i in range(2):
                dve.wait_ge(s_acc[i], 8 * CC + 1)
            V.scalar_tensor_tensor(split(gR[:, 1, 0:N][:, ::-1]), halves(0), 0.5, split(sz[:, 2, :]),
                                   ALU.mult, ALU.mult).then_inc(s_gr, 1)
            def centre(d, src):
                for t in range(TILES):
                    last = V.scalar_tensor_tensor(yn[:, t, d * BN:(d + 1) * BN], src(t), mv[:, t, d, 0:1],
                                                  rowp[:, R_G + d * BN:R_G + (d + 1) * BN], ALU.subtract, ALU.mult)
                last.then_inc(s_yc, 1)

            of = lambda t: ps[:, 2, t * BN:(t + 1) * BN]
            moments(of, lambda t: dve.wait_ge(s_of, 1), 0)
            dve.wait_ge(s_var, 3)
            centre(0, of)
            ob = lambda t: ps[:, 3 + t // 2, (t % 2) * BN:(t % 2 + 1) * BN]
            moments(ob, lambda t: dve.wait_ge(s_o, min(t // 2 * 2 + 2, TILES)), 1)
            dve.wait_ge(s_var, 4)
            centre(1, ob)
            dve.wait_ge(s_yc, 2)
            dve.wait_ge(s_rs, 4)
            for t in range(TILES):
                dve.wait_ge(s_yf, t + 1)
                V.scalar_tensor_tensor(yn[:, t, 0:BN], yn[:, t, BN:2 * BN], rst[:, t, 1:2], yn[:, t, 0:BN],
                                       ALU.mult, ALU.add).then_inc(s_yn, 1)
            done = []

            def residual(t):
                dve.wait_ge(s_up, t + 1)
                done.append(step(V.tensor_tensor(h0[:, t, :], h0[:, t, :], ps[:, t, 0:D], ALU.add)))

            def residual_ready(t):
                if t + 1 < TILES:
                    residual(t + 1)
                dve.wait_ge(s_v, done[t])

            residual(0)
            moments(lambda t: h0[:, t, :], residual_ready)
            dve.wait_ge(s_var, 5)
            dve.wait_ge(s_rs, 5)
            for t in range(TILES):
                V.tensor_scalar(zn[:, t, :], h0[:, t, :], mv[:, t, 0, 0:1], rst[:, t, 0:1],
                                ALU.subtract, ALU.mult).then_inc(s_x2, 1)
            dve.wait_ge(s_xt, 1)
            V.tensor_copy(xfT[:, 0:512], ps[0:DK, 5, :]).then_inc(s_xtc, 1)
            dve.wait_ge(s_xh, 1)
            V.scalar_tensor_tensor(xr[:], zn[:], SPLIT, xhi[:, :, 0:D], ALU.mult, ALU.subtract).then_inc(s_xrr, 1)
            rev = kcon[:, None, K_REV:K_REV + E].broadcast_to([P, TILES, E])
            cmp = kcon[:, K_CMP:K_CMP + TILES * E].rearrange("p (t e) -> p t e", e=E)
            lgt = ps[:, 4, 0:TILES * E].rearrange("p (t e) -> p t e", e=E)
            dve.wait_ge(s_lgp, 1)
            for k in range(TOP):
                src = (lgt, lg2[:])[k]
                link(V.tensor_reduce(mx[:, k, :], src, AX.X, ALU.max))
                link(V.tensor_tensor(key[:], src, mx[:, k, :].rearrange("p (t o) -> p t o", o=1).broadcast_to([P, TILES, E]), ALU.is_equal))
                link(V.tensor_tensor(key[:], key[:], rev, ALU.mult))
                link(V.tensor_reduce(km[:, :, k], key[:], AX.X, ALU.max))
                ins = V.tensor_tensor(ohb[:, :, k, :], cmp, km[:, :, k:k + 1].broadcast_to([P, TILES, E]), ALU.is_equal)
                if k == 0:
                    link(ins)
                    link(V.scalar_tensor_tensor(lg2[:], ohb[:, :, 0, :], -3.0e38, lgt, ALU.mult, ALU.add))
                else:
                    ins.then_inc(s_oh, 1)
            V.tensor_tensor(dm[:], mx[:, 1, :], mx[:, 0, :], ALU.subtract).then_inc(s_m, 1)
            step(V.scalar_tensor_tensor(eb[:], km[:], -float(CAP),
                                        kcon[:, K_BASE:K_BASE + TILES].rearrange("p (t o) -> p t o", o=1).broadcast_to([P, TILES, TOP]),
                                        ALU.mult, ALU.add))
            dve.wait_ge(s_oh, 1)
            dve.wait_ge(s_pos, 1)
            link(V.tensor_tensor(psel[:], ps[:, 5, 0:TILES * TOP * E].rearrange("p (t k e) -> p t k e", k=TOP, e=E), ohb[:], ALU.mult))
            link(V.tensor_reduce(pos[:], psel[:], AX.X, ALU.add))
            step(V.tensor_tensor(slot[:], pos[:], eb[:], ALU.add))
            link(V.tensor_scalar(over[:], pos[:], float(CAP), DROP, ALU.is_gt, ALU.mult))
            link(V.tensor_tensor(slot[:], slot[:], over[:], ALU.add))
            dve.wait_ge(s_route, 48)

            def dispatch(k):
                for t in range(TILES):
                    V.tensor_scalar(disp[:, t, k * KSLOTS:(k + 1) * KSLOTS], iota[:], slot[:, t, k:k + 1], None,
                                    ALU.is_equal).then_inc(s_disp, 1)

            dispatch(0)
            dve.wait_ge(s_em, 1)
            link(V.tensor_scalar(wts[:, 1, :], em[:], 1.0, None, ALU.add))
            link(V.reciprocal(wts[:, 0, :], wts[:, 1, :]))
            link(V.tensor_tensor(wts[:, 1, :], em[:], wts[:, 0, :], ALU.mult))
            wtk = wts[:].rearrange("p k t -> p t k")
            V.tensor_copy(xhi[:, :, D], kcon[:, K_TOK:K_TOK + TILES]).then_inc(s_ext, 1)
            V.tensor_scalar(xhi[:, :, D + 1:D + EXT], wtk, SPLIT, None, ALU.mult).then_inc(s_ext, 1)
            dve.wait_ge(s_ext, 3)
            V.scalar_tensor_tensor(xlo[:, :, D + 1:D + EXT], wtk, SPLIT, xhi[:, :, D + 1:D + EXT], ALU.mult, ALU.subtract).then_inc(s_ext, 1)
            dispatch(1)
            for q in range(4):
                dve.wait_ge(s_g[1], q + 1)
                cols = slice(q * SLOTS // 4, (q + 1) * SLOTS // 4)
                V.tensor_scalar(xgT[:, 1, cols], ps[0:DK + EXT, 5 + 2 * (q % 2), 0:SLOTS // 4], 1.0 / SPLIT, None,
                                ALU.mult).then_inc(s_gc[1], 1)
            for i in range(2):
                dve.sem_inc(s_hg[i], 1)
                dve.sem_inc(s_act[i], 1)
            with dve.Fori(0, E // 2) as j:
                for i in range(2):
                    for s in range(2):
                        dve.wait_ge(s_ht[s], j * 2 + i + 1)
                        V.scalar_tensor_tensor(gt[s][:], thg[s][:], 1.0, ps[:, 2 * s:2 * s + 2, 2 * CAP:4 * CAP],
                                               ALU.add, ALU.mult).then_inc(s_hg[s], 1)
                        dve.wait_ge(s_hg[s], j * 2 + i + 2)
                        dve.wait_ge(s_ye[i], (j + 1) * TOP)
                        V.scalar_tensor_tensor(act_t[i][:, 2 * s:2 * s + 2, :], gt[s][:], 0.5,
                                               ps[:, 2 * s:2 * s + 2, 0:2 * CAP], ALU.mult, ALU.mult).then_inc(s_act[s], 1)

        @block.tensor
        def _(pe):
            mm = nc.tensor.matmul

            def keep_warm(count, bank):
                with pe.Fori(0, max(count // 4, 1)):
                    for _ in range(min(count, 4)):
                        mm(ps[:, bank, :], idle[:, 0:P], idle[:], start=True, stop=True)

            pe.wait_ge(s_idle, 1)
            keep_warm(8, 7)
            for k in range(PK):
                pe.wait_ge(s_px[k], 32)
                for t in range(TILES):
                    last = mm(ps[:, t, 0:D], xT[:, k, t * P:(t + 1) * P], tokW[:, k, :], start=k == 0, stop=k == PK - 1)
                    if k == PK - 1:
                        last.then_inc(s_y, 1)

            def transpose_rows(ready, done):
                for q in range(2 * TILES):
                    k, t = divmod(q, TILES)
                    pe.wait_ge(ready, t + 1 if k == 0 else TILES)
                    last = nc.tensor.transpose(ps[0:DK, 5 + q // 4, (q % 4) * P:(q % 4 + 1) * P],
                                               zn[:, t, k * DK:(k + 1) * DK], ident[:])
                    if q % 4 == 3 or q == 2 * TILES - 1:
                        last.then_inc(done, 1)

            pe.wait_ge(s_id, 16)
            keep_warm(44, 7)
            transpose_rows(s_zn, s_zt)
            keep_warm(2, 4)
            pe.wait_ge(s_w96, 32)
            pe.wait_ge(s_ztc, 3)
            for h in range(2):
                for k in range(2):
                    last = mm(ps[0:BN, h, 0:HALF], w96[:, W_DOWN + k * BN:W_DOWN + (k + 1) * BN],
                              znT[:, k * NP_ + h * HALF:k * NP_ + (h + 1) * HALF], start=k == 0, stop=k == 1)
            last.then_inc(s_h, 1)
            parts = [[(0, P, hF)], [(0, 64, hF), (64, P, hR)], [(0, P, hR)]]

            def in_proj(col, bank, c, done):
                for lo, hi, src in parts[c]:
                    for h in range(2):
                        last = mm(ps[lo:hi, bank + h, 0:HALF], w96[:, col + c * P + lo:col + c * P + hi],
                                  src[:, h * HALF:(h + 1) * HALF], start=True, stop=True)
                last.then_inc(done, 1)

            keep_warm(2, 4)
            pe.wait_ge(s_hf, 1)
            in_proj(W_XS, 2, 0, s_xs)
            pe.wait_ge(s_hr, 1)
            in_proj(W_XS, 4, 1, s_xs)
            in_proj(W_XS, 6, 2, s_xs)
            for c in range(CC):
                if c > 0:
                    pe.wait_ge(s_xc0, c)
                in_proj(W_Z, 2 * c, c, s_zp)
            pe.wait_ge(s_xpw, 16)
            pe.wait_ge(s_xc0, 3)
            keep_warm(12, 6)
            for c in range(CC):
                pe.wait_ge(s_u, c + 1)
                for h in range(2):
                    last = mm(ps[0:XROWS, 6 + h, 0:HALF], xpw[:, c, :], u[:, c, h * HALF:(h + 1) * HALF],
                              start=c == 0, stop=c == CC - 1)
            last.then_inc(s_xp, 1)
            pe.wait_ge(s_zth, 2)
            keep_warm(4, 2)
            pe.wait_ge(s_dtw, 16)
            pe.wait_ge(s_xdt, 1)
            for c in range(CC):
                pe.wait_ge(s_zth, max(DT_BANK[c] // 2, c - 1) + 1)
                for h in range(2):
                    last = mm(ps[:, DT_BANK[c] + h, 0:HALF], dtw[XDT:XROWS, c * P:(c + 1) * P],
                              xdt[XDT:XROWS, h * HALF:(h + 1) * HALF], start=True, stop=True)
                last.then_inc(s_dtp, 1)

            def bcast(bank, parts, idx, done):
                for h in range(2):
                    last = mm(ps[:, bank + h, 0:HALF], sel[:, idx, :].rearrange("p o m -> p (o m)"),
                              parts[:, h * HALF:(h + 1) * HALF], start=True, stop=True)
                last.then_inc(done, 1)

            pe.wait_ge(s_sel, 16)
            pe.wait_ge(s_lo, 1)
            pe.wait_ge(s_relu, 1)
            bcast(2, bparts, slice(0, 1), s_B[0])
            pe.wait_ge(s_hi, 2)
            pe.wait_ge(s_r1, 2)
            keep_warm(12, 7)
            pe.wait_ge(s_relu, CC)
            pe.wait_ge(s_loc, 1)
            for k in range(1, 5):
                if k == 3:
                    keep_warm(2, 0)
                pe.wait_ge(s_Bs[(k - 1) % 2], (k - 1) // 2 + 1)
                bcast(2, bparts, slice(k, k + 1), s_B[k % 2])
                if k < 3:
                    bcast(2 + 2 * k, cparts, slice(k - 1, k), s_C[k - 1])
            pe.wait_ge(s_uD, CC)
            for i in range(2):
                pe.sem_inc(s_acc[i], 1)

            def pe_quad(c, q, more_b=4, more_c=4):
                for i in range(4):
                    pe.wait_ge(s_hc[i % 2], q * 2 + (c * 8 + i // 2 + 2))
                    for h in range(2):
                        last = mm(ps[:, h, 0:HALF], ident[:], hc[i % 2][:, h * HALF:(h + 1) * HALF],
                                  start=False, stop=False, skip_group_check=True)
                    last.then_inc(s_acc[i % 2], 1)
                    if i < more_c:
                        bcast(4 + 2 * (i % 2), cparts, bass.ds(q * 4 + (c * NS + i + 2), 1), s_C[i % 2])
                    if i < more_b:
                        pe.wait_ge(s_Bs[i % 2], q * 2 + (c * 8 + i // 2 + 3))
                        bcast(2, bparts, bass.ds(q * 4 + (c * NS + i + 5), 1), s_B[(i + 1) % 2])

            for c in range(CC):
                if c > 0:
                    pe.wait_ge(s_ysb, c)
                for h in range(2):
                    mm(ps[:, h, 0:HALF], ident[:], uD[:, c, h * HALF:(h + 1) * HALF],
                       start=True, stop=False, skip_group_check=True)
                with pe.Fori(0, QUADS - 2 * (c == CC - 1)) as q:
                    pe_quad(c, q)
            pe_quad(CC - 1, QUADS - 2, more_b=3)
            pe_quad(CC - 1, QUADS - 1, more_b=0, more_c=2)
            pe.wait_ge(s_late, 16)
            pe.wait_ge(s_gate, 3)
            pe.wait_ge(s_zero, 4)
            for t in range(TILES):
                rows = slice(t * P, (t + 1) * P)
                of = ps[:, 2, t * BN:(t + 1) * BN]
                mm(of, g[:, 0, rows], outw[:, 0, :], start=True, stop=False)
                last = mm(of, g[0:64, 1, rows], outw[0:64, 1, :], start=False, stop=True)
            last.then_inc(s_of, 1)
            pe.wait_ge(s_gr, 1)
            for t in range(TILES):
                rows = slice(t * P, (t + 1) * P)
                ob = ps[:, 3 + t // 2, (t % 2) * BN:(t % 2 + 1) * BN]
                mm(ob, gR[:, 1, rows], outw[:, 2, :], start=True, stop=False)
                mm(ob, gR[64:P, 0, rows], outw[64:P, 1, :], start=False, stop=True).then_inc(s_o, 1)
            keep_warm(12, 6)
            for t in range(TILES):
                pe.wait_ge(s_yn, t + 1)
                nc.tensor.transpose(ps[0:BN, 6 + t // 4, (t % 4) * P:(t % 4 + 1) * P], yn[:, t, 0:BN],
                                    ident[:]).then_inc(s_yt, 1)
            keep_warm(4, 5)
            pe.wait_ge(s_ytc, 2)
            for t in range(TILES):
                mm(ps[:, t, 0:D], yT[:, t * P:(t + 1) * P], w96[:, W_UP:W_UP + D],
                   start=True, stop=True).then_inc(s_up, 1)
            keep_warm(20, 5)
            transpose_rows(s_x2, s_xt)
            keep_warm(4, 3)
            pe.wait_ge(s_xtc, 3)
            for t in range(TILES):
                for k in range(2):
                    last = mm(ps[:, 4, t * E:(t + 1) * E], xfT[:, k * NP_ + t * P:k * NP_ + (t + 1) * P],
                              w96[:, W_G + k * E:W_G + (k + 1) * E], start=k == 0, stop=k == 1)
            last.then_inc(s_lgp, 1)
            keep_warm(8, 3)
            pe.wait_ge(s_route, 48)
            pe.wait_ge(s_oh, 1)
            for t in range(TILES):
                for b in range(t + 1):
                    last = mm(ps[:, 5, t * TOP * E:(t + 1) * TOP * E], tri[:] if b == t else ones[:],
                              ohb[:, b].rearrange("p k e -> p (k e)"), start=b == 0, stop=b == t)
            last.then_inc(s_pos, 1)
            keep_warm(8, 3)
            pe.wait_ge(s_xl, 1)
            for q, k in ((0, 0), (1, 0), (0, 1), (1, 1), (2, 0), (2, 1), (3, 0), (3, 1)):
                if q == 0 and k == 1:
                    pe.wait_ge(s_ext, 4)
                if q >= 2:
                    pe.wait_ge(s_gc[k], q - 1)
                width = DK + k * EXT
                for t in range(TILES):
                    pe.wait_ge(s_disp, t + 1 if q < 2 else TILES + t + 1)
                    for part in (xhi, xlo):
                        last = mm(ps[0:width, 4 + 2 * (q % 2) + k, 0:SLOTS // 4], part[:, t, k * DK:k * DK + width],
                                  disp[:, t, q * SLOTS // 4:(q + 1) * SLOTS // 4], start=t == 0 and part is xhi,
                                  stop=t == TILES - 1 and part is xlo)
                last.then_inc(s_g[k], 1)
            for k in range(2):
                pe.wait_ge(s_gc[k], 3)
            for i in range(2):
                pe.sem_inc(s_ye[i], TOP)

            def up(j, i):
                pe.wait_ge(s_w1[i], j * 16 + 16)
                for s in range(2):
                    pe.wait_ge(s_act[s], j * 2 + (i + 1))
                    for q in range(2 * s, 2 * s + 2):
                        for half in range(2):
                            for k in range(2):
                                src = xgT[0:DK, k, :].rearrange("p (k e c) -> p e k c", k=TOP, e=E)[:, bass.ds(j * 2 + i, 1)]
                                col = half * H + q * P
                                last = mm(ps[:, q, half * 2 * CAP:(half + 1) * 2 * CAP].rearrange("p (k c) -> p k c", k=TOP),
                                          w1s[i][:, k, col:col + P], src.rearrange("p o k c -> p (o k) c"),
                                          start=k == 0, stop=k == 1)
                    last.then_inc(s_hp[s], 1)

            def down(j, i):
                pe.wait_ge(s_w2[i], j * 16 + 16)
                pe.wait_ge(s_yec[i], (j + 1) * TOP)
                if i == 0:
                    pe.wait_ge(s_ic, 1)
                for s in range(2):
                    pe.wait_ge(s_act[s], j * 2 + (i + 2))
                for k in range(TOP):
                    for q in range(HC):
                        last = mm(ps[0:CAP, 4 + 2 * k + i, 0:D], act_t[i][:, q, k * CAP:(k + 1) * CAP],
                                  w2s[i][:, q, :], start=q == 0, stop=q == HC - 1)
                    last.then_inc(s_ye[i], 1)

            up(0, 0)
            for k in range(2):
                pe.wait_ge(s_gc[k], 4)
            for b in range(TOP * E):
                last = nc.tensor.transpose(ps[0:CAP, 6, b * EXT:(b + 1) * EXT], xgT[DK:DK + EXT, 1, b * CAP:(b + 1) * CAP],
                                           ident[DK:DK + EXT, DK:DK + EXT])
            last.then_inc(s_info, 1)
            with pe.Fori(0, E // 2 - 1) as j:
                up(j, 1)
                down(j, 0)
                up(j + 1, 0)
                down(j, 1)
            up(E // 2 - 1, 1)
            down(E // 2 - 1, 0)
            down(E // 2 - 1, 1)


def kernel(**inputs):
    import concourse.bacc as bacc
    import ml_dtypes
    from concourse.bass_utils import run_bass_kernel_spmd

    I = {k: np.asarray(v) for k, v in inputs.items()}
    f32 = np.float32

    def both(name):
        v = np.concatenate([I["L0_attn_f_" + name], I["L0_attn_b_" + name]], axis=0)
        return v.reshape((CC, P) + v.shape[1:]).swapaxes(0, 1)

    x = I["x"].reshape(IMAGES, 3, SIDE, PATCH, SIDE, PATCH).transpose(1, 3, 5, 0, 2, 4).reshape(PIX, IMAGES, SEQ - 1)
    xT = np.zeros((PIX, NP_), f32)
    xT[:, :N].reshape(PIX, IMAGES, SEQ)[:, :, 1:] = x
    base = np.zeros((NP_, D), f32)
    base[:N].reshape(IMAGES, SEQ, D)[:, 1:] = I["L0_tok_ln_b"]
    base[:N].reshape(IMAGES, SEQ, D)[:, 0] = I["cls_tok"].reshape(D)
    chanp = np.concatenate([both("conv_w"), both("conv_b")[..., None], both("dt_b")[..., None], both("D")[..., None],
                            both("A_log")], axis=2)
    rowp = np.concatenate([I["L0_tok_b"], I["L0_tok_ln_w"], I["L0_attn_up_b"], I["L0_attn_f_ln_g"],
                           I["L0_attn_b_ln_g"]])[None]
    col96 = np.stack([I["L0_attn_down_b"], I["L0_attn_f_ln_b"], I["L0_attn_b_ln_b"]], axis=1)

    def rows96(w):
        return w.reshape(2, DK, -1).transpose(1, 0, 2).reshape(DK, -1)

    fi, bi = I["L0_attn_f_in_W"], I["L0_attn_b_in_W"]
    w96 = np.concatenate([rows96(I["L0_attn_down_W"]), fi[:, :DI], bi[:, :DI], fi[:, DI:], bi[:, DI:],
                          I["L0_attn_up_W"], rows96(I["L0_ffn_Wg"])], axis=1)
    xpw = np.zeros((CH, XROWS), f32)
    dtw = np.zeros((2 * R, CH), f32)
    sel = np.zeros((3, 2, NS, SEL, P), ml_dtypes.bfloat16)
    for d, w in enumerate("fb"):
        xw = I[f"L0_attn_{w}_xproj_W"]
        mine = slice(d * DI, (d + 1) * DI)
        xpw[mine, XB + d * NS:XB + (d + 1) * NS] = xw[:, R:R + NS]
        xpw[mine, XC + d * NS:XC + (d + 1) * NS] = xw[:, R + NS:]
        xpw[mine, XDT + d * R:XDT + (d + 1) * R] = xw[:, :R]
        dtw[d * R:(d + 1) * R, mine] = I[f"L0_attn_{w}_dt_W"]
        for i in range(SEL):
            c, n = divmod(i, NS)
            ch = np.arange(c * P, (c + 1) * P)
            sel[:, d, n, i, (ch >= d * DI) & (ch < (d + 1) * DI)] = 1
    tok = np.arange(NP_).reshape(TILES, P).T
    rev = np.tile(E - np.arange(E), (P, 1))
    cmp = np.where(tok[:, :, None] < N, rev[:, None], -1).reshape(P, TILES * E)
    kcon = np.concatenate([((tok < N) & (tok % SEQ > 0)), rev, cmp, np.where(tok < N, KSLOTS - 1, DROP), tok + 1], axis=1).astype(f32)
    at = np.arange(P)
    arrays = {
        "xT": xT.reshape(PK, P, NP_).transpose(1, 0, 2),
        "tokW": I["L0_tok_W"].T.reshape(PK, P, D).transpose(1, 0, 2),
        "base": base.reshape(TILES, P, D).transpose(1, 0, 2),
        "chanp": chanp, "rowp": rowp, "col96": col96, "w96": w96, "kcon": kcon,
        "xpw": xpw.reshape(CC, P, XROWS).transpose(1, 0, 2), "dtw": dtw,
        "outw": both("out_W"),
        "sel": sel.reshape(6 * NS, SEL, P),
        "ident": np.eye(P, dtype=f32),
        "tri": (at[:, None] <= at[None, :]).astype(ml_dtypes.bfloat16),
        "ones": np.ones((P, P), ml_dtypes.bfloat16),
        "iota": np.tile(np.arange(KSLOTS), (P, 1)).astype(np.float16),
        "dump": np.repeat(1 + N + np.arange(TOP)[None, :] * CAP + np.arange(CAP)[:, None], E, axis=1).astype(f32),
        "W1": I["L0_ffn_W1"].reshape(E, 2, DK, 2 * H).transpose(0, 2, 1, 3),
        "W2": I["L0_ffn_W2"].reshape(E, HC, P, D).transpose(0, 2, 1, 3),
    }
    arrays = {k: np.ascontiguousarray(v) for k, v in arrays.items()}
    nc = bacc.Bacc("TRN2", target_bir_lowering=False, num_devices=1)
    aps = {k: nc.dram_tensor(k + "_dram", v.shape, mybir.dt.from_np(v.dtype), kind="ExternalInput").ap()
           for k, v in arrays.items()}
    aps["out"] = nc.dram_tensor("out_dram", (N + TOP * CAP, D), F32, kind="ExternalOutput").ap()
    vit_mamba_moe(nc, aps)
    r = run_bass_kernel_spmd(nc, [{k + "_dram": v for k, v in arrays.items()}], core_ids=[0])
    return r.results[0]["out_dram"][:N].reshape(IMAGES, SEQ, D)
```
